# Optimizing a Trainium2 kernel written in Bass

```python
import numpy as np
import jax
import jax.numpy as jnp

def _softmax(x, axis=-1):
    return jax.nn.softmax(x, axis=axis)

def _gelu(x):
    return jax.nn.gelu(x, approximate=True)

def _silu(x):
    return jax.nn.silu(x)

def _sigmoid(x):
    return jax.nn.sigmoid(x)

def _layernorm(x, axis=-1, eps=1e-05):
    m = jnp.mean(x, axis=axis, keepdims=True)
    v = jnp.var(x, axis=axis, keepdims=True)
    return (x - m) / jnp.sqrt(v + eps)

def _scatter_add(tgt, idx, src, axis=0):
    return tgt.at[idx].add(src)

def _segment_sum(src, seg, n):
    return jax.ops.segment_sum(src, seg, n)
kernel_name = 'mk_seq_postln_d2_jaxref_r8_bc95f7'

def setup_inputs(seed: int=0):
    np.random.seed(seed)
    _w = jnp.asarray

    def _L0_attn_setup():
        import jax, jax.numpy as jnp
        import numpy as np
        B, S, D = (2, 256, 128)
        H, DH = (16, 64)
        DQL, DKVL = (64, 64)
        DR = 64
        TOPK = 64
        LN_EPS = 1e-05
        ROPE_BASE = 10000.0

        def _rope_tables(seq_len, dim):
            inv_freq = 1.0 / ROPE_BASE ** (np.arange(0, dim, 2, dtype=np.float32) / dim)
            t = np.arange(seq_len, dtype=np.float32)
            freqs = np.outer(t, inv_freq)
            cos = np.concatenate([np.cos(freqs), np.cos(freqs)], -1)[:, ::2]
            sin = np.concatenate([np.sin(freqs), np.sin(freqs)], -1)[:, ::2]
            return (jnp.asarray(cos), jnp.asarray(sin))

        def _apply_rope_subspace(x, d_rope):
            s = x.shape[-2]
            cos, sin = _rope_tables(s, d_rope)
            xr, xp = (x[..., :d_rope], x[..., d_rope:])
            e, o = (xr[..., 0::2], xr[..., 1::2])
            rot = jnp.stack([e * cos - o * sin, e * sin + o * cos], axis=-1).reshape(xr.shape)
            return jnp.concatenate([rot, xp], axis=-1)

        def _reference_tuple_inner(x, w_down_q, w_down_kv, w_up_q, w_up_k, w_up_v, w_out, ln_scale, ln_bias):
            b, s, d = x.shape
            residual = x
            mu = jnp.mean(x, axis=-1, keepdims=True)
            var = jnp.mean((x - mu) ** 2, axis=-1, keepdims=True)
            h = (x - mu) * jax.lax.rsqrt(var + LN_EPS) * ln_scale + ln_bias
            c_q = h @ w_down_q.T
            c_kv = h @ w_down_kv.T
            q = (c_q @ w_up_q.T).reshape(b, s, H, DH).transpose(0, 2, 1, 3)
            k = (c_kv @ w_up_k.T).reshape(b, s, H, DH).transpose(0, 2, 1, 3)
            v = (c_kv @ w_up_v.T).reshape(b, s, H, DH).transpose(0, 2, 1, 3)
            q = _apply_rope_subspace(q, DR)
            k = _apply_rope_subspace(k, DR)
            scale = 1.0 / np.sqrt(DH).astype(np.float32)
            scores = jnp.einsum('bhqd,bhkd->bhqk', q, k) * scale
            _, indices = jax.lax.top_k(scores, min(TOPK, s))
            attn = jax.nn.softmax(scores, axis=-1)
            out = jnp.einsum('bhqk,bhkd->bhqd', attn, v)
            out = out.transpose(0, 2, 1, 3).reshape(b, s, H * DH)
            out = out @ w_out.T + residual
            return (out, indices.astype(jnp.int64))
        key = jax.random.key(seed)
        ks = jax.random.split(key, 7)
        init = lambda k, shape: jax.random.normal(k, shape, jnp.float32) * 0.02
        return {'x': jax.random.normal(ks[0], (B, S, D), jnp.float32), 'w_down_q': init(ks[1], (DQL, D)), 'w_down_kv': init(ks[2], (DKVL, D)), 'w_up_q': init(ks[3], (H * DH, DQL)), 'w_up_k': init(ks[4], (H * DH, DKVL)), 'w_up_v': init(ks[5], (H * DH, DKVL)), 'w_out': init(ks[6], (D, H * DH)), 'ln_scale': jnp.ones((D,), jnp.float32), 'ln_bias': jnp.zeros((D,), jnp.float32)}
    _L0_attn_in = _L0_attn_setup()

    def _L0_ffn_setup():
        import jax, jax.numpy as jnp
        import numpy as np
        H = 128
        I = 64
        E = 8
        TOPK = 2
        NGROUP = 4
        TOPKG = 2
        SCALE = 1.0
        B, S = (4, 128)

        def _gate(xf, gate_weight, bias):
            T = xf.shape[0]
            logits = xf @ gate_weight.T
            scores = jax.nn.sigmoid(logits)
            scores_for_choice = scores + bias[None, :]
            gsz = E // NGROUP
            grp = scores_for_choice.reshape(T, NGROUP, gsz)
            group_scores = jax.lax.top_k(grp, 2)[0].sum(-1)
            _, group_idx = jax.lax.top_k(group_scores, TOPKG)
            rows = jnp.arange(T)[:, None]
            group_mask = jnp.zeros((T, NGROUP), xf.dtype).at[rows, group_idx].set(1.0)
            score_mask = jnp.broadcast_to(group_mask[:, :, None], (T, NGROUP, gsz)).reshape(T, E)
            tmp_scores = jnp.where(score_mask > 0, scores_for_choice, 0.0)
            _, topk_idx = jax.lax.top_k(tmp_scores, TOPK)
            topk_weight = jnp.take_along_axis(scores, topk_idx, axis=1)
            if TOPK > 1:
                topk_weight = topk_weight / (topk_weight.sum(-1, keepdims=True) + 1e-20)
            topk_weight = topk_weight * SCALE
            return (topk_idx, topk_weight)
        key = jax.random.key(seed)
        k0, k1, k2, k3, k4 = jax.random.split(key, 5)
        return {'hidden_states': jax.random.normal(k0, (B, S, H), jnp.float32), 'gate_weight': jax.random.normal(k1, (E, H), jnp.float32) * (1.0 / np.sqrt(H)), 'e_score_correction_bias': jnp.zeros((E,), jnp.float32), 'gate_proj': jax.random.normal(k2, (E, I, H), jnp.float32) * 0.02, 'up_proj': jax.random.normal(k3, (E, I, H), jnp.float32) * 0.02, 'down_proj': jax.random.normal(k4, (E, H, I), jnp.float32) * 0.02}
    _L0_ffn_in = _L0_ffn_setup()

    def _L1_attn_setup():
        import jax, jax.numpy as jnp
        import numpy as np
        HEADS = 16
        EPS = 1e-06
        key = jax.random.key(seed)
        k0, k1, k2, k3, k4 = jax.random.split(key, 5)
        b, t, dim = (2, 256, 128)
        scale = 0.02
        return {'hidden_states': jax.random.normal(k0, (b, t, dim), dtype=jnp.float32), 'Wq': jax.random.normal(k1, (dim, dim), dtype=jnp.float32) * scale, 'Wk': jax.random.normal(k2, (dim, dim), dtype=jnp.float32) * scale, 'Wv': jax.random.normal(k3, (dim, dim), dtype=jnp.float32) * scale, 'Wo': jax.random.normal(k4, (dim, dim), dtype=jnp.float32) * scale}
    _L1_attn_in = _L1_attn_setup()

    def _L1_ffn_setup():
        import jax, jax.numpy as jnp
        import numpy as np
        GROUP = 16
        EPS = 1e-05

        def _dequant(q, scale):
            w = q.astype(jnp.float32) / 7.5 - 1.0
            return w * jnp.repeat(scale, GROUP, axis=1)

        def _qlora_linear(x, q, scale, bias, la, lb):
            w = _dequant(q, scale)
            base = jnp.einsum('btd,od->bto', x, w) + bias
            lora = jnp.einsum('btr,or->bto', jnp.einsum('btd,rd->btr', x, la), lb)
            return base + lora

        def _layernorm(x, g, b):
            mu = jnp.mean(x, axis=-1, keepdims=True)
            var = jnp.mean(jnp.square(x - mu), axis=-1, keepdims=True)
            return (x - mu) * jax.lax.rsqrt(var + EPS) * g + b
        key = jax.random.key(seed)
        ks = jax.random.split(key, 6)
        D, R, B, T = (128, 32, 8, 512)
        x = jax.random.normal(ks[0], (B, T, D), dtype=jnp.float32)
        qweights = jax.random.randint(ks[1], (6, D, D), 0, 16, dtype=jnp.int32)
        scales = jax.random.uniform(ks[2], (6, D, D // GROUP), dtype=jnp.float32)
        biases = jax.random.normal(ks[3], (6, D), dtype=jnp.float32) * 0.02
        lora_a = jax.random.normal(ks[4], (6, R, D), dtype=jnp.float32) * 0.02
        lora_b = jax.random.normal(ks[5], (6, D, R), dtype=jnp.float32) * 0.02
        ln_gamma = jnp.ones((3, D), dtype=jnp.float32)
        ln_beta = jnp.zeros((3, D), dtype=jnp.float32)
        return {'x': x, 'qweights': qweights, 'scales': scales, 'biases': biases, 'lora_a': lora_a, 'lora_b': lora_b, 'ln_gamma': ln_gamma, 'ln_beta': ln_beta}
    _L1_ffn_in = _L1_ffn_setup()
    _d = {'L0_attn_x': _L0_attn_in['x'], 'L0_attn_w_down_q': _L0_attn_in['w_down_q'], 'L0_attn_w_down_kv': _L0_attn_in['w_down_kv'], 'L0_attn_w_up_q': _L0_attn_in['w_up_q'], 'L0_attn_w_up_k': _L0_attn_in['w_up_k'], 'L0_attn_w_up_v': _L0_attn_in['w_up_v'], 'L0_attn_w_out': _L0_attn_in['w_out'], 'L0_attn_ln_scale': _L0_attn_in['ln_scale'], 'L0_attn_ln_bias': _L0_attn_in['ln_bias'], 'L0_ffn_gate_weight': _L0_ffn_in['gate_weight'], 'L0_ffn_e_score_correction_bias': _L0_ffn_in['e_score_correction_bias'], 'L0_ffn_gate_proj': _L0_ffn_in['gate_proj'], 'L0_ffn_up_proj': _L0_ffn_in['up_proj'], 'L0_ffn_down_proj': _L0_ffn_in['down_proj'], 'L1_attn_Wq': _L1_attn_in['Wq'], 'L1_attn_Wk': _L1_attn_in['Wk'], 'L1_attn_Wv': _L1_attn_in['Wv'], 'L1_attn_Wo': _L1_attn_in['Wo'], 'L1_ffn_qweights': _L1_ffn_in['qweights'], 'L1_ffn_scales': _L1_ffn_in['scales'], 'L1_ffn_biases': _L1_ffn_in['biases'], 'L1_ffn_lora_a': _L1_ffn_in['lora_a'], 'L1_ffn_lora_b': _L1_ffn_in['lora_b'], 'L1_ffn_ln_gamma': _L1_ffn_in['ln_gamma'], 'L1_ffn_ln_beta': _L1_ffn_in['ln_beta']}
    _x0 = _d['L0_attn_x']
    _d['L0_attn_x'] = jax.random.normal(jax.random.fold_in(jax.random.key(seed), 1), (4, 1024, 128), dtype=_x0.dtype)
    del _x0
    return _d

def reference(L0_attn_x, L0_attn_w_down_q, L0_attn_w_down_kv, L0_attn_w_up_q, L0_attn_w_up_k, L0_attn_w_up_v, L0_attn_w_out, L0_attn_ln_scale, L0_attn_ln_bias, L0_ffn_gate_weight, L0_ffn_e_score_correction_bias, L0_ffn_gate_proj, L0_ffn_up_proj, L0_ffn_down_proj, L1_attn_Wq, L1_attn_Wk, L1_attn_Wv, L1_attn_Wo, L1_ffn_qweights, L1_ffn_scales, L1_ffn_biases, L1_ffn_lora_a, L1_ffn_lora_b, L1_ffn_ln_gamma, L1_ffn_ln_beta):

    def _L0_attn_ref(x, w_down_q, w_down_kv, w_up_q, w_up_k, w_up_v, w_out, ln_scale, ln_bias):
        import jax, jax.numpy as jnp
        import numpy as np
        B, S, D = (2, 256, 128)
        H, DH = (16, 64)
        DQL, DKVL = (64, 64)
        DR = 64
        TOPK = 64
        LN_EPS = 1e-05
        ROPE_BASE = 10000.0

        def _rope_tables(seq_len, dim):
            inv_freq = 1.0 / ROPE_BASE ** (np.arange(0, dim, 2, dtype=np.float32) / dim)
            t = np.arange(seq_len, dtype=np.float32)
            freqs = np.outer(t, inv_freq)
            cos = np.concatenate([np.cos(freqs), np.cos(freqs)], -1)[:, ::2]
            sin = np.concatenate([np.sin(freqs), np.sin(freqs)], -1)[:, ::2]
            return (jnp.asarray(cos), jnp.asarray(sin))

        def _apply_rope_subspace(x, d_rope):
            s = x.shape[-2]
            cos, sin = _rope_tables(s, d_rope)
            xr, xp = (x[..., :d_rope], x[..., d_rope:])
            e, o = (xr[..., 0::2], xr[..., 1::2])
            rot = jnp.stack([e * cos - o * sin, e * sin + o * cos], axis=-1).reshape(xr.shape)
            return jnp.concatenate([rot, xp], axis=-1)

        def _reference_tuple_inner(x, w_down_q, w_down_kv, w_up_q, w_up_k, w_up_v, w_out, ln_scale, ln_bias):
            b, s, d = x.shape
            residual = x
            mu = jnp.mean(x, axis=-1, keepdims=True)
            var = jnp.mean((x - mu) ** 2, axis=-1, keepdims=True)
            h = (x - mu) * jax.lax.rsqrt(var + LN_EPS) * ln_scale + ln_bias
            c_q = h @ w_down_q.T
            c_kv = h @ w_down_kv.T
            q = (c_q @ w_up_q.T).reshape(b, s, H, DH).transpose(0, 2, 1, 3)
            k = (c_kv @ w_up_k.T).reshape(b, s, H, DH).transpose(0, 2, 1, 3)
            v = (c_kv @ w_up_v.T).reshape(b, s, H, DH).transpose(0, 2, 1, 3)
            q = _apply_rope_subspace(q, DR)
            k = _apply_rope_subspace(k, DR)
            scale = 1.0 / np.sqrt(DH).astype(np.float32)
            scores = jnp.einsum('bhqd,bhkd->bhqk', q, k) * scale
            _, indices = jax.lax.top_k(scores, min(TOPK, s))
            attn = jax.nn.softmax(scores, axis=-1)
            out = jnp.einsum('bhqk,bhkd->bhqd', attn, v)
            out = out.transpose(0, 2, 1, 3).reshape(b, s, H * DH)
            out = out @ w_out.T + residual
            return (out, indices.astype(jnp.int64))
        return _reference_tuple_inner(x, w_down_q, w_down_kv, w_up_q, w_up_k, w_up_v, w_out, ln_scale, ln_bias)[0]

    def _L0_ffn_ref(hidden_states, gate_weight, e_score_correction_bias, gate_proj, up_proj, down_proj):
        import jax, jax.numpy as jnp
        import numpy as np
        H = 128
        I = 64
        E = 8
        TOPK = 2
        NGROUP = 4
        TOPKG = 2
        SCALE = 1.0
        B, S = (4, 128)

        def _gate(xf, gate_weight, bias):
            T = xf.shape[0]
            logits = xf @ gate_weight.T
            scores = jax.nn.sigmoid(logits)
            scores_for_choice = scores + bias[None, :]
            gsz = E // NGROUP
            grp = scores_for_choice.reshape(T, NGROUP, gsz)
            group_scores = jax.lax.top_k(grp, 2)[0].sum(-1)
            _, group_idx = jax.lax.top_k(group_scores, TOPKG)
            rows = jnp.arange(T)[:, None]
            group_mask = jnp.zeros((T, NGROUP), xf.dtype).at[rows, group_idx].set(1.0)
            score_mask = jnp.broadcast_to(group_mask[:, :, None], (T, NGROUP, gsz)).reshape(T, E)
            tmp_scores = jnp.where(score_mask > 0, scores_for_choice, 0.0)
            _, topk_idx = jax.lax.top_k(tmp_scores, TOPK)
            topk_weight = jnp.take_along_axis(scores, topk_idx, axis=1)
            if TOPK > 1:
                topk_weight = topk_weight / (topk_weight.sum(-1, keepdims=True) + 1e-20)
            topk_weight = topk_weight * SCALE
            return (topk_idx, topk_weight)
        Bv, Sv, Hv = hidden_states.shape
        xf = hidden_states.reshape(-1, Hv).astype(jnp.float32)
        topk_idx, topk_weight = _gate(xf, gate_weight.astype(jnp.float32), e_score_correction_bias.astype(jnp.float32))
        y = jnp.zeros_like(xf)
        for e in range(E):
            combine_w = jnp.where(topk_idx == e, topk_weight, 0.0).sum(-1)
            g = xf @ gate_proj[e].T
            u = xf @ up_proj[e].T
            o = jax.nn.silu(g) * u @ down_proj[e].T
            y = y + combine_w[:, None] * o
        return y.reshape(Bv, Sv, Hv)

    def _L1_attn_ref(hidden_states, Wq, Wk, Wv, Wo):
        import jax, jax.numpy as jnp
        import numpy as np
        HEADS = 16
        EPS = 1e-06
        b, t, dim = hidden_states.shape
        h = HEADS
        d = dim // h

        def proj(W):
            return (hidden_states @ W.T).reshape(b, t, h, d).transpose(0, 2, 1, 3)
        q = proj(Wq) * d ** (-0.5)
        k = proj(Wk)
        v = proj(Wv)
        s = jnp.einsum('bhqd,bhkd->bhqk', q, k)
        attn = 1.0 + s + 0.5 * s * s
        causal = jnp.tril(jnp.ones((t, t), dtype=bool))
        attn = jnp.where(causal, attn, 0.0)
        o = jnp.einsum('bhqk,bhkd->bhqd', attn, v)
        z = jnp.sum(attn, axis=-1, keepdims=True) + EPS
        o = o / z
        y = o.transpose(0, 2, 1, 3).reshape(b, t, dim)
        return y @ Wo.T

    def _L1_ffn_ref(x, qweights, scales, biases, lora_a, lora_b, ln_gamma, ln_beta):
        import jax, jax.numpy as jnp
        import numpy as np
        GROUP = 16
        EPS = 1e-05

        def _dequant(q, scale):
            w = q.astype(jnp.float32) / 7.5 - 1.0
            return w * jnp.repeat(scale, GROUP, axis=1)

        def _qlora_linear(x, q, scale, bias, la, lb):
            w = _dequant(q, scale)
            base = jnp.einsum('btd,od->bto', x, w) + bias
            lora = jnp.einsum('btr,or->bto', jnp.einsum('btd,rd->btr', x, la), lb)
            return base + lora

        def _layernorm(x, g, b):
            mu = jnp.mean(x, axis=-1, keepdims=True)
            var = jnp.mean(jnp.square(x - mu), axis=-1, keepdims=True)
            return (x - mu) * jax.lax.rsqrt(var + EPS) * g + b
        h = x
        for blk in range(3):
            i0, i1 = (2 * blk, 2 * blk + 1)
            y = _qlora_linear(h, qweights[i0], scales[i0], biases[i0], lora_a[i0], lora_b[i0])
            y = _layernorm(y, ln_gamma[blk], ln_beta[blk])
            y = jax.nn.gelu(y, approximate=False)
            y = _qlora_linear(y, qweights[i1], scales[i1], biases[i1], lora_a[i1], lora_b[i1])
            h = y + h
        return h
    x = L0_attn_x
    x = _layernorm(x + _L0_attn_ref(x, L0_attn_w_down_q, L0_attn_w_down_kv, L0_attn_w_up_q, L0_attn_w_up_k, L0_attn_w_up_v, L0_attn_w_out, L0_attn_ln_scale, L0_attn_ln_bias), axis=-1)
    x = _layernorm(x + _L0_ffn_ref(x, L0_ffn_gate_weight, L0_ffn_e_score_correction_bias, L0_ffn_gate_proj, L0_ffn_up_proj, L0_ffn_down_proj), axis=-1)
    x = _layernorm(x + _L1_attn_ref(x, L1_attn_Wq, L1_attn_Wk, L1_attn_Wv, L1_attn_Wo), axis=-1)
    x = _layernorm(x + _L1_ffn_ref(x, L1_ffn_qweights, L1_ffn_scales, L1_ffn_biases, L1_ffn_lora_a, L1_ffn_lora_b, L1_ffn_ln_gamma, L1_ffn_ln_beta), axis=-1)
    return x

_drawn_inputs = setup_inputs


def setup_inputs(seed=0):
    import zlib

    import numpy as np

    out = dict(_drawn_inputs(seed))
    spreads = {'L0_attn_ln_scale': (1.0, 0.6),
     'L0_attn_ln_bias': (0.0, 0.8),
     'L0_ffn_e_score_correction_bias': (0.0, 0.8),
     'L1_ffn_ln_gamma': (1.0, 0.2),
     'L1_ffn_ln_beta': (0.0, 0.1)}
    factors = {'L0_attn_w_down_q': 8.0,
     'L0_attn_w_down_kv': 8.0,
     'L0_attn_w_up_q': 8.0,
     'L0_attn_w_up_k': 8.0,
     'L0_attn_w_up_v': 8.0,
     'L0_attn_w_out': 8.0,
     'L0_ffn_gate_weight': 8.0,
     'L0_ffn_gate_proj': 8.0,
     'L0_ffn_up_proj': 8.0,
     'L0_ffn_down_proj': 8.0,
     'L1_attn_Wq': 8.0,
     'L1_attn_Wk': 8.0,
     'L1_attn_Wv': 8.0,
     'L1_attn_Wo': 8.0,
     'L1_ffn_biases': 5.21,
     'L1_ffn_lora_a': 5.163,
     'L1_ffn_lora_b': 5.228}
    for name, (base, spread) in spreads.items():
        noise = np.random.default_rng([zlib.crc32(name.encode()), seed]).standard_normal(out[name].shape)
        drawn = base * np.exp(spread * noise) if base else spread * noise
        out[name] = jnp.asarray(drawn.astype(out[name].dtype))
    for name, factor in factors.items():
        out[name] = (out[name] * factor).astype(out[name].dtype)
    return out
```

```python
from contextlib import ExitStack

import numpy as np

import concourse.bass as bass
from concourse import mybir

ALU = mybir.AluOpType
ACT = mybir.ActivationFunctionType
AX = mybir.AxisListType
F32 = mybir.dt.float32
F32R = mybir.dt.float32r
I32 = mybir.dt.int32

P = 128
B, S, D = 4, 1024, 128
TT = S // P
QC = 512
NQC = S // QC
CT = QC // P
H, DH = 16, 64
PAIRS = H // 2
NP = B * PAIRS
UNITS = NQC * TT
LN_EPS = 1e-5
SWAP = [i ^ 1 for i in range(32)]
RSQRT_GUESS = 0x5F3759DF


def rsqrt_on_vector(dve, done, base, value, half, guess):
    dve.tensor_scalar(half.bitcast(I32), value.bitcast(I32), 1, None, ALU.logical_shift_right).then_inc(done, 1)
    dve.wait_ge(done, base + 1)
    dve.tensor_scalar(guess.bitcast(I32), half.bitcast(I32), -1, RSQRT_GUESS, ALU.mult, ALU.add).then_inc(done, 1)
    for k in range(3):
        dve.wait_ge(done, base + 3 * k + 2)
        dve.scalar_tensor_tensor(half, guess, -0.5, guess, ALU.mult, ALU.mult).then_inc(done, 1)
        dve.wait_ge(done, base + 3 * k + 3)
        dve.tensor_tensor(half, half, value, ALU.mult).then_inc(done, 1)
        dve.wait_ge(done, base + 3 * k + 4)
        dve.scalar_tensor_tensor(guess, half, 1.5, guess, ALU.add, ALU.mult).then_inc(done, 1)
    dve.wait_ge(done, base + 11)


RSQRT_STEPS = 11


def semaphores(nc, stage, t):
    made, before = [], t.made_before
    t.made_before = made

    def end():
        for s in made:
            nc.gpsimd.sem_clear(s)
        for s in before:
            nc.release_semaphore(s)

    def sem(name):
        made.append(nc.alloc_semaphore(name))
        return made[-1]

    stage.callback(end)
    return sem


def project_inputs(nc, t, d):
    with ExitStack() as ctx:
        sb = lambda n, s, dt=F32: ctx.enter_context(nc.sbuf_tensor(n, s, dt))
        sem = semaphores(nc, ctx, t)
        x_tm = sb("x_tm", [P, 2, TT, D])
        n_tm = sb("n_tm", [P, 2, TT, D])
        h_fm = sb("h_fm", [P, 2, S])
        stats = sb("stats", [P, TT, 6])
        mean_var = sb("mean_var", [P, TT, 2])
        var = sb("var", [P, TT])
        half = sb("half", [P, TT])
        rstd = sb("rstd", [P, TT])
        wd = sb("wd", [P, P])
        lnp = sb("lnp", [P, 2])
        wv = sb("wv", [DH, H, DH])
        wo = sb("wo", [DH, H, D])
        ps = ctx.enter_context(nc.psum_tensor("ps_a", [P, 8, QC], F32))

        weights_in, tables_in = sem("a_weights_in"), sem("a_tables_in")
        x_in = [sem(f"a_x_in{i}") for i in range(2)]
        stats_done, aggr_done, var_done, rsqrt_done = sem("a_stats"), sem("a_aggr"), sem("a_var"), sem("a_rsqrt")
        norm_done = sem("a_norm")
        x_turned, n_turned = sem("a_x_turned"), sem("a_n_turned")
        x_copied, h_ready = sem("a_x_copied"), sem("a_h_ready")
        c_done, v_done, c_copied, v_copied = sem("a_c_done"), sem("a_v_done"), sem("a_c_copied"), sem("a_v_copied")
        g_done, g_copied = sem("a_g_done"), sem("a_g_copied")
        block = ctx.enter_context(nc.Block())

        @block.sync
        def _(sp):
            for dst, src in ((t.ident[:], d.ident), (wd[:], d.wd), (lnp[:], d.lnp), (wv[:], d.wv), (wo[:], d.wo)):
                sp.dma_start(dst, src).then_inc(weights_in, 16)
            for b in range(B):
                if b >= 2:
                    sp.wait_ge(x_turned, 2 * (b - 1))
                    sp.wait_ge(norm_done, TT * (b - 1))
                sp.dma_start(x_tm[:, b % 2], d.x[b * S:(b + 1) * S, :].rearrange("(t p) f -> p t f", p=P)).then_inc(x_in[b % 2], 16)
            for dst, src in ((t.cos[:], d.cos), (t.sin[:], d.sin)):
                sp.dma_start(dst, src).then_inc(tables_in, 16)
            sp.wait_ge(tables_in, 16 * 2)

        @block.vector
        def _(dve):
            for b in range(B):
                dve.wait_ge(x_in[b % 2], 16 * (b // 2 + 1))
                for k in range(TT):
                    dve.bn_stats(stats[:, k], x_tm[:, b % 2, k]).then_inc(stats_done, 1)
                for k in range(TT):
                    dve.wait_ge(stats_done, TT * b + k + 1)
                    dve.bn_aggr(mean_var[:, k], stats[:, k]).then_inc(aggr_done, 1)
                dve.wait_ge(aggr_done, TT * (b + 1))
                dve.tensor_scalar(var[:], mean_var[:, :, 1], LN_EPS, None, ALU.add).then_inc(var_done, 1)
                dve.wait_ge(var_done, b + 1)
                rsqrt_on_vector(dve, rsqrt_done, RSQRT_STEPS * b, var[:], half[:], rstd[:])
                if b >= 2:
                    dve.wait_ge(n_turned, 2 * (b - 1))
                for k in range(TT):
                    dve.tensor_scalar(n_tm[:, b % 2, k], x_tm[:, b % 2, k], mean_var[:, k, 0:1], rstd[:, k:k + 1],
                                      ALU.subtract, ALU.mult).then_inc(norm_done, 1)
                dve.wait_ge(v_done, b + 1)
                dve.tensor_copy(t.v_tm[:, b * TT:(b + 1) * TT], ps[:, 4].rearrange("p (k c) -> p k c", k=TT)).then_inc(v_copied, 1)
                dve.wait_ge(norm_done, TT * (b + 1))
            for g in range(4):
                dve.wait_ge(g_done, g + 1)
                dve.tensor_copy(t.g_all[:, 2 * g:2 * g + 2], ps[:, 7, 0:2 * D].rearrange("p (k o) -> p k o", k=2)).then_inc(g_copied, 1)

        @block.scalar
        def _(act):
            act.wait_ge(weights_in, 16 * 5)
            for b in range(B):
                for c in range(NQC):
                    at = slice(b * S + c * QC, b * S + (c + 1) * QC)
                    act.wait_ge(x_turned, NQC * b + c + 1)
                    act.mul(t.y_fm[:, at], ps[:, c], 2.0).then_inc(x_copied, 1)
                for c in range(NQC):
                    act.wait_ge(n_turned, NQC * b + c + 1)
                    if b >= 2 and c == 0:
                        act.wait_ge(v_done, b - 1)
                    act.activation(h_fm[:, b % 2, c * QC:(c + 1) * QC], ps[:, 2 + c], ACT.Identity, bias=lnp[:, 1:2],
                                   scale=lnp[:, 0:1]).then_inc(h_ready, 1)
                for c in range(NQC):
                    at = slice(b * S + c * QC, b * S + (c + 1) * QC)
                    act.wait_ge(c_done, NQC * b + c + 1)
                    act.copy(t.c_fm[:, at], ps[:, 5 + c]).then_inc(c_copied, 1)

        @block.tensor
        def _(pe):
            pe.wait_ge(weights_in, 16 * 5)
            for b in range(B):
                pe.wait_ge(x_in[b % 2], 16 * (b // 2 + 1))
                for c in range(NQC):
                    if b >= 1:
                        pe.wait_ge(x_copied, NQC * (b - 1) + c + 1)
                    for k in range(CT):
                        last = pe.transpose(ps[:, c, k * P:(k + 1) * P], x_tm[:, b % 2, c * CT + k], t.ident[:])
                    last.then_inc(x_turned, 1)
                for c in range(NQC):
                    if b >= 1:
                        pe.wait_ge(h_ready, NQC * (b - 1) + c + 1)
                    for k in range(CT):
                        pe.wait_ge(norm_done, TT * b + c * CT + k + 1)
                        last = pe.transpose(ps[:, 2 + c, k * P:(k + 1) * P], n_tm[:, b % 2, c * CT + k], t.ident[:])
                    last.then_inc(n_turned, 1)
                for c in range(NQC):
                    pe.wait_ge(h_ready, NQC * b + c + 1)
                    if b >= 1:
                        pe.wait_ge(c_copied, NQC * (b - 1) + c + 1)
                    pe.matmul(ps[:, 5 + c], wd[:], h_fm[:, b % 2, c * QC:(c + 1) * QC], start=True, stop=True).then_inc(c_done, 1)
                if b >= 1:
                    pe.wait_ge(v_copied, b)
                for k in range(TT):
                    last = pe.matmul(ps[:, 4, k * DH:(k + 1) * DH], h_fm[:, b % 2, k * P:(k + 1) * P], wd[:, DH:P],
                                     start=True, stop=True, skip_group_check=True)
                last.then_inc(v_done, 1)
            for g in range(4):
                if g:
                    pe.wait_ge(g_copied, g)
                for k in range(2):
                    for h in range(2):
                        head = 2 * (2 * g + k) + h
                        last = pe.matmul(ps[h * DH:(h + 1) * DH, 7, k * D:(k + 1) * D], wv[:, head], wo[:, head],
                                         start=True, stop=True, skip_group_check=True)
                last.then_inc(g_done, 1)


def latent_attention(nc, t, d):
    with ExitStack() as ctx:
        sb = lambda n, s, dt=F32: ctx.enter_context(nc.sbuf_tensor(n, s, dt))
        sem = semaphores(nc, ctx, t)
        q_hi_twice = [[sb(f"q_hi_twice{p}{h}", [P, S], F32R) for h in range(2)] for p in range(2)]
        k_hi_lo = [[sb(f"k_hi_lo{p}{h}", [P, S], F32R) for h in range(2)] for p in range(2)]
        q_lo_shift = [[sb(f"q_lo_shift{p}{h}", [P, S], F32R) for h in range(2)] for p in range(2)]
        k_hi_one = [[sb(f"k_hi_one{p}{h}", [P, S], F32R) for h in range(2)] for p in range(2)]
        rot = [sb(f"rot{h}", [P, S]) for h in range(2)]
        swapped = [sb(f"swapped{h}", [P, S]) for h in range(2)]
        probs = [sb(f"probs{i}", [P, 2, QC]) for i in range(4)]
        prob_sum = [sb(f"prob_sum{i}", [P, 2, QC]) for i in range(2)]
        wqk = [sb(f"wqk{i}", [P, 2, P]) for i in range(2)]
        v_now = [sb(f"v_now{i}", [P, TT, DH]) for i in range(2)]
        g_now = [sb(f"g_now{i}", [P, D]) for i in range(2)]
        ones = sb("ones", [P, DH])
        o_raw = sb("o_raw", [P, QC])
        recip = sb("recip", [P, QC])
        o_norm = sb("o_norm", [P, QC])
        maxima = sb("maxima", [P, 2 * TT])
        shift_tm = sb("shift_tm", [P, 2 * TT])
        shift_fm = sb("shift_fm", [2 * TT, P], F32R)
        ps_s = ctx.enter_context(nc.psum_tensor("ps_s", [P, 2, 2, QC], F32))
        ps_p = ctx.enter_context(nc.psum_tensor("ps_p", [P, S], F32))
        ps_o = ctx.enter_context(nc.psum_tensor("ps_o", [P, QC], F32))
        ps_x = ctx.enter_context(nc.psum_tensor("ps_x", [P, QC], F32))

        const_set = sem("b_const_set")
        wqk_in, vg_in = sem("b_wqk_in"), sem("b_vg_in")
        hi_done, lo_done = sem("b_hi_done"), sem("b_lo_done")
        moved1 = [sem(f"b_moved1_{h}") for h in range(2)]
        moved2 = [sem(f"b_moved2_{h}") for h in range(2)]
        shift_in = sem("b_shift_in")
        prep_full, prep_read = sem("b_prep_full"), sem("b_prep_read")
        shift_turned = sem("b_shift_turned")
        sin_done, cos_done, rot_done = sem("b_sin"), sem("b_cos"), sem("b_rot")
        neg_done, shift_ready = sem("b_neg_done"), sem("b_shift_ready")
        qk_done, exp_done, pv_done, added = sem("b_qk_done"), sem("b_exp_done"), sem("b_pv_done"), sem("b_added")
        o_copied, sum_done, recip_done, norm_done = sem("b_o_copied"), sem("b_sum_done"), sem("b_recip_done"), sem("b_norm_done")
        out_done, y_added = sem("b_out_done"), sem("b_y_added")
        block = ctx.enter_context(nc.Block())

        USES = 2 + 2 * TT

        def use(m, r):
            return 2 + USES * (m + 1) + r

        def schedule(emit_step, make_loop):
            where = lambda m: ((m // PAIRS) % B, m % PAIRS)
            emit_step(-1, 1, where, False, True)
            emit_step(0, 0, where, False, True)
            with make_loop(0, (NP - 2) // 2) as i:
                for k in (1, 2):
                    def at(m_minus_n, i=i, k=k):
                        j = k + m_minus_n
                        half = i + j // 2
                        return (half // (PAIRS // 2)) % B, (half % (PAIRS // 2)) * 2 + j % 2
                    emit_step(2 * i + k, k % 2, at, True, True)
            emit_step(NP - 1, (NP - 1) % 2, where, True, False)

        def locate(n, at, m_minus_n):
            return at(n + m_minus_n) if isinstance(n, int) else at(m_minus_n)

        @block.sync
        def _(sp):
            sp.dma_start(wqk[0][:], d.wqk[0]).then_inc(wqk_in, 16)
            sp.wait_ge(wqk_in, 16)
            sp.dma_start(wqk[1][:], d.wqk[1]).then_inc(wqk_in, 16)
            sp.wait_ge(const_set, 9)

            def step(n, p, at, attend, prepare):
                if not prepare:
                    return
                nxt = 1 - p
                _, pair = locate(n, at, 3)
                sp.wait_ge(prep_full, use(n, 1))
                sp.dma_start(wqk[nxt][:], d.wqk[bass.ds(pair, 1)].rearrange("a p h f -> p (a h) f")).then_inc(wqk_in, 16)
                for h in range(2):
                    u, w = q_hi_twice[nxt][h][:].bitcast(F32), k_hi_lo[nxt][h][:].bitcast(F32)
                    m2, s2 = q_lo_shift[nxt][h][:].bitcast(F32), k_hi_one[nxt][h][:].bitcast(F32)
                    sp.wait_ge(lo_done, 2 * (n + 1) + h + 1)
                    sp.dma_start(s2[0:DH, :], u[DH:P, :]).then_inc(moved1[h], 16)
                    sp.dma_start(m2[0:DH, :], w[0:DH, :]).then_inc(moved1[h], 16)
                    sp.wait_ge(moved1[h], 32 * (n + 2))
                    sp.dma_start(u[DH:P, :], u[0:DH, :]).then_inc(moved2[h], 16)
                    sp.dma_start(w[0:DH, :], s2[0:DH, :]).then_inc(moved2[h], 16)
                b1, pair1 = locate(n, at, 1)
                if not (isinstance(n, int) and n < 1):
                    sp.wait_ge(out_done, 2 * n)
                sp.dma_start(v_now[nxt][:], t.v_tm[:, bass.ds(b1 * TT, TT), :]).then_inc(vg_in, 16)
                sp.dma_start(g_now[nxt][:], t.g_all[:, bass.ds(pair1, 1), :].rearrange("p a o -> p (a o)")).then_inc(vg_in, 16)
                sp.wait_ge(shift_ready, n + 2)
                for h in range(2):
                    sp.dma_start(q_lo_shift[nxt][h][DH:DH + 1, :].bitcast(F32).rearrange("o (t q) -> o t q", t=TT),
                                 shift_fm[h * TT:(h + 1) * TT, :].bitcast(F32)).then_inc(shift_in, 16)

            schedule(step, sp.Fori)
            sp.wait_ge(wqk_in, 16 * (NP + 2))
            sp.wait_ge(shift_in, 32 * NP)

        @block.gpsimd
        def _(pool):
            for p in range(2):
                for h in range(2):
                    pool.memset(q_lo_shift[p][h][DH:P, :].bitcast(F32), 0.0)
                    pool.memset(k_hi_one[p][h][DH:P, :].bitcast(F32), 0.0).then_inc(const_set, 1)

            def step(n, p, at, attend, prepare):
                if isinstance(n, int) and n < 0:
                    return
                for c in range(NQC):
                    for k in range(1, TT):
                        u = c * TT + k
                        pool.wait_ge(exp_done, UNITS * n + u + 1)
                        if k == 1:
                            if not (isinstance(n, int) and n == 0):
                                pool.wait_ge(sum_done, 2 * n + c - 1)
                        else:
                            pool.wait_ge(added, 7 * (2 * n + c) + k - 1)
                        first = probs[(u - 1) % 4] if k == 1 else prob_sum[c]
                        pool.tensor_tensor(prob_sum[c][:], first[:], probs[u % 4][:], ALU.add).then_inc(added, 1)

            schedule(step, pool.Fori)

        @block.scalar
        def _(act):
            def step(n, p, at, attend, prepare):
                zero = isinstance(n, int) and n == 0
                if isinstance(n, int) and n < 0:
                    for h in range(2):
                        hi(n + 1, h, 1 - p, True)
                    return
                for u in range(UNITS + (not prepare) * 2):
                    if u < UNITS:
                        act.wait_ge(qk_done, UNITS * n + u + 1)
                        if not (zero and u < 4):
                            act.wait_ge(pv_done, UNITS * n + u - 3)
                            c, k = divmod((u - 4) % UNITS, TT)
                            if u >= 4:
                                act.wait_ge(added, 7 * (2 * n + c) + max(k, 1))
                            else:
                                act.wait_ge(added, 7 * (2 * n - 2 + c) + k)
                        act.activation(probs[u % 4][:], ps_s[:, u % 2], ACT.Exp, scale=DH ** -0.5).then_inc(exp_done, 1)
                    if u == 1 and not zero:
                        copy_o(2 * n - 1)
                    if u == 9:
                        copy_o(2 * n)
                    if u == UNITS + 1:
                        copy_o(2 * n + 1)
                    if prepare and u in (0, 1):
                        hi(n + 1, u, 1 - p, False)

            def hi(m, h, par, start):
                act.wait_ge(rot_done, 2 * m + h + 1)
                if not start and h == 0 and not (isinstance(m, int) and m < 2):
                    act.wait_ge(qk_done, UNITS * (m - 1))
                act.copy(q_hi_twice[par][h][:], rot[h][:]).then_inc(hi_done, 1)

            def copy_o(c):
                act.wait_ge(pv_done, TT * (c + 1))
                if not (isinstance(c, int) and c == 0):
                    act.wait_ge(norm_done, c)
                act.copy(o_raw[:], ps_o[:]).then_inc(o_copied, 1)

            schedule(step, act.Fori)

        @block.vector
        def _(dve):
            dve.memset(ones[:], 1.0).then_inc(const_set, 1)
            for p in range(2):
                for h in range(2):
                    dve.wait_ge(const_set, 5)
                    dve.memset(k_hi_one[p][h][DH:DH + 1, :].bitcast(F32), 1.0).then_inc(const_set, 1)

            def rope(m, base, h):
                done = 2 * m + h
                if not (isinstance(m, int) and m == 0):
                    dve.wait_ge(lo_done, 2 * m - 1 + h)
                dve.wait_ge(prep_full, base + h + 1)
                dve.tensor_tensor(rot[h][:], ps_p[:], t.cos[:], ALU.mult).then_inc(cos_done, 1)
                dve.stream_shuffle(swapped[h][:], ps_p[:], SWAP).then_inc(prep_read, 1)
                dve.wait_ge(prep_read, base + h + 1)
                dve.tensor_tensor(swapped[h][:], swapped[h][:], t.sin[:], ALU.mult).then_inc(sin_done, 1)
                dve.wait_ge(sin_done, done + 1)
                dve.wait_ge(cos_done, done + 1)
                dve.tensor_tensor(rot[h][:], rot[h][:], swapped[h][:], ALU.add).then_inc(rot_done, 1)

            def lo(m, h, par):
                dve.wait_ge(hi_done, 2 * m + h + 1)
                dve.tensor_tensor(k_hi_lo[par][h][:], rot[h][:], q_hi_twice[par][h][:].bitcast(F32),
                                  ALU.subtract).then_inc(lo_done, 1)

            def normalise(c):
                dve.wait_ge(sum_done, c + 1)
                dve.reciprocal(recip[:], ps_x[:]).then_inc(recip_done, 1)
                dve.wait_ge(recip_done, c + 1)
                dve.wait_ge(o_copied, c + 1)
                if not (isinstance(c, int) and c == 0):
                    dve.wait_ge(out_done, c)
                dve.tensor_tensor(o_norm[:], o_raw[:], recip[:], ALU.mult).then_inc(norm_done, 1)

            def add_y(c, batch, half):
                dve.wait_ge(out_done, c + 1)
                if not (isinstance(c, int) and c == 0):
                    dve.wait_ge(y_added, c)
                at = t.y_fm[:, bass.ds(batch * S + half * QC, QC)]
                dve.tensor_tensor(at, at, ps_x[:], ALU.add).then_inc(y_added, 1)

            def step(n, p, at, attend, prepare):
                past = not (isinstance(n, int) and n < 1)
                nxt = 1 - p
                if prepare:
                    for h in range(2):
                        lo(n + 1, h, nxt)
                    rope(n + 2, use(n, 0), 0)
                if past:
                    normalise(2 * n - 1)
                if prepare:
                    rope(n + 2, use(n, 0), 1)
                if past:
                    add_y(2 * n - 1, locate(n, at, -1)[0], 1)
                now = not (isinstance(n, int) and n < 0)
                for j in range(2 * TT):
                    if prepare:
                        dve.wait_ge(prep_full, use(n, 2 + j) + 1)
                        if j == 0:
                            dve.wait_ge(neg_done, n + 1) if not (isinstance(n, int) and n < 0) else None
                        dve.tensor_reduce(maxima[:, j:j + 1], ps_p[:], AX.X, ALU.max).then_inc(prep_read, 1)
                    if j == 11 and now:
                        normalise(2 * n)
                    if j == 15 and now:
                        add_y(2 * n, locate(n, at, 0)[0], 0)
                if prepare:
                    dve.wait_ge(prep_read, use(n, 2 + 2 * TT))
                    if not (isinstance(n, int) and n < 0):
                        dve.wait_ge(shift_turned, n + 1)
                    dve.tensor_scalar(shift_tm[:], maxima[:], -1.0, None, ALU.mult).then_inc(neg_done, 1)
                    dve.wait_ge(shift_turned, n + 2)
                    if not (isinstance(n, int) and n < 0):
                        dve.wait_ge(shift_in, 32 * (n + 1))
                    dve.tensor_copy(shift_fm[:], ps_p[0:2 * TT, 0:P]).then_inc(shift_ready, 1)
                if not prepare:
                    normalise(2 * n + 1)
                    add_y(2 * n + 1, locate(n, at, 0)[0], 1)

            for h in range(2):
                rope(0, 0, h)
            schedule(step, dve.Fori)

        @block.tensor
        def _(pe):
            pe.wait_ge(const_set, 9)

            def project(m, par, at, base, h):
                batch = at
                pe.wait_ge(wqk_in, 16 * (m + 1))
                if not (isinstance(base, int) and base + h == 0):
                    pe.wait_ge(prep_read, base + h)
                if h == 0 and not (isinstance(m, int) and m < 2):
                    pe.wait_ge(shift_ready, m - 1)
                for c in range(NQC):
                    last = pe.matmul(ps_p[:, c * QC:(c + 1) * QC], wqk[par][:, h],
                                     t.c_fm[:, bass.ds(batch * S + c * QC, QC)], start=True, stop=True)
                last.then_inc(prep_full, 1)

            def scores(n, p, u):
                c, k = divmod(u, TT)
                if not (isinstance(n, int) and n == 0 and u < 2):
                    pe.wait_ge(exp_done, UNITS * n + u - 1)
                if u == 0:
                    pe.wait_ge(shift_in, 32 * (n + 1))
                for h in range(2):
                    if u == 0:
                        pe.wait_ge(moved2[h], 32 * (n + 1))
                    q, keys = slice(c * QC, (c + 1) * QC), slice(k * P, (k + 1) * P)
                    pe.matmul(ps_s[:, u % 2, h], k_hi_lo[p][h][:, keys], q_hi_twice[p][h][:, q], start=True, stop=False)
                    last = pe.matmul(ps_s[:, u % 2, h], k_hi_one[p][h][:, keys], q_lo_shift[p][h][:, q], start=False, stop=True)
                last.then_inc(qk_done, 1)

            def weigh(n, p, u):
                c, k = divmod(u, TT)
                pe.wait_ge(exp_done, UNITS * n + u + 1)
                if k == 0:
                    if u == 0:
                        pe.wait_ge(vg_in, 32 * (n + 1))
                    if not (isinstance(n, int) and n == 0 and c == 0):
                        pe.wait_ge(o_copied, 2 * n + c)
                for h in range(2):
                    last = pe.matmul(ps_o[h * DH:(h + 1) * DH, :], v_now[p][:, k], probs[u % 4][:, h],
                                     start=(k == 0), stop=(k == TT - 1))
                last.then_inc(pv_done, 1)

            def sums(c, half):
                pe.wait_ge(added, 7 * (c + 1))
                if not (isinstance(c, int) and c == 0):
                    pe.wait_ge(y_added, c)
                for h in range(2):
                    last = pe.matmul(ps_x[h * DH:(h + 1) * DH, :], ones[:], prob_sum[half][:, h], start=True, stop=True)
                last.then_inc(sum_done, 1)

            def project_out(c, par):
                pe.wait_ge(norm_done, c + 1)
                pe.matmul(ps_x[:], g_now[par][:], o_norm[:], start=True, stop=True).then_inc(out_done, 1)

            def maximum(n, nxt, j):
                h, k = divmod(j, TT)
                if k == 0:
                    pe.wait_ge(moved2[h], 32 * (n + 2))
                pe.wait_ge(prep_read, use(n, 2 + j))
                for c in range(NQC):
                    last = pe.matmul(ps_p[:, c * QC:(c + 1) * QC], q_hi_twice[nxt][h][:, k * P:(k + 1) * P],
                                     k_hi_lo[nxt][h][:, c * QC:(c + 1) * QC], start=True, stop=True)
                last.then_inc(prep_full, 1)

            def turn_shift(n):
                pe.wait_ge(neg_done, n + 2)
                pe.wait_ge(prep_read, use(n, 2 + 2 * TT))
                pe.transpose(ps_p[0:2 * TT, 0:P], shift_tm[:], t.ident[:]).then_inc(shift_turned, 1)

            def step(n, p, at, attend, prepare):
                nxt = 1 - p
                past = not (isinstance(n, int) and n < 1)
                now = not (isinstance(n, int) and n < 0)
                done = 0
                for u in range(UNITS):
                    if now:
                        scores(n, p, u)
                        if u >= 2:
                            weigh(n, p, u - 2)
                        elif past:
                            weigh(n - 1, 1 - p, UNITS - 2 + u)
                    if prepare and u == 0:
                        project(n + 2, p, locate(n, at, 2)[0], use(n, 0), 0)
                    if prepare and u == 2:
                        project(n + 2, p, locate(n, at, 2)[0], use(n, 0), 1)
                    if u == 3 and past:
                        sums(2 * n - 1, 1)
                    if u == 5 and past:
                        project_out(2 * n - 1, 1 - p)
                    if u == 11 and now:
                        sums(2 * n, 0)
                    if u == 13 and now:
                        project_out(2 * n, p)
                    if prepare and u >= 5:
                        for _ in range(2):
                            if done < 2 * TT:
                                maximum(n, nxt, done)
                                done += 1
                    if prepare and u == 14:
                        turn_shift(n)
                if not prepare:
                    weigh(n, p, UNITS - 2)
                    weigh(n, p, UNITS - 1)
                    sums(2 * n + 1, 1)
                    project_out(2 * n + 1, p)

            for h in range(2):
                project(0, 0, 0, 0, h)
            schedule(step, pe.Fori)


LN_STEPS = CT + 7 + RSQRT_STEPS


class Bag:
    pass


def norm_buffers(sb, sem, name):
    w = Bag()
    w.stats = sb(f"{name}_stats", [P, CT, 6])
    w.mean, w.gap, w.sq, w.var, w.half, w.rstd = (sb(f"{name}_{x}", [P, CT]) for x in ("mean", "gap", "sq", "var", "half", "rstd"))
    w.chain = sem(f"{name}_chain")
    return w


def layer_norm(dve, w, base, src, dst, done):
    for k in range(CT):
        dve.bn_stats(w.stats[:, k], src(k)).then_inc(w.chain, 1)
    even, odd, even_sq, odd_sq = (w.stats[:, :, j] for j in (1, 4, 2, 5))
    dve.wait_ge(w.chain, base + CT)
    dve.tensor_tensor(w.mean[:], even, odd, ALU.add).then_inc(w.chain, 1)
    dve.tensor_tensor(w.gap[:], even, odd, ALU.subtract).then_inc(w.chain, 1)
    dve.tensor_tensor(w.sq[:], even_sq, odd_sq, ALU.add).then_inc(w.chain, 1)
    dve.wait_ge(w.chain, base + CT + 3)
    dve.tensor_scalar(w.mean[:], w.mean[:], 0.5, None, ALU.mult).then_inc(w.chain, 1)
    dve.scalar_tensor_tensor(w.gap[:], w.gap[:], 0.25, w.gap[:], ALU.mult, ALU.mult).then_inc(w.chain, 1)
    dve.tensor_scalar(w.sq[:], w.sq[:], 1.0 / D, LN_EPS, ALU.mult, ALU.add).then_inc(w.chain, 1)
    dve.wait_ge(w.chain, base + CT + 6)
    dve.tensor_tensor(w.var[:], w.gap[:], w.sq[:], ALU.add).then_inc(w.chain, 1)
    dve.wait_ge(w.chain, base + CT + 7)
    rsqrt_on_vector(dve, w.chain, base + CT + 7, w.var[:], w.half[:], w.rstd[:])
    for k in range(CT):
        dve.tensor_scalar(dst(k), src(k), w.mean[:, k:k + 1], w.rstd[:, k:k + 1],
                          ALU.subtract, ALU.mult).then_inc(done, 1)


NCH = B * S // QC
LANES = 2
E, EI, EP = 8, 64, 4
NG, GS = 4, 2
ROUTE_STEPS = 16


def experts(nc, t, d):
    with ExitStack() as ctx:
        sb = lambda n, s, dt=F32: ctx.enter_context(nc.sbuf_tensor(n, s, dt))
        sem = semaphores(nc, ctx, t)
        lanes = range(LANES)
        weights_in = sem("c_weights_in")
        gate_w = sb("gate_w", [P, E])
        bias = sb("bias", [P, CT, E])
        before_g = sb("before_g", [P, CT, NG, NG])
        before_e = sb("before_e", [P, CT, E, E])
        w_gate, w_up, w_down = (sb(n, [P, EP, P]) for n in ("w_gate", "w_up", "w_down"))
        y_now = [sb(f"y_now{x}", [P, QC]) for x in lanes]
        x1_tm = [sb(f"x1_tm{x}", [P, CT, D]) for x in lanes]
        x1_fm = [sb(f"x1_fm{x}", [P, QC]) for x in lanes]
        scores = [sb(f"scores{x}", [P, CT, E]) for x in lanes]
        choice = [sb(f"choice{x}", [P, CT, E]) for x in lanes]
        group = [sb(f"group{x}", [P, CT, NG]) for x in lanes]
        gt = [sb(f"gt{x}", [P, CT, E, E]) for x in lanes]
        eq = [sb(f"eq{x}", [P, CT, E, E]) for x in lanes]
        rank = [sb(f"rank{x}", [P, CT, E]) for x in lanes]
        rank_g = [sb(f"rank_g{x}", [P, CT, NG]) for x in lanes]
        weight = [sb(f"weight{x}", [P, CT, E]) for x in lanes]
        total = [sb(f"total{x}", [P, CT]) for x in lanes]
        spread = [sb(f"spread{x}", [P, CT, E, EI]) for x in lanes]
        sig = [sb(f"sig{x}", [P, QC]) for x in lanes]
        hid = [sb(f"hid{x}", [P, QC]) for x in lanes]
        z_tm = [sb(f"z_tm{x}", [P, CT, D]) for x in lanes]
        x2_now = [sb(f"x2_now{x}", [P, CT, D]) for x in lanes]
        x2_fm = [sb(f"x2_fm{x}", [P, QC]) for x in lanes]
        ln = [norm_buffers(sb, sem, f"c_ln{x}") for x in lanes]
        ps = [ctx.enter_context(nc.psum_tensor(f"ps_c{x}", [P, 4, QC], F32)) for x in lanes]

        each = lambda n: [sem(f"c_{n}{x}") for x in lanes]
        y_in, y_turned, x1_done, x1_turned, x1_ready = map(each, ("y_in", "y_turned", "x1_done", "x1_turned", "x1_ready"))
        logits_done, scores_ready, route, spread_done = map(each, ("logits_done", "scores_ready", "route", "spread_done"))
        spread_total = each("spread_total")
        gate_up_done, sig_done, mul1, mul2, hid_done, down_done = map(
            each, ("gate_up_done", "sig_done", "mul1", "mul2", "hid_done", "down_done"))
        z_done, x2_done, x2_kept, x2_turned, x2_copied, x2_fm_kept = map(
            each, ("z_done", "x2_done", "x2_kept", "x2_turned", "x2_copied", "x2_fm_kept"))
        block = ctx.enter_context(nc.Block())
        ITER = NCH // LANES

        def column(i, x):
            return bass.ds((i * LANES + x) * QC, QC)

        @block.sync
        def _(sp):
            for dst, src in ((gate_w, d.gate_w), (bias, d.route_bias), (before_g, d.before_g), (before_e, d.before_e),
                             (w_gate, d.w_gate), (w_up, d.w_up), (w_down, d.w_down)):
                sp.dma_start(dst[:], src).then_inc(weights_in, 16)
            with sp.Fori(0, ITER) as i:
                for x in lanes:
                    sp.wait_ge(y_turned[x], i)
                    sp.dma_start(y_now[x][:], t.y_fm[:, column(i, x)]).then_inc(y_in[x], 16)
                for x in lanes:
                    sp.wait_ge(x2_done[x], CT * (i + 1))
                    sp.dma_start(t.x2_tm[:, bass.ds((i * LANES + x) * CT, CT), :], x2_now[x][:]).then_inc(x2_kept[x], 16)
                for x in lanes:
                    sp.wait_ge(x2_copied[x], i + 1)
                    sp.dma_start(t.y_fm[:, column(i, x)], x2_fm[x][:]).then_inc(x2_fm_kept[x], 16)
            for x in lanes:
                sp.wait_ge(x2_kept[x], 16 * ITER)
                sp.wait_ge(x2_fm_kept[x], 16 * ITER)

        @block.scalar
        def _(act):
            act.wait_ge(weights_in, 16 * 7)
            with act.Fori(0, ITER) as i:
                for x in lanes:
                    act.wait_ge(x1_turned[x], i + 1)
                    act.wait_ge(gate_up_done[x], EP * i)
                    act.copy(x1_fm[x][:], ps[x][:, 1]).then_inc(x1_ready[x], 1)
                for x in lanes:
                    act.wait_ge(logits_done[x], i + 1)
                    act.wait_ge(spread_done[x], i)
                    act.activation(scores[x][:].rearrange("p k e -> p (k e)"), ps[x][:, 0, 0:CT * E],
                                   ACT.Sigmoid).then_inc(scores_ready[x], 1)
                for e in range(EP):
                    for x in lanes:
                        act.wait_ge(gate_up_done[x], EP * i + e + 1)
                        act.wait_ge(mul1[x], EP * i + e)
                        act.activation(sig[x][:], ps[x][:, 1], ACT.Sigmoid).then_inc(sig_done[x], 1)
                for x in lanes:
                    act.wait_ge(x2_turned[x], i + 1)
                    act.wait_ge(x2_fm_kept[x], 16 * i)
                    act.copy(x2_fm[x][:], ps[x][:, 1]).then_inc(x2_copied[x], 1)

        @block.vector
        def _(dve):
            dve.wait_ge(weights_in, 16 * 7)
            with dve.Fori(0, ITER) as i:
                for x in lanes:
                    dve.wait_ge(y_turned[x], i + 1)
                    dve.wait_ge(z_done[x], i)
                    tile = lambda k, x=x: ps[x][:, 0, k * P:(k + 1) * P]
                    layer_norm(dve, ln[x], 2 * LN_STEPS * i, tile, lambda k, x=x: x1_tm[x][:, k], x1_done[x])
                for x in lanes:
                    steps = 0

                    def then(ins, x=x):
                        nonlocal steps
                        steps += 1
                        ins.then_inc(route[x], 1)
                        dve.wait_ge(route[x], ROUTE_STEPS * i + steps)

                    def ranks(out, score, n, before, x=x):
                        g, q = (m[x][:, :, 0:n, 0:n] for m in (gt, eq))
                        b = score.unsqueeze(2).broadcast_to([P, CT, n, n])
                        a = score.unsqueeze(3).broadcast_to([P, CT, n, n])
                        then(dve.tensor_tensor(g, b, a, ALU.is_gt))
                        then(dve.tensor_tensor(q, b, a, ALU.is_equal))
                        then(dve.tensor_tensor(q, q, before[:], ALU.mult))
                        then(dve.tensor_tensor(g, g, q, ALU.add))
                        then(dve.tensor_reduce(out[:], g, AX.X, ALU.add))

                    dve.wait_ge(scores_ready[x], i + 1)
                    then(dve.tensor_tensor(choice[x][:], scores[x][:], bias[:], ALU.add))
                    then(dve.tensor_tensor(group[x][:], choice[x][:, :, 0::GS], choice[x][:, :, 1::GS], ALU.add))
                    ranks(rank_g[x], group[x][:], NG, before_g)
                    kept = rank_g[x][:].rearrange("p k g -> p (k g)").unsqueeze(2).broadcast_to([P, CT * NG, GS])
                    by_group = choice[x][:].rearrange("p k (g s) -> p (k g) s", g=NG)
                    then(dve.scalar_tensor_tensor(by_group, kept, 2.0, by_group, ALU.is_lt, ALU.mult))
                    ranks(rank[x], choice[x][:], E, before_e)
                    then(dve.scalar_tensor_tensor(weight[x][:], rank[x][:], 2.0, scores[x][:], ALU.is_lt, ALU.mult))
                    then(dve.tensor_reduce(total[x][:], weight[x][:], AX.X, ALU.add))
                    dve.tensor_scalar(total[x][:], total[x][:], 1e-20, None, ALU.add).then_inc(route[x], 1)
                    assert steps == ROUTE_STEPS - 1 + 0, steps
                for x in lanes:
                    dve.wait_ge(route[x], ROUTE_STEPS * (i + 1))
                    dve.reciprocal(total[x][:], total[x][:]).then_inc(spread_total[x], 1)
                    dve.wait_ge(spread_total[x], i + 1)
                    dve.tensor_tensor(spread[x][:], weight[x][:].unsqueeze(3).broadcast_to([P, CT, E, EI]),
                                      total[x][:].unsqueeze(2).unsqueeze(3).broadcast_to([P, CT, E, EI]),
                                      ALU.mult).then_inc(spread_done[x], 1)
                for e in range(EP):
                    for x in lanes:
                        n = EP * i + e
                        dve.wait_ge(sig_done[x], n + 1)
                        dve.wait_ge(down_done[x], n)
                        dve.tensor_tensor(hid[x][:], sig[x][:], ps[x][:, 1], ALU.mult).then_inc(mul1[x], 1)
                        dve.wait_ge(mul1[x], n + 1)
                        dve.tensor_tensor(hid[x][:], hid[x][:], ps[x][:, 2], ALU.mult).then_inc(mul2[x], 1)
                        dve.wait_ge(mul2[x], n + 1)
                        dve.tensor_tensor(hid[x][:], hid[x][:], ps[x][:, 3], ALU.mult).then_inc(hid_done[x], 1)
                for x in lanes:
                    dve.wait_ge(down_done[x], EP * (i + 1))
                    dve.tensor_tensor(z_tm[x][:].rearrange("p k f -> p (k f)"), x1_tm[x][:].rearrange("p k f -> p (k f)"),
                                      ps[x][:, 0], ALU.add).then_inc(z_done[x], 1)
                for x in lanes:
                    dve.wait_ge(z_done[x], i + 1)
                    dve.wait_ge(x2_kept[x], 16 * i)
                    dve.wait_ge(x2_turned[x], i)
                    layer_norm(dve, ln[x], 2 * LN_STEPS * i + LN_STEPS, lambda k, x=x: z_tm[x][:, k],
                               lambda k, x=x: x2_now[x][:, k], x2_done[x])

        @block.tensor
        def _(pe):
            pe.wait_ge(weights_in, 16 * 7)
            with pe.Fori(0, ITER) as i:
                def turn(bank, src, x):
                    for k in range(CT):
                        last = pe.transpose(ps[x][:, bank, k * P:(k + 1) * P], src(k), t.ident[:])
                    return last

                for x in lanes:
                    pe.wait_ge(y_in[x], 16 * (i + 1))
                    pe.wait_ge(z_done[x], i)
                    turn(0, lambda k: y_now[x][:, k * P:(k + 1) * P], x).then_inc(y_turned[x], 1)
                for x in lanes:
                    pe.wait_ge(x1_done[x], CT * (i + 1))
                    pe.wait_ge(x2_copied[x], i)
                    turn(1, lambda k: x1_tm[x][:, k], x).then_inc(x1_turned[x], 1)
                for x in lanes:
                    pe.wait_ge(x1_ready[x], i + 1)
                    for k in range(CT):
                        last = pe.matmul(ps[x][:, 0, k * E:(k + 1) * E], x1_fm[x][:, k * P:(k + 1) * P], gate_w[:],
                                         start=True, stop=True, skip_group_check=True)
                    last.then_inc(logits_done[x], 1)
                for e in range(EP):
                    for x in lanes:
                        n = EP * i + e
                        pe.wait_ge(hid_done[x], n)
                        if e == 0:
                            pe.wait_ge(scores_ready[x], i + 1)
                        pe.matmul(ps[x][:, 1], w_gate[:, e], x1_fm[x][:], start=True, stop=True)
                        pe.matmul(ps[x][:, 2], w_up[:, e], x1_fm[x][:], start=True, stop=True)
                        if e == 0:
                            pe.wait_ge(spread_done[x], i + 1)
                        two = lambda k: spread[x][:, k, 2 * e:2 * e + 2].rearrange("p e r -> p (e r)")
                        turn(3, two, x).then_inc(gate_up_done[x], 1)
                    for x in lanes:
                        pe.wait_ge(hid_done[x], EP * i + e + 1)
                        for k in range(CT):
                            last = pe.matmul(ps[x][:, 0, k * P:(k + 1) * P], hid[x][:, k * P:(k + 1) * P], w_down[:, e],
                                             start=(e == 0 and k == 0), stop=(e == EP - 1), skip_group_check=True)
                        last.then_inc(down_done[x], 1)
                for x in lanes:
                    pe.wait_ge(x2_done[x], CT * (i + 1))
                    turn(1, lambda k: x2_now[x][:, k], x).then_inc(x2_turned[x], 1)


AH, AD = 16, 8
AG, AR = 4, 4
SLOT = P // AR
Z_EPS = 1e-6
STEPS = [(c, k) for c in range(NQC) for k in range(CT * (c + 1))]
HALVES = 2 * len(STEPS)


def causal(nc, t, d):
    with ExitStack() as ctx:
        sb = lambda n, s, dt=F32: ctx.enter_context(nc.sbuf_tensor(n, s, dt))
        sem = semaphores(nc, ctx, t)
        weights_in = sem("d_weights_in")
        wq, wk = sb("wq1", [P, AG, P]), sb("wk1", [P, AG, P])
        wv, wo = sb("wv1", [P, D]), sb("wo1", [P, D])
        rows = sb("part_rows", [P, 4])
        mask = sb("causal_mask", [P, 2, P])
        shift = sb("square_shift", [P, 1])
        x_now = sb("x_now", [P, S])
        vx = sb("vx", [P, TT, AH, SLOT])
        q_rows = [[sb(f"q_rows{p}{r}", [P, S], F32R) for r in range(AR)] for p in range(2)]
        k_rows = [sb(f"k_rows{p}", [P, S], F32R) for p in range(2)]
        q_hi, k_hi = sb("q_hi", [P, QC], F32R), sb("k_hi", [P, QC], F32R)
        q_part, k_part = sb("q_part", [P, QC]), sb("k_part", [P, QC])
        a = [sb(f"a{i}", [P, 2, QC]) for i in range(4)]
        o_rows = [sb(f"o_rows{i}", [P, QC]) for i in range(2)]
        z = [sb(f"z{i}", [P, CT, AR]) for i in range(2)]
        out_tm = sb("out_tm", [P, TT, D])
        out_fm = [sb(f"out_fm{c}", [P, QC]) for c in range(NQC)]
        z_tm = [sb(f"sum_tm{c}", [P, CT, D]) for c in range(NQC)]
        x3_tm = [sb(f"x3_tm{c}", [P, CT, D]) for c in range(NQC)]
        x3_fm = [sb(f"x3_fm{c}", [P, QC]) for c in range(NQC)]
        ln = [norm_buffers(sb, sem, f"d_ln{c}") for c in range(NQC)]
        ps_s = [ctx.enter_context(nc.psum_tensor(f"ps_d_s{i}", [P, 2, QC], F32)) for i in range(2)]
        bank = lambda n: ctx.enter_context(nc.psum_tensor(n, [P, QC], F32))
        ps_o, ps_t, ps_q, ps_k = bank("ps_d_o"), bank("ps_d_t"), bank("ps_d_q"), bank("ps_d_k")
        turn_bank, sum_bank = [ps_q, ps_o], [ps_k, ps_t]

        vx_set, vx_zero = sem("d_vx_set"), sem("d_vx_zero")
        x_in, v_done, v_copied = sem("d_x_in"), sem("d_v_done"), sem("d_v_copied")
        proj_done, split_done, rows_done = sem("d_proj_done"), sem("d_split_done"), sem("d_rows_done")
        qk_done, squared, a_ready, pv_done = sem("d_qk_done"), sem("d_squared"), sem("d_a_ready"), sem("d_pv_done")
        o_copied, o_turned, z_ready, z_recip, out_done = map(sem, ("d_o_copied", "d_o_turned", "d_z_ready", "d_z_recip", "d_out_done"))
        each = lambda n: [sem(f"d_{n}{c}") for c in range(NQC)]
        y_turned, y_ready, wo_done, sum_done, x3_done, x3_turned, x3_copied, x3_kept = map(
            each, ("y_turned", "y_ready", "wo_done", "sum_done", "x3_done", "x3_turned", "x3_copied", "x3_kept"))
        block = ctx.enter_context(nc.Block())
        PROJ = AG * NQC
        AHEAD = {(0, 2): 0, (1, 1): 1}

        def each_step():
            for g in range(AG):
                for s, (c, k) in enumerate(STEPS):
                    yield g, s, c, k, max(0, (k - CT * c) * P)

        def copy_o(act, b, g, c):
            n = NQC * g + c - 1
            steps = len(STEPS) * (n // NQC) + (CT if n % NQC == 0 else len(STEPS))
            act.wait_ge(pv_done, len(STEPS) * AG * b + steps)
            act.wait_ge(o_turned, PROJ * b + max(n - 1, 0))
            act.copy(o_rows[n % 2][:], ps_o[:]).then_inc(o_copied, 1)

        @block.sync
        def _(sp):
            for dst, src in ((wq, d.wq1), (wk, d.wk1), (wv, d.wv1), (wo, d.wo1), (rows, d.part_rows), (mask, d.causal_mask)):
                sp.dma_start(dst[:], src).then_inc(weights_in, 16)
            with sp.Fori(0, B) as b:
                sp.wait_ge(proj_done, PROJ * b)
                sp.dma_start(x_now[:], t.y_fm[:, bass.ds(b * S, S)]).then_inc(x_in, 16)
                for c in range(NQC):
                    sp.wait_ge(x3_copied[c], b + 1)
                    sp.dma_start(t.y_fm[:, bass.ds(b * S + c * QC, QC)], x3_fm[c][:]).then_inc(x3_kept[c], 16)
            for c in range(NQC):
                sp.wait_ge(x3_kept[c], 16 * B)

        @block.gpsimd
        def _(pool):
            pool.memset(vx[:], 0.0).then_inc(vx_zero, 1)
            for p in range(2):
                for r in range(AR):
                    pool.memset(q_rows[p][r][:].bitcast(F32), 0.0).then_inc(vx_set, 1)

        @block.scalar
        def _(act):
            act.wait_ge(weights_in, 16 * 6)
            act.wait_ge(vx_set, 2 * AR + 2)
            with act.Fori(0, B) as b:
                def split(g, c):
                    n = PROJ * b + NQC * g + c
                    act.wait_ge(proj_done, n + 1)
                    act.wait_ge(rows_done, n)
                    act.copy(q_hi[:], ps_q[:])
                    act.mul(q_part[:], ps_q[:], rows[:, 0:1])
                    act.copy(k_hi[:], ps_k[:])
                    act.mul(k_part[:], ps_k[:], rows[:, 2:3]).then_inc(split_done, 1)

                split(0, 0)
                split(0, 1)
                for g, s, c, k, off in each_step():
                    for r in range(2):
                        half = HALVES * g + 2 * s + r
                        act.wait_ge(qk_done, HALVES * AG * b + half + 1)
                        act.wait_ge(pv_done, len(STEPS) * AG * b + max(len(STEPS) * g + s - 1, 0))
                        act.activation(a[half % 4][:, :, off:], ps_s[r][:, :, off:], ACT.Square, bias=shift[:],
                                       scale=0.25).then_inc(squared, 1)
                    if g < AG - 1 and (c, k) in AHEAD:
                        split(g + 1, AHEAD[c, k])
                    if k == 0 and (g or c):
                        copy_o(act, b, g, c)
                    if (g, c, k) == (AG - 1, NQC - 1, TT - 1):
                        copy_o(act, b, AG, 0)
                for c in range(NQC):
                    act.wait_ge(y_turned[c], b + 1)
                    act.copy(out_fm[c][:], turn_bank[c][:]).then_inc(y_ready[c], 1)
                for c in range(NQC):
                    act.wait_ge(x3_turned[c], b + 1)
                    act.wait_ge(x3_kept[c], 16 * b)
                    act.copy(x3_fm[c][:], turn_bank[c][:]).then_inc(x3_copied[c], 1)

        @block.vector
        def _(dve):
            dve.memset(shift[:], 0.5 ** 0.5).then_inc(vx_set, 1)
            dve.wait_ge(vx_zero, 1)
            dve.memset(vx[:, :, :, AD:AD + 1], 1.0).then_inc(vx_set, 1)
            dve.wait_ge(vx_set, 2 * AR + 2)
            dve.wait_ge(weights_in, 16 * 6)
            with dve.Fori(0, B) as b:
                def make_rows(g, c):
                    n = PROJ * b + NQC * g + c
                    at = slice(c * QC, (c + 1) * QC)
                    dve.wait_ge(split_done, n + 1)
                    dve.wait_ge(qk_done, HALVES * AG * b + max(HALVES * (g - 1), 0))
                    for r in range(AR):
                        q = slice(r * SLOT, (r + 1) * SLOT)
                        dve.scalar_tensor_tensor(q_rows[g % 2][r][q, at], q_hi[q, :].bitcast(F32), rows[q, 1:2], q_part[q, :],
                                                 ALU.mult, ALU.add)
                    dve.scalar_tensor_tensor(k_rows[g % 2][:, at], k_hi[:].bitcast(F32), rows[:, 3:4], k_part[:],
                                             ALU.mult, ALU.add).then_inc(rows_done, 1)

                def normalise(n):
                    g, c = divmod(n, NQC)
                    turned = ps_t[:].rearrange("p (k r f) -> p k r f", k=CT, r=AR)
                    dve.wait_ge(o_turned, PROJ * b + n + 1)
                    dve.wait_ge(out_done, PROJ * b + max(n - 1, 0))
                    dve.tensor_scalar(z[n % 2][:], turned[:, :, :, AD], Z_EPS, None, ALU.add).then_inc(z_ready, 1)
                    dve.wait_ge(z_ready, PROJ * b + n + 1)
                    dve.reciprocal(z[n % 2][:], z[n % 2][:]).then_inc(z_recip, 1)
                    dve.wait_ge(z_recip, PROJ * b + n + 1)
                    to = out_tm[:, CT * c:CT * (c + 1), AR * AD * g:AR * AD * (g + 1)]
                    dve.tensor_tensor(to.rearrange("p k (r f) -> p k r f", r=AR), turned[:, :, :, 0:AD],
                                      z[n % 2][:].unsqueeze(3).broadcast_to([P, CT, AR, AD]), ALU.mult).then_inc(out_done, 1)

                for c in range(NQC):
                    dve.wait_ge(v_done, NQC * b + c + 1)
                    bank = (ps_q, ps_k)[c]
                    dve.tensor_copy(vx[:, CT * c:CT * (c + 1), :, 0:AD].rearrange("p k h f -> p (k h) f"),
                                    bank[:].rearrange("p (k f) -> p k f", f=AD)).then_inc(v_copied, 1)
                make_rows(0, 0)
                make_rows(0, 1)
                for g, s, c, k, off in each_step():
                    for r in range(2):
                        half = HALVES * g + 2 * s + r
                        buf = a[half % 4]
                        diagonal = k >= CT * c
                        dve.wait_ge(squared, HALVES * AG * b + half + 1)
                        full = off + P * diagonal
                        if diagonal:
                            last = dve.scalar_tensor_tensor(buf[:, :, off:full], buf[:, :, off:full], 0.5, mask[:],
                                                            ALU.add, ALU.mult)
                        if full < QC:
                            last = dve.tensor_scalar(buf[:, :, full:], buf[:, :, full:], 0.5, None, ALU.add)
                        last.then_inc(a_ready, 1)
                    if g < AG - 1 and (c, k) in AHEAD:
                        make_rows(g + 1, AHEAD[c, k])
                    if k == 1 and (g or c):
                        normalise(NQC * g + c - 1)
                normalise(PROJ - 1)
                for c in range(NQC):
                    dve.wait_ge(wo_done[c], b + 1)
                    dve.tensor_tensor(z_tm[c][:], sum_bank[c][:].rearrange("p (k f) -> p k f", k=CT),
                                      t.x2_tm[:, bass.ds(b * TT + c * CT, CT), :], ALU.add).then_inc(sum_done[c], 1)
                for c in range(NQC):
                    dve.wait_ge(sum_done[c], b + 1)
                    dve.wait_ge(x3_turned[c], b)
                    layer_norm(dve, ln[c], LN_STEPS * b, lambda k, c=c: z_tm[c][:, k], lambda k, c=c: x3_tm[c][:, k], x3_done[c])

        @block.tensor
        def _(pe):
            pe.wait_ge(weights_in, 16 * 6)
            pe.wait_ge(vx_set, 2 * AR + 2)
            with pe.Fori(0, B) as b:
                def project(g, c):
                    n = PROJ * b + NQC * g + c
                    at = slice(c * QC, (c + 1) * QC)
                    pe.wait_ge(split_done, n)
                    pe.matmul(ps_q[:], wq[:, g], x_now[:, at], start=True, stop=True)
                    pe.matmul(ps_k[:], wk[:, g], x_now[:, at], start=True, stop=True).then_inc(proj_done, 1)

                def scores(g, s, c, k, off):
                    for r in range(2):
                        half = HALVES * g + 2 * s + r
                        pe.wait_ge(squared, HALVES * AG * b + max(half - 1, 0))
                        for h in range(2):
                            last = pe.matmul(ps_s[r][:, h, off:], k_rows[g % 2][:, k * P:(k + 1) * P],
                                             q_rows[g % 2][2 * r + h][:, c * QC + off:(c + 1) * QC], start=True, stop=True)
                        last.then_inc(qk_done, 1)

                def weigh(g, s, c, k, off):
                    pe.wait_ge(a_ready, HALVES * AG * b + HALVES * g + 2 * s + 2)
                    if k == 0:
                        pe.wait_ge(o_copied, PROJ * b + NQC * g + c)
                    for r in range(AR):
                        half = HALVES * g + 2 * s + r // 2
                        last = pe.matmul(ps_o[r * SLOT:(r + 1) * SLOT, off:], vx[:, k, AR * g + r],
                                         a[half % 4][:, r % 2, off:], start=(k == 0), stop=(k == CT * (c + 1) - 1))
                    last.then_inc(pv_done, 1)

                def turn_o(n):
                    pe.wait_ge(o_copied, PROJ * b + n + 1)
                    pe.wait_ge(out_done, PROJ * b + n)
                    for k in range(CT):
                        last = pe.transpose(ps_t[:, k * P:(k + 1) * P], o_rows[n % 2][:, k * P:(k + 1) * P], t.ident[:])
                    last.then_inc(o_turned, 1)

                pe.wait_ge(x_in, 16 * (b + 1))
                for c in range(NQC):
                    pe.wait_ge((x3_copied, sum_done)[c][0], b)
                    for k in range(CT):
                        tile = CT * c + k
                        last = pe.matmul((ps_q, ps_k)[c][:, k * P:(k + 1) * P], x_now[:, tile * P:(tile + 1) * P], wv[:],
                                         start=True, stop=True, skip_group_check=True)
                    last.then_inc(v_done, 1)
                pe.wait_ge(v_copied, NQC * (b + 1))
                project(0, 0)
                project(0, 1)
                before = None
                for g, s, c, k, off in each_step():
                    if s == 0:
                        pe.wait_ge(rows_done, PROJ * b + NQC * (g + 1))
                    scores(g, s, c, k, off)
                    if before:
                        weigh(*before)
                    before = (g, s, c, k, off)
                    if g < AG - 1 and (c, k) in AHEAD:
                        project(g + 1, AHEAD[c, k])
                    if k == 1 and (g or c):
                        turn_o(NQC * g + c - 1)
                weigh(*before)
                turn_o(PROJ - 1)
                for c in range(NQC):
                    pe.wait_ge(out_done, PROJ * (b + 1))
                    for k in range(CT):
                        last = pe.transpose(turn_bank[c][:, k * P:(k + 1) * P], out_tm[:, CT * c + k], t.ident[:])
                    last.then_inc(y_turned[c], 1)
                for c in range(NQC):
                    pe.wait_ge(y_ready[c], b + 1)
                    for k in range(CT):
                        last = pe.matmul(sum_bank[c][:, k * P:(k + 1) * P], out_fm[c][:, k * P:(k + 1) * P], wo[:],
                                         start=True, stop=True, skip_group_check=True)
                    last.then_inc(wo_done[c], 1)
                for c in range(NQC):
                    pe.wait_ge(x3_done[c], CT * (b + 1))
                    for k in range(CT):
                        last = pe.transpose(turn_bank[c][:, k * P:(k + 1) * P], x3_tm[c][:, k], t.ident[:])
                    last.then_inc(x3_turned[c], 1)


QB = 3
LORA = 32
QGROUP = 16
HALF_RANGE = 7.5


def qlora(nc, t, d):
    with ExitStack() as ctx:
        sb = lambda n, s, dt=F32: ctx.enter_context(nc.sbuf_tensor(n, s, dt))
        sem = semaphores(nc, ctx, t)
        lanes = range(LANES)
        NW = 2 * QB
        weights_in = sem("e_weights_in")
        q_in = sb("q_in", [P, NW, D], I32)
        scale = sb("scale", [P, NW, D // QGROUP])
        la, lb = sb("la", [LORA, NW, D]), sb("lb", [LORA, NW, D])
        w = sb("w", [P, NW, D])
        w_t = sb("w_t", [P, NW, D])
        bias1 = sb("bias1", [P, QB, D])
        cols = sb("cols", [P, 3, QB])
        h_fm = [sb(f"h_fm{x}", [P, QC]) for x in lanes]
        y_tm = [sb(f"y_tm{x}", [P, CT, D]) for x in lanes]
        n_tm = [sb(f"n_tm{x}", [P, CT, D]) for x in lanes]
        g_fm = [sb(f"g_fm{x}", [P, QC]) for x in lanes]
        out_tm = [sb(f"out_tm{x}", [P, CT, D]) for x in lanes]
        ln = [norm_buffers(sb, sem, f"e_ln{x}") for x in lanes]
        ps = [ctx.enter_context(nc.psum_tensor(f"ps_e{x}", [P, 4, QC], F32)) for x in lanes]
        each = lambda n: [sem(f"e_{n}{x}") for x in lanes]
        dequant, lora_done, w_ready, w_turned, w_copied = map(
            sem, ("e_dequant", "e_lora_done", "e_w_ready", "e_w_turned", "e_w_copied"))
        h_in, lin1_done, y_done, n_done, n_turned, g_ready, lin2_done = map(
            each, ("h_in", "lin1_done", "y_done", "n_done", "n_turned", "g_ready", "lin2_done"))
        h_added, total_done, total_turned, out_done, out_kept = map(
            each, ("h_added", "total_done", "total_turned", "out_done", "out_kept"))
        block = ctx.enter_context(nc.Block())
        ITER = NCH // LANES

        @block.sync
        def _(sp):
            for dst, src in ((q_in, d.qweights), (scale, d.qscales), (la, d.la), (lb, d.lb), (bias1, d.bias1), (cols, d.cols)):
                sp.dma_start(dst[:], src).then_inc(weights_in, 16)
            with sp.Fori(0, ITER) as i:
                for x in lanes:
                    sp.wait_ge(total_done[x], i)
                    sp.dma_start(h_fm[x][:], t.y_fm[:, bass.ds((i * LANES + x) * QC, QC)]).then_inc(h_in[x], 16)
                for x in lanes:
                    sp.wait_ge(out_done[x], CT * (i + 1))
                    sp.dma_start(d.out[bass.ds((i * LANES + x) * QC, QC), :].rearrange("(k p) f -> p k f", p=P),
                                 out_tm[x][:]).then_inc(out_kept[x], 16)
            for x in lanes:
                sp.wait_ge(out_kept[x], 16 * ITER)

        @block.scalar
        def _(act):
            act.wait_ge(weights_in, 16 * 6)
            for m in range(NW):
                act.wait_ge(w_turned, m + 1)
                act.copy(w_t[:, m], ps[1][:, m % 4, 0:P]).then_inc(w_copied, 1)
            with act.Fori(0, ITER) as i:
                for m in range(QB):
                    for x in lanes:
                        act.wait_ge(n_turned[x], QB * i + m + 1)
                        act.wait_ge(lin2_done[x], QB * i + m)
                        act.activation(g_fm[x][:], ps[x][:, 1], ACT.Gelu, bias=cols[:, 1, m:m + 1],
                                       scale=cols[:, 0, m:m + 1]).then_inc(g_ready[x], 1)

        @block.vector
        def _(dve):
            dve.wait_ge(weights_in, 16 * 6)
            dve.tensor_scalar(w[:], q_in[:], 1.0 / HALF_RANGE, -1.0, ALU.mult, ALU.add).then_inc(dequant, 1)
            dve.wait_ge(dequant, 1)
            by_group = w[:].rearrange("p m (g f) -> p (m g) f", f=QGROUP)
            dve.tensor_tensor(by_group, by_group, scale[:].rearrange("p m g -> p (m g)").unsqueeze(2).broadcast_to(
                [P, NW * D // QGROUP, QGROUP]), ALU.mult).then_inc(dequant, 1)
            dve.wait_ge(dequant, 2)
            for m in range(NW):
                dve.wait_ge(lora_done, m + 1)
                dve.tensor_tensor(w[:, m], w[:, m], ps[0][:, m % 4, 0:P], ALU.add).then_inc(w_ready, 1)
            with dve.Fori(0, ITER) as i:
                for m in range(QB):
                    for x in lanes:
                        n = QB * i + m
                        dve.wait_ge(lin1_done[x], n + 1)
                        bias = bias1[:, m].unsqueeze(1).broadcast_to([P, CT, D])
                        dve.tensor_tensor(y_tm[x][:], ps[x][:, 0].rearrange("p (k f) -> p k f", k=CT), bias,
                                          ALU.add).then_inc(y_done[x], 1)
                    for x in lanes:
                        n = QB * i + m
                        dve.wait_ge(y_done[x], n + 1)
                        dve.wait_ge(n_turned[x], n)
                        layer_norm(dve, ln[x], LN_STEPS * ((QB + 1) * i + m), lambda k, x=x: y_tm[x][:, k],
                                   lambda k, x=x: n_tm[x][:, k], n_done[x])
                    for x in lanes:
                        n = QB * i + m
                        dve.wait_ge(lin2_done[x], n + 1)
                        dve.scalar_tensor_tensor(h_fm[x][:], ps[x][:, 2], cols[:, 2, m:m + 1], h_fm[x][:],
                                                 ALU.add, ALU.add).then_inc(h_added[x], 1)
                for x in lanes:
                    dve.wait_ge(h_added[x], QB * (i + 1))
                    dve.tensor_tensor(g_fm[x][:], h_fm[x][:], t.y_fm[:, bass.ds((i * LANES + x) * QC, QC)],
                                      ALU.add).then_inc(total_done[x], 1)
                for x in lanes:
                    dve.wait_ge(total_turned[x], i + 1)
                    dve.wait_ge(out_kept[x], 16 * i)
                    layer_norm(dve, ln[x], LN_STEPS * ((QB + 1) * i + QB), lambda k, x=x: ps[x][:, 3, k * P:(k + 1) * P],
                               lambda k, x=x: out_tm[x][:, k], out_done[x])

        @block.tensor
        def _(pe):
            pe.wait_ge(weights_in, 16 * 6)
            for m in range(NW):
                if m >= 4:
                    pe.wait_ge(w_ready, m - 3)
                pe.matmul(ps[0][:, m % 4, 0:P], lb[:, m], la[:, m], start=True, stop=True).then_inc(lora_done, 1)
            for m in range(NW):
                pe.wait_ge(w_ready, m + 1)
                if m >= 4:
                    pe.wait_ge(w_copied, m - 3)
                pe.transpose(ps[1][:, m % 4, 0:P], w[:, m], t.ident[:]).then_inc(w_turned, 1)
            pe.wait_ge(w_copied, NW)
            with pe.Fori(0, ITER) as i:
                for m in range(QB):
                    for x in lanes:
                        n = QB * i + m
                        if m == 0:
                            pe.wait_ge(h_in[x], 16 * (i + 1))
                        else:
                            pe.wait_ge(h_added[x], n)
                        for k in range(CT):
                            last = pe.matmul(ps[x][:, 0, k * P:(k + 1) * P], h_fm[x][:, k * P:(k + 1) * P], w_t[:, 2 * m],
                                             start=True, stop=True, skip_group_check=True)
                        last.then_inc(lin1_done[x], 1)
                    for x in lanes:
                        n = QB * i + m
                        pe.wait_ge(n_done[x], CT * (n + 1))
                        for k in range(CT):
                            last = pe.transpose(ps[x][:, 1, k * P:(k + 1) * P], n_tm[x][:, k], t.ident[:])
                        last.then_inc(n_turned[x], 1)
                    for x in lanes:
                        n = QB * i + m
                        pe.wait_ge(g_ready[x], n + 1)
                        pe.matmul(ps[x][:, 2], w_t[:, 2 * m + 1], g_fm[x][:], start=True, stop=True).then_inc(lin2_done[x], 1)
                for x in lanes:
                    pe.wait_ge(total_done[x], i + 1)
                    pe.wait_ge(out_done[x], CT * i)
                    for k in range(CT):
                        last = pe.transpose(ps[x][:, 3, k * P:(k + 1) * P], g_fm[x][:, k * P:(k + 1) * P], t.ident[:])
                    last.then_inc(total_turned[x], 1)


def build(nc, d):
    with ExitStack() as ctx:
        t = Bag()
        t.made_before = []
        t.ident = ctx.enter_context(nc.sbuf_tensor("ident", [P, P], F32))
        t.y_fm = ctx.enter_context(nc.sbuf_tensor("y_fm", [P, B * S], F32))
        with ExitStack() as attention:
            t.cos = attention.enter_context(nc.sbuf_tensor("cos", [P, S], F32))
            t.sin = attention.enter_context(nc.sbuf_tensor("sin", [P, S], F32))
            t.c_fm = attention.enter_context(nc.sbuf_tensor("c_fm", [P, B * S], F32))
            t.v_tm = attention.enter_context(nc.sbuf_tensor("v_tm", [P, B * TT, DH], F32))
            t.g_all = attention.enter_context(nc.sbuf_tensor("g_all", [P, PAIRS, D], F32))
            project_inputs(nc, t, d)
            latent_attention(nc, t, d)
        t.x2_tm = ctx.enter_context(nc.sbuf_tensor("x2_tm", [P, B * TT, D], F32))
        experts(nc, t, d)
        causal(nc, t, d)
        qlora(nc, t, d)


def lay_out(i):
    f = {n: np.ascontiguousarray(a) for n, a in i.items()}
    f32 = np.float32
    wq, wk = (f[n].reshape(PAIRS, 2, DH, DH) for n in ("L0_attn_w_up_q", "L0_attn_w_up_k"))
    wqk = np.zeros((PAIRS, P, 2, P), f32)
    wqk[:, :DH, :, :DH] = wq.transpose(0, 3, 1, 2)
    wqk[:, DH:, :, DH:] = wk.transpose(0, 3, 1, 2)
    inv = (1.0 / 10000.0 ** (np.arange(0, DH, 2, dtype=f32) / DH)).astype(f32)
    freqs = np.outer(np.arange(S, dtype=f32), inv)
    cos, sin = (np.concatenate([g(freqs), g(freqs)], -1)[:, ::2].astype(f32) for g in (np.cos, np.sin))
    sign = np.tile(np.array([-1.0, 1.0], f32), P // 2)[:, None]
    rows = np.tile(np.repeat(np.arange(DH // 2), 2), 2)
    tiled = lambda a: np.ascontiguousarray(np.broadcast_to(a, (P, CT) + a.shape))
    before = lambda n: tiled(np.tril(np.ones((n, n), f32), -1))
    gp, up = (f["L0_ffn_" + n].reshape(EP, P, D).transpose(2, 0, 1) for n in ("gate_proj", "up_proj"))
    kinds = {"q": [0, 1, 0, 1], "k": [0, 0, 1, 1]}
    is_lo = {n: np.tile(np.repeat(np.array(v, f32), AD), AR) for n, v in kinds.items()}
    four = lambda w: np.ascontiguousarray(np.broadcast_to(
        w.reshape(AG, AR, 1, AD, D), (AG, AR, 4, AD, D)).reshape(AG, P, D).transpose(2, 0, 1))
    return {
        "wq1": four(f["L1_attn_Wq"]),
        "wk1": four(f["L1_attn_Wk"]),
        "wv1": np.ascontiguousarray(f["L1_attn_Wv"].T),
        "wo1": np.ascontiguousarray(f["L1_attn_Wo"].T),
        "part_rows": np.stack([is_lo["q"], 1 - 2 * is_lo["q"], is_lo["k"], 1 - 2 * is_lo["k"]], 1),
        "causal_mask": np.ascontiguousarray(np.broadcast_to(np.triu(np.ones((P, 1, P), f32)[:, 0])[:, None], (P, 2, P))),
        "qweights": np.ascontiguousarray(f["L1_ffn_qweights"].transpose(1, 0, 2)),
        "qscales": np.ascontiguousarray(f["L1_ffn_scales"].transpose(1, 0, 2)),
        "la": np.ascontiguousarray(f["L1_ffn_lora_a"].transpose(1, 0, 2)),
        "lb": np.ascontiguousarray(f["L1_ffn_lora_b"].transpose(2, 0, 1)),
        "bias1": np.ascontiguousarray(np.broadcast_to(f["L1_ffn_biases"][0::2], (P, QB, D))),
        "cols": np.ascontiguousarray(np.stack([f["L1_ffn_ln_gamma"].T, f["L1_ffn_ln_beta"].T, f["L1_ffn_biases"][1::2].T], 1)),
        "gate_w": np.ascontiguousarray(f["L0_ffn_gate_weight"].T),
        "route_bias": tiled(f["L0_ffn_e_score_correction_bias"]),
        "before_g": before(NG),
        "before_e": before(E),
        "w_gate": np.ascontiguousarray(gp),
        "w_up": np.ascontiguousarray(up),
        "w_down": np.ascontiguousarray(f["L0_ffn_down_proj"].transpose(0, 2, 1).reshape(EP, P, D).transpose(1, 0, 2)),
        "x": f["L0_attn_x"].reshape(B * S, D),
        "ident": np.eye(P, dtype=f32),
        "wd": np.ascontiguousarray(np.concatenate([f["L0_attn_w_down_q"], f["L0_attn_w_down_kv"]], 0).T),
        "lnp": np.stack([f["L0_attn_ln_scale"], f["L0_attn_ln_bias"]], 1),
        "wv": np.ascontiguousarray(f["L0_attn_w_up_v"].reshape(H, DH, DH).transpose(1, 0, 2)),
        "wo": np.ascontiguousarray(f["L0_attn_w_out"].T.reshape(H, DH, D).transpose(1, 0, 2)),
        "wqk": wqk,
        "cos": np.ascontiguousarray(cos.T[rows]),
        "sin": np.ascontiguousarray(sin.T[rows] * sign),
    }


def kernel(**inputs):
    from concourse import bacc
    from concourse.bass_utils import run_bass_kernel_spmd

    nc = bacc.Bacc("TRN2", target_bir_lowering=False, num_devices=1)
    arrays = lay_out(inputs)
    d = Bag()
    for name, a in arrays.items():
        d.__dict__[name] = nc.dram_tensor(f"in_{name}", a.shape, mybir.dt.from_np(a.dtype), kind="ExternalInput").ap()
    d.out = nc.dram_tensor("out", (B * S, D), F32, kind="ExternalOutput").ap()
    build(nc, d)
    r = run_bass_kernel_spmd(nc, [{f"in_{n}": a for n, a in arrays.items()}], core_ids=[0])
    return r.results[0]["out"].reshape(B, S, D)
```

```python
from contextlib import ExitStack

import numpy as np

import concourse.bass as bass
from concourse import mybir

ALU = mybir.AluOpType
ACT = mybir.ActivationFunctionType
AX = mybir.AxisListType
F32 = mybir.dt.float32
F32R = mybir.dt.float32r
I32 = mybir.dt.int32

P = 128
B, S, D = 4, 1024, 128
TT = S // P
QC = 512
NQC = S // QC
CT = QC // P
H, DH = 16, 64
PAIRS = H // 2
NP = B * PAIRS
UNITS = NQC * TT
LN_EPS = 1e-5
MAXIMA_IN_SLOT = [0] * 6 + [1, 2] * 5 + [1] + [0] * 10 + [1] * 16 + [0] * 5
PROJECT_AT, TURN_AT = [[17, 18], [21, 23]], 44
SUMS_AT, SPREAD_AT, OUT_AT = (7, 29), (11, 32), (16, 37)
HI_AT = (8, 9)
LO_AT = (2 * TT, 2 * TT)


def maxima_before(slot):
    return sum(MAXIMA_IN_SLOT[:slot])


def place_of(slot):
    full = -(-maxima_before(slot) // NQC)
    if full == TT and slot > PROJECT_AT[1][1]:
        return "rope 1"
    if full == TT and slot > PROJECT_AT[0][1]:
        return "rope 0"
    return full


SWAP = [i ^ 1 for i in range(32)]
RSQRT_GUESS = 0x5F3759DF


def rsqrt_on_vector(dve, done, base, value, half, guess):
    dve.tensor_scalar(half.bitcast(I32), value.bitcast(I32), 1, None, ALU.logical_shift_right).then_inc(done, 1)
    dve.wait_ge(done, base + 1)
    dve.tensor_scalar(guess.bitcast(I32), half.bitcast(I32), -1, RSQRT_GUESS, ALU.mult, ALU.add).then_inc(done, 1)
    for k in range(3):
        dve.wait_ge(done, base + 3 * k + 2)
        dve.scalar_tensor_tensor(half, guess, -0.5, guess, ALU.mult, ALU.mult).then_inc(done, 1)
        dve.wait_ge(done, base + 3 * k + 3)
        dve.tensor_tensor(half, half, value, ALU.mult).then_inc(done, 1)
        dve.wait_ge(done, base + 3 * k + 4)
        dve.scalar_tensor_tensor(guess, half, 1.5, guess, ALU.add, ALU.mult).then_inc(done, 1)
    dve.wait_ge(done, base + 11)


RSQRT_STEPS = 11


def semaphores(nc, stage, t):
    made, before = [], t.made_before
    t.made_before = made

    def end():
        for s in made:
            nc.gpsimd.sem_clear(s)
        for s in before:
            nc.release_semaphore(s)

    def sem(name):
        made.append(nc.alloc_semaphore(name))
        return made[-1]

    stage.callback(end)
    return sem


def project_inputs(nc, t, d):
    with ExitStack() as ctx:
        sb = lambda n, s, dt=F32: ctx.enter_context(nc.sbuf_tensor(n, s, dt))
        sem = semaphores(nc, ctx, t)
        x_tm = sb("x_tm", [P, 2, TT, D])
        n_tm = sb("n_tm", [P, 2, TT, D])
        h_fm = sb("h_fm", [P, 2, S])
        stats = sb("stats", [P, TT, 6])
        mean_var = sb("mean_var", [P, TT, 2])
        var = sb("var", [P, TT])
        half = sb("half", [P, TT])
        rstd = sb("rstd", [P, TT])
        wd = sb("wd", [P, P])
        lnp = sb("lnp", [P, 2])
        wv = sb("wv", [DH, H, DH])
        wo = sb("wo", [DH, H, D])
        ps = ctx.enter_context(nc.psum_tensor("ps_a", [P, 8, QC], F32))

        weights_in, tables_in = sem("a_weights_in"), sem("a_tables_in")
        x_in = [sem(f"a_x_in{i}") for i in range(2)]
        stats_done, aggr_done, var_done, rsqrt_done = sem("a_stats"), sem("a_aggr"), sem("a_var"), sem("a_rsqrt")
        norm_done = sem("a_norm")
        x_turned, n_turned = sem("a_x_turned"), sem("a_n_turned")
        x_copied, h_ready = sem("a_x_copied"), sem("a_h_ready")
        c_done, v_done, c_copied, v_copied = sem("a_c_done"), sem("a_v_done"), sem("a_c_copied"), sem("a_v_copied")
        g_done, g_copied = sem("a_g_done"), sem("a_g_copied")
        block = ctx.enter_context(nc.Block())

        @block.sync
        def _(sp):
            for dst, src in ((t.ident[:], d.ident), (wd[:], d.wd), (lnp[:], d.lnp), (wv[:], d.wv), (wo[:], d.wo)):
                sp.dma_start(dst, src).then_inc(weights_in, 16)
            for b in range(B):
                if b >= 2:
                    sp.wait_ge(x_turned, 2 * (b - 1))
                    sp.wait_ge(norm_done, TT * (b - 1))
                sp.dma_start(x_tm[:, b % 2], d.x[b * S:(b + 1) * S, :].rearrange("(t p) f -> p t f", p=P)).then_inc(x_in[b % 2], 16)
            for dst, src in ((t.cos[:], d.cos), (t.sin[:], d.sin)):
                sp.dma_start(dst, src).then_inc(tables_in, 16)
            sp.wait_ge(tables_in, 16 * 2)

        @block.vector
        def _(dve):
            for b in range(B):
                dve.wait_ge(x_in[b % 2], 16 * (b // 2 + 1))
                for k in range(TT):
                    dve.bn_stats(stats[:, k], x_tm[:, b % 2, k]).then_inc(stats_done, 1)
                for k in range(TT):
                    dve.wait_ge(stats_done, TT * b + k + 1)
                    dve.bn_aggr(mean_var[:, k], stats[:, k]).then_inc(aggr_done, 1)
                dve.wait_ge(aggr_done, TT * (b + 1))
                dve.tensor_scalar(var[:], mean_var[:, :, 1], LN_EPS, None, ALU.add).then_inc(var_done, 1)
                dve.wait_ge(var_done, b + 1)
                rsqrt_on_vector(dve, rsqrt_done, RSQRT_STEPS * b, var[:], half[:], rstd[:])
                if b >= 2:
                    dve.wait_ge(n_turned, 2 * (b - 1))
                for k in range(TT):
                    dve.tensor_scalar(n_tm[:, b % 2, k], x_tm[:, b % 2, k], mean_var[:, k, 0:1], rstd[:, k:k + 1],
                                      ALU.subtract, ALU.mult).then_inc(norm_done, 1)
                dve.wait_ge(v_done, b + 1)
                dve.tensor_copy(t.v_tm[:, b * TT:(b + 1) * TT], ps[:, 4].rearrange("p (k c) -> p k c", k=TT)).then_inc(v_copied, 1)
                dve.wait_ge(norm_done, TT * (b + 1))
            for g in range(4):
                dve.wait_ge(g_done, g + 1)
                dve.tensor_copy(t.g_all[:, 2 * g:2 * g + 2], ps[:, 7, 0:2 * D].rearrange("p (k o) -> p k o", k=2)).then_inc(g_copied, 1)

        @block.scalar
        def _(act):
            act.wait_ge(weights_in, 16 * 5)
            for b in range(B):
                for c in range(NQC):
                    at = slice(b * S + c * QC, b * S + (c + 1) * QC)
                    act.wait_ge(x_turned, NQC * b + c + 1)
                    act.mul(t.y_fm[:, at], ps[:, c], 2.0).then_inc(x_copied, 1)
                for c in range(NQC):
                    act.wait_ge(n_turned, NQC * b + c + 1)
                    if b >= 2 and c == 0:
                        act.wait_ge(v_done, b - 1)
                    act.activation(h_fm[:, b % 2, c * QC:(c + 1) * QC], ps[:, 2 + c], ACT.Identity, bias=lnp[:, 1:2],
                                   scale=lnp[:, 0:1]).then_inc(h_ready, 1)
                for c in range(NQC):
                    at = slice(b * S + c * QC, b * S + (c + 1) * QC)
                    act.wait_ge(c_done, NQC * b + c + 1)
                    act.copy(t.c_fm[:, at], ps[:, 5 + c]).then_inc(c_copied, 1)

        @block.tensor
        def _(pe):
            pe.wait_ge(weights_in, 16 * 5)
            for b in range(B):
                pe.wait_ge(x_in[b % 2], 16 * (b // 2 + 1))
                for c in range(NQC):
                    if b >= 1:
                        pe.wait_ge(x_copied, NQC * (b - 1) + c + 1)
                    for k in range(CT):
                        last = pe.transpose(ps[:, c, k * P:(k + 1) * P], x_tm[:, b % 2, c * CT + k], t.ident[:])
                    last.then_inc(x_turned, 1)
                for c in range(NQC):
                    if b >= 1:
                        pe.wait_ge(h_ready, NQC * (b - 1) + c + 1)
                    for k in range(CT):
                        pe.wait_ge(norm_done, TT * b + c * CT + k + 1)
                        last = pe.transpose(ps[:, 2 + c, k * P:(k + 1) * P], n_tm[:, b % 2, c * CT + k], t.ident[:])
                    last.then_inc(n_turned, 1)
                for c in range(NQC):
                    pe.wait_ge(h_ready, NQC * b + c + 1)
                    if b >= 1:
                        pe.wait_ge(c_copied, NQC * (b - 1) + c + 1)
                    pe.matmul(ps[:, 5 + c], wd[:], h_fm[:, b % 2, c * QC:(c + 1) * QC], start=True, stop=True).then_inc(c_done, 1)
                if b >= 1:
                    pe.wait_ge(v_copied, b)
                for k in range(TT):
                    last = pe.matmul(ps[:, 4, k * DH:(k + 1) * DH], h_fm[:, b % 2, k * P:(k + 1) * P], wd[:, DH:P],
                                     start=True, stop=True, skip_group_check=True)
                last.then_inc(v_done, 1)
            for g in range(4):
                if g:
                    pe.wait_ge(g_copied, g)
                for k in range(2):
                    for h in range(2):
                        head = 2 * (2 * g + k) + h
                        last = pe.matmul(ps[h * DH:(h + 1) * DH, 7, k * D:(k + 1) * D], wv[:, head], wo[:, head],
                                         start=True, stop=True, skip_group_check=True)
                last.then_inc(g_done, 1)


def latent_attention(nc, t, d):
    with ExitStack() as ctx:
        sb = lambda n, s, dt=F32: ctx.enter_context(nc.sbuf_tensor(n, s, dt))
        sem = semaphores(nc, ctx, t)
        q_hi_twice = [[sb(f"q_hi_twice{p}{h}", [P, S], F32R) for h in range(2)] for p in range(2)]
        k_hi_lo = [[sb(f"k_hi_lo{p}{h}", [P, S], F32R) for h in range(2)] for p in range(2)]
        q_lo_shift = [[sb(f"q_lo_shift{p}{h}", [P, S], F32R) for h in range(2)] for p in range(2)]
        k_hi_one = [[sb(f"k_hi_one{p}{h}", [P, S], F32R) for h in range(2)] for p in range(2)]
        rot = [sb(f"rot{h}", [P, S]) for h in range(2)]
        swapped = [sb(f"swapped{h}", [P, S]) for h in range(2)]
        probs = [sb(f"probs{i}", [P, 2, QC]) for i in range(4)]
        prob_sum = [sb(f"prob_sum{i}", [P, 2, QC]) for i in range(2)]
        wqk = [sb(f"wqk{i}", [P, 2, P]) for i in range(2)]
        v_now = [sb(f"v_now{i}", [P, TT, DH]) for i in range(2)]
        g_now = [sb(f"g_now{i}", [P, D]) for i in range(2)]
        ones = sb("ones", [P, DH])
        o_raw = sb("o_raw", [P, QC])
        recip_tm = sb("recip_tm", [P, 2 * CT])
        o_norm = sb("o_norm", [P, QC])
        maxima = sb("maxima", [P, NQC, 2 * TT])
        shift_tm = sb("shift_tm", [P, 2 * TT])
        shift_fm = sb("shift_fm", [2 * TT, P], F32R)
        ps_s = ctx.enter_context(nc.psum_tensor("ps_s", [P, 2, 2, QC], F32))
        ps_p = ctx.enter_context(nc.psum_tensor("ps_p", [P, S], F32))
        ps_o = ctx.enter_context(nc.psum_tensor("ps_o", [P, QC], F32))
        ps_x = ctx.enter_context(nc.psum_tensor("ps_x", [P, QC], F32))

        const_set = sem("b_const_set")
        wqk_in, vg_in = sem("b_wqk_in"), sem("b_vg_in")
        hi_done, lo_done = sem("b_hi_done"), sem("b_lo_done")
        hi_placed = [sem(f"b_hi_placed{h}") for h in range(2)]
        rest_placed = [sem(f"b_rest_placed{h}") for h in range(2)]
        shift_in = sem("b_shift_in")
        prep_full, prep_read = ([sem(f"b_{n}{c}") for c in range(NQC)] for n in ("prep_full", "prep_read"))
        shift_turned = sem("b_shift_turned")
        sin_done, cos_done, rot_done = sem("b_sin"), sem("b_cos"), sem("b_rot")
        max_done, shift_ready = sem("b_max_done"), sem("b_shift_ready")
        qk_done, exp_done, pv_done, added = sem("b_qk_done"), sem("b_exp_done"), sem("b_pv_done"), sem("b_added")
        o_copied, sum_done, recip_done, norm_done = sem("b_o_copied"), sem("b_sum_done"), sem("b_recip_done"), sem("b_norm_done")
        spread_done = sem("b_spread_done")
        out_done, y_added = sem("b_out_done"), sem("b_y_added")
        block = ctx.enter_context(nc.Block())

        USES = 2 * TT + 2
        max_use = lambda j: j if j < TT else j + 2
        ROPE_USE = TT

        def use(m, r):
            return 2 + USES * (m + 1) + r

        def schedule(emit_step, make_loop):
            where = lambda m: ((m // PAIRS) % B, m % PAIRS)
            emit_step(-1, 1, where, False, True)
            emit_step(0, 0, where, False, True)
            with make_loop(0, (NP - 2) // 2) as i:
                for k in (1, 2):
                    def at(m_minus_n, i=i, k=k):
                        j = k + m_minus_n
                        half = i + j // 2
                        return (half // (PAIRS // 2)) % B, (half % (PAIRS // 2)) * 2 + j % 2
                    emit_step(2 * i + k, k % 2, at, True, True)
            emit_step(NP - 1, (NP - 1) % 2, where, True, False)

        def locate(n, at, m_minus_n):
            return at(n + m_minus_n) if isinstance(n, int) else at(m_minus_n)

        @block.sync
        def _(sp):
            sp.dma_start(wqk[0][:], d.wqk[0]).then_inc(wqk_in, 16)
            sp.wait_ge(wqk_in, 16)
            sp.dma_start(wqk[1][:], d.wqk[1]).then_inc(wqk_in, 16)
            sp.wait_ge(const_set, 9)

            def step(n, p, at, attend, prepare):
                if not prepare:
                    return
                nxt = 1 - p
                if not (isinstance(n, int) and n < 1):
                    sp.wait_ge(qk_done, UNITS * n)
                hi, lo = ([x[:].bitcast(F32) for x in xs] for xs in (swapped, rot))
                for h in range(2):
                    q2, k2 = q_hi_twice[nxt][h][:].bitcast(F32), k_hi_lo[nxt][h][:].bitcast(F32)
                    for dst, src in ((q2[0:DH], hi[h][0:DH]), (q2[DH:P], hi[h][0:DH]),
                                     (k2[0:DH], hi[h][DH:P]), (k2[DH:P], lo[h][DH:P])):
                        sp.dma_start(dst, src).then_inc(hi_placed[h], 16)
                for h in range(2):
                    for dst, src in ((q_lo_shift[nxt][h], lo[h][0:DH]), (k_hi_one[nxt][h], hi[h][DH:P])):
                        sp.dma_start(dst[0:DH].bitcast(F32), src).then_inc(rest_placed[h], 16)
                b1, pair1 = locate(n, at, 1)
                if not (isinstance(n, int) and n < 1):
                    sp.wait_ge(out_done, 2 * n)
                sp.dma_start(v_now[nxt][:], t.v_tm[:, bass.ds(b1 * TT, TT), :]).then_inc(vg_in, 16)
                sp.wait_ge(wqk_in, 16 * (n + 3))
                sp.dma_start(g_now[nxt][:], t.g_all[:, bass.ds(pair1, 1), :].rearrange("p a o -> p (a o)")).then_inc(vg_in, 16)
                sp.wait_ge(shift_ready, n + 2)
                for h in range(2):
                    sp.dma_start(q_lo_shift[nxt][h][DH:DH + 1, :].bitcast(F32).rearrange("o (t q) -> o t q", t=TT),
                                 shift_fm[h * TT:(h + 1) * TT, :].bitcast(F32)).then_inc(shift_in, 16)
                _, pair = locate(n, at, 3)
                sp.wait_ge(lo_done, 2 * (n + 3))
                sp.dma_start(wqk[nxt][:], d.wqk[bass.ds(pair, 1)].rearrange("a p h f -> p (a h) f")).then_inc(wqk_in, 16)

            sp.wait_ge(lo_done, 2)
            schedule(step, sp.Fori)
            sp.wait_ge(wqk_in, 16 * (NP + 2))
            sp.wait_ge(shift_in, 32 * NP)

        @block.gpsimd
        def _(pool):
            for p in range(2):
                for h in range(2):
                    pool.memset(q_lo_shift[p][h][DH:P, :].bitcast(F32), 0.0)
                    pool.memset(k_hi_one[p][h][DH:P, :].bitcast(F32), 0.0).then_inc(const_set, 1)

            def step(n, p, at, attend, prepare):
                if isinstance(n, int) and n < 0:
                    return
                for c in range(NQC):
                    for k in range(1, TT):
                        u = c * TT + k
                        pool.wait_ge(exp_done, UNITS * n + u + 1)
                        if k == 1:
                            if not (isinstance(n, int) and n == 0):
                                pool.wait_ge(sum_done, 2 * n + c - 1)
                        else:
                            pool.wait_ge(added, 7 * (2 * n + c) + k - 1)
                        first = probs[(u - 1) % 4] if k == 1 else prob_sum[c]
                        pool.tensor_tensor(prob_sum[c][:], first[:], probs[u % 4][:], ALU.add).then_inc(added, 1)

            schedule(step, pool.Fori)

        @block.scalar
        def _(act):
            def step(n, p, at, attend, prepare):
                zero = isinstance(n, int) and n == 0
                if isinstance(n, int) and n < 0:
                    for h in range(2):
                        hi(n + 2, h)
                    return
                for u in range(UNITS + (not prepare) * 2):
                    if u < UNITS:
                        act.wait_ge(qk_done, UNITS * n + u + 1)
                        if not (zero and u < 4):
                            act.wait_ge(pv_done, UNITS * n + u - 3)
                            c, k = divmod((u - 4) % UNITS, TT)
                            if u >= 4:
                                act.wait_ge(added, 7 * (2 * n + c) + max(k, 1))
                            else:
                                act.wait_ge(added, 7 * (2 * n - 2 + c) + k)
                        act.activation(probs[u % 4][:], ps_s[:, u % 2], ACT.Exp, scale=DH ** -0.5).then_inc(exp_done, 1)
                    if u == 1 and not zero:
                        copy_o(2 * n - 1)
                    if u == 9:
                        copy_o(2 * n)
                    if u == UNITS + 1:
                        copy_o(2 * n + 1)
                    if prepare and u in HI_AT:
                        hi(n + 2, HI_AT.index(u))

            def hi(m, h):
                act.wait_ge(rot_done, 2 * m + h + 1)
                act.copy(swapped[h][:].bitcast(F32R), rot[h][:]).then_inc(hi_done, 1)

            def copy_o(c):
                act.wait_ge(pv_done, TT * (c + 1))
                if not (isinstance(c, int) and c == 0):
                    act.wait_ge(norm_done, c)
                act.copy(o_raw[:], ps_o[:]).then_inc(o_copied, 1)

            for h in range(2):
                hi(0, h)
            schedule(step, act.Fori)

        @block.vector
        def _(dve):
            dve.memset(ones[:], 1.0).then_inc(const_set, 1)
            for p in range(2):
                for h in range(2):
                    dve.wait_ge(const_set, 5)
                    dve.memset(k_hi_one[p][h][DH:DH + 1, :].bitcast(F32), -1.0).then_inc(const_set, 1)

            def rope(m, base, h):
                done = 2 * m + h
                if not (isinstance(m, int) and m == 0):
                    dve.wait_ge(hi_placed[h], 64 * m)
                    dve.wait_ge(rest_placed[h], 32 * m)
                for c in range(NQC):
                    half = slice(c * QC, (c + 1) * QC)
                    dve.wait_ge(prep_full[c], base + h + 1)
                    dve.tensor_tensor(rot[h][:, half], ps_p[:, half], t.cos[:, half], ALU.mult).then_inc(cos_done, 1)
                    dve.stream_shuffle(swapped[h][:, half], ps_p[:, half], SWAP).then_inc(prep_read[c], 1)
                for c in range(NQC):
                    dve.wait_ge(prep_read[c], base + h + 1)
                dve.tensor_tensor(swapped[h][:], swapped[h][:], t.sin[:], ALU.mult).then_inc(sin_done, 1)
                dve.wait_ge(sin_done, done + 1)
                dve.wait_ge(cos_done, NQC * (done + 1))
                dve.tensor_tensor(rot[h][:], rot[h][:], swapped[h][:], ALU.add).then_inc(rot_done, 1)

            def lo(m, h):
                dve.wait_ge(hi_done, 2 * m + h + 1)
                dve.tensor_tensor(rot[h][:].bitcast(F32R), rot[h][:], swapped[h][:], ALU.subtract).then_inc(lo_done, 1)

            def invert(c):
                dve.wait_ge(sum_done, c + 1)
                if not (isinstance(c, int) and c == 0):
                    dve.wait_ge(spread_done, c)
                dve.reciprocal(recip_tm[:], ps_x[:, 0:2 * CT]).then_inc(recip_done, 1)

            def normalise(c):
                dve.wait_ge(spread_done, c + 1)
                dve.wait_ge(o_copied, c + 1)
                if not (isinstance(c, int) and c == 0):
                    dve.wait_ge(out_done, c)
                dve.tensor_tensor(o_norm[:], o_raw[:], ps_x[:], ALU.mult).then_inc(norm_done, 1)

            def add_y(c, batch, half):
                dve.wait_ge(out_done, c + 1)
                if not (isinstance(c, int) and c == 0):
                    dve.wait_ge(y_added, c)
                at = t.y_fm[:, bass.ds(batch * S + half * QC, QC)]
                dve.tensor_tensor(at, at, ps_x[:], ALU.add).then_inc(y_added, 1)

            def step(n, p, at, attend, prepare):
                past = not (isinstance(n, int) and n < 1)
                nxt = 1 - p
                now = not (isinstance(n, int) and n < 0)
                def rest(place):
                    if place == place_of(SUMS_AT[0]) and past:
                        invert(2 * n - 1)
                    if place == place_of(SPREAD_AT[0]) and past:
                        normalise(2 * n - 1)
                    if place == place_of(OUT_AT[0]) and past:
                        add_y(2 * n - 1, locate(n, at, -1)[0], 1)
                    if place == place_of(SUMS_AT[1]) and now:
                        invert(2 * n)
                    if place == place_of(SPREAD_AT[1]) and now:
                        normalise(2 * n)
                    if place == place_of(OUT_AT[1]) and now:
                        add_y(2 * n, locate(n, at, 0)[0], 0)

                for j in range(2 * TT):
                    rest(j)
                    if j == TT:
                        if prepare:
                            rope(n + 2, use(n, ROPE_USE), 0)
                        rest("rope 0")
                        if prepare:
                            rope(n + 2, use(n, ROPE_USE), 1)
                        rest("rope 1")
                    if not prepare:
                        continue
                    for h in range(2):
                        if j == LO_AT[h]:
                            lo(n + 2, h)
                    if j == 0 and now:
                        dve.wait_ge(max_done, n + 1)
                    for c in range(NQC):
                        dve.wait_ge(prep_full[c], use(n, max_use(j)) + 1)
                        dve.tensor_reduce(maxima[:, c, j:j + 1], ps_p[:, c * QC:(c + 1) * QC],
                                          AX.X, ALU.max).then_inc(prep_read[c], 1)
                if prepare:
                    for c in range(NQC):
                        dve.wait_ge(prep_read[c], use(n, USES))
                    if now:
                        dve.wait_ge(shift_turned, n + 1)
                    dve.tensor_tensor(shift_tm[:], maxima[:, 0], maxima[:, 1], ALU.max).then_inc(max_done, 1)
                    dve.wait_ge(shift_turned, n + 2)
                    if now:
                        dve.wait_ge(shift_in, 32 * (n + 1))
                    dve.tensor_copy(shift_fm[:], ps_p[0:2 * TT, 0:P]).then_inc(shift_ready, 1)
                    for h in range(2):
                        if LO_AT[h] == 2 * TT:
                            lo(n + 2, h)
                rest(2 * TT)
                if not prepare:
                    invert(2 * n + 1)
                    normalise(2 * n + 1)
                    add_y(2 * n + 1, locate(n, at, 0)[0], 1)

            for h in range(2):
                rope(0, 0, h)
            for h in range(2):
                lo(0, h)
            schedule(step, dve.Fori)

        @block.tensor
        def _(pe):
            pe.wait_ge(const_set, 9)

            def project(m, par, batch, base, h, c):
                if h == 0 and c == 0:
                    pe.wait_ge(wqk_in, 16 * (m + 1))
                if not (isinstance(base, int) and base + h == 0):
                    pe.wait_ge(prep_read[c], base + h)
                pe.matmul(ps_p[:, c * QC:(c + 1) * QC], wqk[par][:, h],
                          t.c_fm[:, bass.ds(batch * S + c * QC, QC)], start=True, stop=True).then_inc(prep_full[c], 1)

            def scores(n, p, u, heads):
                c, k = divmod(u, TT)
                if 0 in heads and not (isinstance(n, int) and n == 0 and u < 2):
                    pe.wait_ge(exp_done, UNITS * n + u - 1)
                if u == 0 and 0 in heads:
                    pe.wait_ge(shift_in, 32 * (n + 1))
                for h in heads:
                    if u == 0:
                        pe.wait_ge(rest_placed[h], 32 * (n + 1))
                    q, keys = slice(c * QC, (c + 1) * QC), slice(k * P, (k + 1) * P)
                    pe.matmul(ps_s[:, u % 2, h], k_hi_lo[p][h][:, keys], q_hi_twice[p][h][:, q], start=True, stop=False)
                    last = pe.matmul(ps_s[:, u % 2, h], k_hi_one[p][h][:, keys], q_lo_shift[p][h][:, q], start=False, stop=True)
                if 1 in heads:
                    last.then_inc(qk_done, 1)

            def weigh(n, p, u):
                c, k = divmod(u, TT)
                pe.wait_ge(exp_done, UNITS * n + u + 1)
                if k == 0:
                    if u == 0:
                        pe.wait_ge(vg_in, 32 * (n + 1))
                    if not (isinstance(n, int) and n == 0 and c == 0):
                        pe.wait_ge(o_copied, 2 * n + c)
                for h in range(2):
                    last = pe.matmul(ps_o[h * DH:(h + 1) * DH, :], v_now[p][:, k], probs[u % 4][:, h],
                                     start=(k == 0), stop=(k == TT - 1))
                last.then_inc(pv_done, 1)

            def sums(c, half):
                pe.wait_ge(added, 7 * (c + 1))
                if not (isinstance(c, int) and c == 0):
                    pe.wait_ge(y_added, c)
                for h in range(2):
                    for k in range(CT):
                        at = h * CT + k
                        last = pe.matmul(ps_x[:, at:at + 1], prob_sum[half][:, h, k * P:(k + 1) * P], ones[:, 0:1],
                                         start=True, stop=True)
                last.then_inc(sum_done, 1)

            def spread(c):
                pe.wait_ge(recip_done, c + 1)
                for h in range(2):
                    for k in range(CT):
                        at = h * CT + k
                        last = pe.matmul(ps_x[h * DH:(h + 1) * DH, k * P:(k + 1) * P],
                                         recip_tm[:, at:at + 1].broadcast_to((P, DH)), t.ident[:], start=True, stop=True)
                last.then_inc(spread_done, 1)

            def project_out(c, par):
                pe.wait_ge(norm_done, c + 1)
                pe.matmul(ps_x[:], g_now[par][:], o_norm[:], start=True, stop=True).then_inc(out_done, 1)

            def maximum(n, nxt, j, c):
                h, k = divmod(j, TT)
                if k == 0 and c == 0:
                    pe.wait_ge(hi_placed[h], 64 * (n + 2))
                if j == 0 and c == 0 and not (isinstance(n, int) and n < 0):
                    pe.wait_ge(shift_ready, n + 1)
                pe.wait_ge(prep_read[c], use(n, max_use(j)))
                pe.matmul(ps_p[:, c * QC:(c + 1) * QC], q_hi_twice[nxt][h][:, k * P:(k + 1) * P],
                          k_hi_lo[nxt][h][:, c * QC:(c + 1) * QC], start=True, stop=True).then_inc(prep_full[c], 1)

            def turn_shift(n):
                pe.wait_ge(max_done, n + 2)
                pe.transpose(ps_p[0:2 * TT, 0:P], shift_tm[:], t.ident[:]).then_inc(shift_turned, 1)

            def step(n, p, at, attend, prepare):
                nxt = 1 - p
                past = not (isinstance(n, int) and n < 1)
                now = not (isinstance(n, int) and n < 0)

                def prepare_next(slot):
                    for r in range(maxima_before(slot), maxima_before(slot + 1)):
                        maximum(n, nxt, r // NQC, r % NQC)
                    if slot == TURN_AT:
                        turn_shift(n)
                    for h in range(2):
                        for c in range(NQC):
                            if slot == PROJECT_AT[h][c]:
                                project(n + 2, p, locate(n, at, 2)[0], use(n, ROPE_USE), h, c)

                def finish(slot):
                    if slot == SUMS_AT[0] and past:
                        sums(2 * n - 1, 1)
                    if slot == SUMS_AT[1] and now:
                        sums(2 * n, 0)
                    if slot == SPREAD_AT[0] and past:
                        spread(2 * n - 1)
                    if slot == SPREAD_AT[1] and now:
                        spread(2 * n)
                    if slot == OUT_AT[0] and past:
                        project_out(2 * n - 1, 1 - p)
                    if slot == OUT_AT[1] and now:
                        project_out(2 * n, p)
                    if prepare:
                        prepare_next(slot)

                for u in range(UNITS):
                    for h in range(2):
                        if now:
                            scores(n, p, u, [h])
                        finish(3 * u + h)
                    if now and u >= 2:
                        weigh(n, p, u - 2)
                    elif past:
                        weigh(n - 1, 1 - p, UNITS - 2 + u)
                    finish(3 * u + 2)
                if not prepare:
                    weigh(n, p, UNITS - 2)
                    weigh(n, p, UNITS - 1)
                    sums(2 * n + 1, 1)
                    spread(2 * n + 1)
                    project_out(2 * n + 1, p)

            for h in range(2):
                for c in range(NQC):
                    project(0, 0, 0, 0, h, c)
            schedule(step, pe.Fori)


class Bag:
    pass


def norm_steps(tiles):
    return tiles + 7 + RSQRT_STEPS


def norm_buffers(sb, sem, name, tiles=CT):
    w = Bag()
    w.tiles = tiles
    w.stats = sb(f"{name}_stats", [P, tiles, 6])
    w.mean, w.gap, w.sq, w.var, w.half, w.rstd = (sb(f"{name}_{x}", [P, tiles]) for x in ("mean", "gap", "sq", "var", "half", "rstd"))
    w.chain = sem(f"{name}_chain")
    return w


def layer_norm(dve, w, base, src, dst, done, meanwhile=None):
    for k in range(w.tiles):
        dve.bn_stats(w.stats[:, k], src(k)).then_inc(w.chain, 1)
    even, odd, even_sq, odd_sq = (w.stats[:, :, j] for j in (1, 4, 2, 5))
    dve.wait_ge(w.chain, base + w.tiles)
    dve.tensor_tensor(w.mean[:], even, odd, ALU.add).then_inc(w.chain, 1)
    dve.tensor_tensor(w.gap[:], even, odd, ALU.subtract).then_inc(w.chain, 1)
    dve.tensor_tensor(w.sq[:], even_sq, odd_sq, ALU.add).then_inc(w.chain, 1)
    dve.wait_ge(w.chain, base + w.tiles + 3)
    dve.tensor_scalar(w.mean[:], w.mean[:], 0.5, None, ALU.mult).then_inc(w.chain, 1)
    dve.scalar_tensor_tensor(w.gap[:], w.gap[:], 0.25, w.gap[:], ALU.mult, ALU.mult).then_inc(w.chain, 1)
    dve.tensor_scalar(w.sq[:], w.sq[:], 1.0 / D, LN_EPS, ALU.mult, ALU.add).then_inc(w.chain, 1)
    dve.wait_ge(w.chain, base + w.tiles + 6)
    dve.tensor_tensor(w.var[:], w.gap[:], w.sq[:], ALU.add).then_inc(w.chain, 1)
    dve.wait_ge(w.chain, base + w.tiles + 7)
    rsqrt_on_vector(dve, w.chain, base + w.tiles + 7, w.var[:], w.half[:], w.rstd[:])
    if meanwhile:
        meanwhile()
    for k in range(w.tiles):
        dve.tensor_scalar(dst(k), src(k), w.mean[:, k:k + 1], w.rstd[:, k:k + 1],
                          ALU.subtract, ALU.mult).then_inc(done[k * len(done) // w.tiles], 1)


NCH = B * S // QC
LANES = 2
E, EI, EP = 8, 64, 4
NG, GS = 4, 2
ROUTE_STEPS = 16


def experts(nc, t, d):
    with ExitStack() as ctx:
        sb = lambda n, s, dt=F32: ctx.enter_context(nc.sbuf_tensor(n, s, dt))
        sem = semaphores(nc, ctx, t)
        lanes = range(LANES)
        LT = LANES * CT
        weights_in = sem("c_weights_in")
        gate_w = sb("gate_w", [P, E])
        bias = sb("bias", [P, LT, E])
        before_g = sb("before_g", [P, LT, NG, NG])
        before_e = sb("before_e", [P, LT, E, E])
        w_gate, w_up, w_down = (sb(n, [P, EP, P]) for n in ("w_gate", "w_up", "w_down"))
        y_now = [sb(f"y_now{x}", [P, QC]) for x in lanes]
        x1_tm = [sb(f"x1_tm{x}", [P, CT, D]) for x in lanes]
        x1_fm = [sb(f"x1_fm{x}", [P, QC]) for x in lanes]
        scores = sb("scores", [P, LT, E])
        choice = sb("choice", [P, LT, E])
        group = sb("group", [P, LT, NG])
        gt = sb("gt", [P, LT, E, E])
        eq = sb("eq", [P, LT, E, E])
        rank = sb("rank", [P, LT, E])
        rank_g = sb("rank_g", [P, LT, NG])
        weight = sb("weight", [P, LT, E])
        total = sb("total", [P, LT])
        spread = [sb(f"spread{x}", [P, CT, E, EI]) for x in lanes]
        sig = [sb(f"sig{x}", [P, QC]) for x in lanes]
        hid = [sb(f"hid{x}", [P, QC]) for x in lanes]
        z_tm = [sb(f"z_tm{x}", [P, CT, D]) for x in lanes]
        x2_now = [sb(f"x2_now{x}", [P, CT, D]) for x in lanes]
        x2_fm = [sb(f"x2_fm{x}", [P, QC]) for x in lanes]
        ln = norm_buffers(sb, sem, "c_ln", LT)
        ps = [ctx.enter_context(nc.psum_tensor(f"ps_c{x}", [P, 4, QC], F32)) for x in lanes]

        each = lambda n: [sem(f"c_{n}{x}") for x in lanes]
        y_in, y_turned, x1_done, x1_turned, x1_ready = map(each, ("y_in", "y_turned", "x1_done", "x1_turned", "x1_ready"))
        logits_done, scores_ready, spread_done = map(each, ("logits_done", "scores_ready", "spread_done"))
        route, spread_total = sem("c_route"), sem("c_spread_total")
        gate_up_done, sig_done, mul1, mul2, hid_done, down_done = map(
            each, ("gate_up_done", "sig_done", "mul1", "mul2", "hid_done", "down_done"))
        z_done, x2_done, x2_kept, x2_turned, x2_copied, x2_fm_kept = map(
            each, ("z_done", "x2_done", "x2_kept", "x2_turned", "x2_copied", "x2_fm_kept"))
        block = ctx.enter_context(nc.Block())
        ITER = NCH // LANES

        def column(i, x):
            return bass.ds((i * LANES + x) * QC, QC)

        @block.sync
        def _(sp):
            for dst, src in ((gate_w, d.gate_w), (bias, d.route_bias), (before_g, d.before_g), (before_e, d.before_e),
                             (w_gate, d.w_gate), (w_up, d.w_up), (w_down, d.w_down)):
                sp.dma_start(dst[:], src).then_inc(weights_in, 16)
            with sp.Fori(0, ITER) as i:
                for x in lanes:
                    sp.wait_ge(y_turned[x], i)
                    sp.dma_start(y_now[x][:], t.y_fm[:, column(i, x)]).then_inc(y_in[x], 16)
                for x in lanes:
                    sp.wait_ge(x2_done[x], CT * (i + 1))
                    sp.dma_start(t.x2_tm[:, bass.ds((i * LANES + x) * CT, CT), :], x2_now[x][:]).then_inc(x2_kept[x], 16)
                for x in lanes:
                    sp.wait_ge(x2_copied[x], i + 1)
                    sp.dma_start(t.y_fm[:, column(i, x)], x2_fm[x][:]).then_inc(x2_fm_kept[x], 16)
            for x in lanes:
                sp.wait_ge(x2_kept[x], 16 * ITER)
                sp.wait_ge(x2_fm_kept[x], 16 * ITER)

        @block.scalar
        def _(act):
            act.wait_ge(weights_in, 16 * 7)
            with act.Fori(0, ITER) as i:
                for x in lanes:
                    act.wait_ge(x1_turned[x], i + 1)
                    act.wait_ge(gate_up_done[x], EP * i)
                    act.copy(x1_fm[x][:], ps[x][:, 1]).then_inc(x1_ready[x], 1)
                for x in lanes:
                    act.wait_ge(logits_done[x], i + 1)
                    act.wait_ge(spread_done[x], i)
                    act.activation(scores[:, x * CT:(x + 1) * CT].rearrange("p k e -> p (k e)"), ps[x][:, 0, 0:CT * E],
                                   ACT.Sigmoid).then_inc(scores_ready[x], 1)
                for e in range(EP):
                    for x in lanes:
                        act.wait_ge(gate_up_done[x], EP * i + e + 1)
                        act.wait_ge(mul1[x], EP * i + e)
                        act.activation(sig[x][:], ps[x][:, 1], ACT.Sigmoid).then_inc(sig_done[x], 1)
                for x in lanes:
                    act.wait_ge(x2_turned[x], i + 1)
                    act.wait_ge(x2_fm_kept[x], 16 * i)
                    act.copy(x2_fm[x][:], ps[x][:, 1]).then_inc(x2_copied[x], 1)

        @block.vector
        def _(dve):
            dve.wait_ge(weights_in, 16 * 7)
            with dve.Fori(0, ITER) as i:
                for x in lanes:
                    dve.wait_ge(y_turned[x], i + 1)
                    dve.wait_ge(z_done[x], i)
                layer_norm(dve, ln, 2 * norm_steps(LT) * i, lambda k: ps[k // CT][:, 0, k % CT * P:(k % CT + 1) * P],
                           lambda k: x1_tm[k // CT][:, k % CT], x1_done)
                steps = 0

                def then(ins):
                    nonlocal steps
                    steps += 1
                    ins.then_inc(route, 1)
                    dve.wait_ge(route, ROUTE_STEPS * i + steps)

                def ranks(out, score, n, before):
                    g, q = (m[:, :, 0:n, 0:n] for m in (gt, eq))
                    b = score.unsqueeze(2).broadcast_to([P, LT, n, n])
                    a = score.unsqueeze(3).broadcast_to([P, LT, n, n])
                    then(dve.tensor_tensor(g, b, a, ALU.is_gt))
                    then(dve.tensor_tensor(q, b, a, ALU.is_equal))
                    then(dve.tensor_tensor(q, q, before[:], ALU.mult))
                    then(dve.tensor_tensor(g, g, q, ALU.add))
                    then(dve.tensor_reduce(out[:], g, AX.X, ALU.add))

                for x in lanes:
                    dve.wait_ge(scores_ready[x], i + 1)
                then(dve.tensor_tensor(choice[:], scores[:], bias[:], ALU.add))
                then(dve.tensor_tensor(group[:], choice[:, :, 0::GS], choice[:, :, 1::GS], ALU.add))
                ranks(rank_g, group[:], NG, before_g)
                kept = rank_g[:].rearrange("p k g -> p (k g)").unsqueeze(2).broadcast_to([P, LT * NG, GS])
                by_group = choice[:].rearrange("p k (g s) -> p (k g) s", g=NG)
                then(dve.scalar_tensor_tensor(by_group, kept, 2.0, by_group, ALU.is_lt, ALU.mult))
                ranks(rank, choice[:], E, before_e)
                then(dve.scalar_tensor_tensor(weight[:], rank[:], 2.0, scores[:], ALU.is_lt, ALU.mult))
                then(dve.tensor_reduce(total[:], weight[:], AX.X, ALU.add))
                then(dve.tensor_scalar(total[:], total[:], 1e-20, None, ALU.add))
                dve.reciprocal(total[:], total[:]).then_inc(spread_total, 1)
                dve.wait_ge(spread_total, i + 1)
                for x in lanes:
                    mine = slice(x * CT, (x + 1) * CT)
                    dve.tensor_tensor(spread[x][:], weight[:, mine].unsqueeze(3).broadcast_to([P, CT, E, EI]),
                                      total[:, mine].unsqueeze(2).unsqueeze(3).broadcast_to([P, CT, E, EI]),
                                      ALU.mult).then_inc(spread_done[x], 1)
                for e in range(EP):
                    for x in lanes:
                        n = EP * i + e
                        dve.wait_ge(sig_done[x], n + 1)
                        dve.wait_ge(down_done[x], n)
                        dve.tensor_tensor(hid[x][:], sig[x][:], ps[x][:, 1], ALU.mult).then_inc(mul1[x], 1)
                        dve.wait_ge(mul1[x], n + 1)
                        dve.tensor_tensor(hid[x][:], hid[x][:], ps[x][:, 2], ALU.mult).then_inc(mul2[x], 1)
                        dve.wait_ge(mul2[x], n + 1)
                        dve.tensor_tensor(hid[x][:], hid[x][:], ps[x][:, 3], ALU.mult).then_inc(hid_done[x], 1)
                for x in lanes:
                    dve.wait_ge(down_done[x], EP * (i + 1))
                    dve.tensor_tensor(z_tm[x][:].rearrange("p k f -> p (k f)"), x1_tm[x][:].rearrange("p k f -> p (k f)"),
                                      ps[x][:, 0], ALU.add).then_inc(z_done[x], 1)
                for x in lanes:
                    dve.wait_ge(z_done[x], i + 1)
                    dve.wait_ge(x2_kept[x], 16 * i)
                    dve.wait_ge(x2_turned[x], i)
                layer_norm(dve, ln, 2 * norm_steps(LT) * i + norm_steps(LT), lambda k: z_tm[k // CT][:, k % CT],
                           lambda k: x2_now[k // CT][:, k % CT], x2_done)

        @block.tensor
        def _(pe):
            pe.wait_ge(weights_in, 16 * 7)
            with pe.Fori(0, ITER) as i:
                def turn(bank, src, x):
                    for k in range(CT):
                        last = pe.transpose(ps[x][:, bank, k * P:(k + 1) * P], src(k), t.ident[:])
                    return last

                for x in lanes:
                    pe.wait_ge(y_in[x], 16 * (i + 1))
                    pe.wait_ge(z_done[x], i)
                    turn(0, lambda k: y_now[x][:, k * P:(k + 1) * P], x).then_inc(y_turned[x], 1)
                for x in lanes:
                    pe.wait_ge(x1_done[x], CT * (i + 1))
                    pe.wait_ge(x2_copied[x], i)
                    turn(1, lambda k: x1_tm[x][:, k], x).then_inc(x1_turned[x], 1)
                for x in lanes:
                    pe.wait_ge(x1_ready[x], i + 1)
                    for k in range(CT):
                        last = pe.matmul(ps[x][:, 0, k * E:(k + 1) * E], x1_fm[x][:, k * P:(k + 1) * P], gate_w[:],
                                         start=True, stop=True, skip_group_check=True)
                    last.then_inc(logits_done[x], 1)
                def gate_up(x, e):
                    pe.wait_ge(hid_done[x], EP * i + e)
                    if e == 0:
                        pe.wait_ge(scores_ready[x], i + 1)
                    pe.matmul(ps[x][:, 1], w_gate[:, e], x1_fm[x][:], start=True, stop=True)
                    pe.matmul(ps[x][:, 2], w_up[:, e], x1_fm[x][:], start=True, stop=True)
                    if e == 0:
                        pe.wait_ge(spread_done[x], i + 1)
                    two = lambda k: spread[x][:, k, 2 * e:2 * e + 2].rearrange("p e r -> p (e r)")
                    turn(3, two, x).then_inc(gate_up_done[x], 1)

                def down(x, e):
                    pe.wait_ge(hid_done[x], EP * i + e + 1)
                    for k in range(CT):
                        last = pe.matmul(ps[x][:, 0, k * P:(k + 1) * P], hid[x][:, k * P:(k + 1) * P], w_down[:, e],
                                         start=(e == 0 and k == 0), stop=(e == EP - 1), skip_group_check=True)
                    last.then_inc(down_done[x], 1)

                for x in lanes:
                    gate_up(x, 0)
                for e in range(EP):
                    for x in lanes:
                        down(x, e)
                        if e < EP - 1:
                            gate_up(x, e + 1)
                for x in lanes:
                    pe.wait_ge(x2_done[x], CT * (i + 1))
                    turn(1, lambda k: x2_now[x][:, k], x).then_inc(x2_turned[x], 1)


AH, AD = 16, 8
AG, AR = 4, 4
SLOT = P // AR
Z_EPS = 1e-6
STEPS = [(c, k) for c in range(NQC) for k in range(CT * (c + 1))]
HALVES = 2 * len(STEPS)
LAG = 2


def causal(nc, t, d):
    with ExitStack() as ctx:
        sb = lambda n, s, dt=F32: ctx.enter_context(nc.sbuf_tensor(n, s, dt))
        sem = semaphores(nc, ctx, t)
        weights_in = sem("d_weights_in")
        wq, wk = sb("wq1", [P, AG, P]), sb("wk1", [P, AG, P])
        wv, wo = sb("wv1", [P, D]), sb("wo1", [P, D])
        rows = sb("part_rows", [P, 4])
        mask = sb("causal_mask", [P, 2, P])
        shift = sb("square_shift", [P, 1])
        x_now = sb("x_now", [P, S])
        vx = sb("vx", [P, TT, AH, SLOT])
        q_rows = [[sb(f"q_rows{p}{r}", [P, S], F32R) for r in range(AR)] for p in range(2)]
        k_rows = [sb(f"k_rows{p}", [P, S], F32R) for p in range(2)]
        q_hi, k_hi = sb("q_hi", [P, QC], F32R), sb("k_hi", [P, QC], F32R)
        q_part, k_part = sb("q_part", [P, QC]), sb("k_part", [P, QC])
        a = [sb(f"a{i}", [P, 2, QC]) for i in range(2 * (LAG + 1))]
        o_rows = [sb(f"o_rows{i}", [P, QC]) for i in range(2)]
        z = [sb(f"z{i}", [P, CT, AR]) for i in range(2)]
        out_tm = sb("out_tm", [P, TT, D])
        out_fm = [sb(f"out_fm{c}", [P, QC]) for c in range(NQC)]
        z_tm = [sb(f"sum_tm{c}", [P, CT, D]) for c in range(NQC)]
        x3_tm = [sb(f"x3_tm{c}", [P, CT, D]) for c in range(NQC)]
        x3_fm = [sb(f"x3_fm{c}", [P, QC]) for c in range(NQC)]
        ln = [norm_buffers(sb, sem, f"d_ln{c}") for c in range(NQC)]
        ps_s = [ctx.enter_context(nc.psum_tensor(f"ps_d_s{i}", [P, 2, QC], F32)) for i in range(2)]
        bank = lambda n: ctx.enter_context(nc.psum_tensor(n, [P, QC], F32))
        ps_o, ps_t, ps_q, ps_k = bank("ps_d_o"), bank("ps_d_t"), bank("ps_d_q"), bank("ps_d_k")
        turn_bank, sum_bank = [ps_q, ps_o], [ps_k, ps_t]

        vx_set, vx_zero = sem("d_vx_set"), sem("d_vx_zero")
        x_in, v_done, v_copied = sem("d_x_in"), sem("d_v_done"), sem("d_v_copied")
        proj_done, split_done, rows_done = sem("d_proj_done"), sem("d_split_done"), sem("d_rows_done")
        qk_done, squared, a_ready, pv_done = sem("d_qk_done"), sem("d_squared"), sem("d_a_ready"), sem("d_pv_done")
        o_copied, o_turned, z_ready, z_recip, out_done = map(sem, ("d_o_copied", "d_o_turned", "d_z_ready", "d_z_recip", "d_out_done"))
        each = lambda n: [sem(f"d_{n}{c}") for c in range(NQC)]
        y_turned, y_ready, wo_done, sum_done, x3_done, x3_turned, x3_copied, x3_kept = map(
            each, ("y_turned", "y_ready", "wo_done", "sum_done", "x3_done", "x3_turned", "x3_copied", "x3_kept"))
        block = ctx.enter_context(nc.Block())
        PROJ = AG * NQC
        AHEAD = {(0, 2): 0, (1, 1): 1}

        def each_step():
            for g in range(AG):
                for s, (c, k) in enumerate(STEPS):
                    yield g, s, c, k, max(0, (k - CT * c) * P)

        def copy_o(act, b, g, c):
            n = NQC * g + c - 1
            steps = len(STEPS) * (n // NQC) + (CT if n % NQC == 0 else len(STEPS))
            act.wait_ge(pv_done, len(STEPS) * AG * b + steps)
            act.wait_ge(o_turned, PROJ * b + max(n - 1, 0))
            act.copy(o_rows[n % 2][:], ps_o[:]).then_inc(o_copied, 1)

        @block.sync
        def _(sp):
            for dst, src in ((wq, d.wq1), (wk, d.wk1), (wv, d.wv1), (wo, d.wo1), (rows, d.part_rows), (mask, d.causal_mask)):
                sp.dma_start(dst[:], src).then_inc(weights_in, 16)
            with sp.Fori(0, B) as b:
                sp.wait_ge(proj_done, PROJ * b)
                sp.dma_start(x_now[:], t.y_fm[:, bass.ds(b * S, S)]).then_inc(x_in, 16)
                for c in range(NQC):
                    sp.wait_ge(x3_copied[c], b + 1)
                    sp.dma_start(t.y_fm[:, bass.ds(b * S + c * QC, QC)], x3_fm[c][:]).then_inc(x3_kept[c], 16)
            for c in range(NQC):
                sp.wait_ge(x3_kept[c], 16 * B)

        @block.gpsimd
        def _(pool):
            pool.memset(vx[:], 0.0).then_inc(vx_zero, 1)
            for p in range(2):
                for r in range(AR):
                    pool.memset(q_rows[p][r][:].bitcast(F32), 0.0).then_inc(vx_set, 1)

        @block.scalar
        def _(act):
            act.wait_ge(weights_in, 16 * 6)
            act.wait_ge(vx_set, 2 * AR + 2)
            with act.Fori(0, B) as b:
                def split(g, c):
                    n = PROJ * b + NQC * g + c
                    act.wait_ge(proj_done, n + 1)
                    act.wait_ge(rows_done, n)
                    act.copy(q_hi[:], ps_q[:])
                    act.mul(q_part[:], ps_q[:], rows[:, 0:1])
                    act.copy(k_hi[:], ps_k[:])
                    act.mul(k_part[:], ps_k[:], rows[:, 2:3]).then_inc(split_done, 1)

                split(0, 0)
                split(0, 1)
                for g, s, c, k, off in each_step():
                    for r in range(2):
                        half = HALVES * g + 2 * s + r
                        act.wait_ge(qk_done, HALVES * AG * b + half + 1)
                        act.wait_ge(pv_done, len(STEPS) * AG * b + max(len(STEPS) * g + s - LAG, 0))
                        act.activation(a[half % len(a)][:, :, off:], ps_s[r][:, :, off:], ACT.Square, bias=shift[:],
                                       scale=0.25).then_inc(squared, 1)
                    if g < AG - 1 and (c, k) in AHEAD:
                        split(g + 1, AHEAD[c, k])
                    if k == LAG - 1 and (g or c):
                        copy_o(act, b, g, c)
                    if (g, c, k) == (AG - 1, NQC - 1, TT - 1):
                        copy_o(act, b, AG, 0)
                for c in range(NQC):
                    act.wait_ge(y_turned[c], b + 1)
                    act.copy(out_fm[c][:], turn_bank[c][:]).then_inc(y_ready[c], 1)
                for c in range(NQC):
                    act.wait_ge(x3_turned[c], b + 1)
                    act.wait_ge(x3_kept[c], 16 * b)
                    act.copy(x3_fm[c][:], turn_bank[c][:]).then_inc(x3_copied[c], 1)

        @block.vector
        def _(dve):
            dve.memset(shift[:], 0.5 ** 0.5).then_inc(vx_set, 1)
            dve.wait_ge(vx_zero, 1)
            dve.memset(vx[:, :, :, AD:AD + 1], 1.0).then_inc(vx_set, 1)
            dve.wait_ge(vx_set, 2 * AR + 2)
            dve.wait_ge(weights_in, 16 * 6)
            with dve.Fori(0, B) as b:
                def make_rows(g, c):
                    n = PROJ * b + NQC * g + c
                    at = slice(c * QC, (c + 1) * QC)
                    dve.wait_ge(split_done, n + 1)
                    dve.wait_ge(qk_done, HALVES * AG * b + max(HALVES * (g - 1), 0))
                    for r in range(AR):
                        q = slice(r * SLOT, (r + 1) * SLOT)
                        dve.scalar_tensor_tensor(q_rows[g % 2][r][q, at], q_hi[q, :].bitcast(F32), rows[q, 1:2], q_part[q, :],
                                                 ALU.mult, ALU.add)
                    dve.scalar_tensor_tensor(k_rows[g % 2][:, at], k_hi[:].bitcast(F32), rows[:, 3:4], k_part[:],
                                             ALU.mult, ALU.add).then_inc(rows_done, 1)

                def normalise(n):
                    g, c = divmod(n, NQC)
                    turned = ps_t[:].rearrange("p (k r f) -> p k r f", k=CT, r=AR)
                    dve.wait_ge(o_turned, PROJ * b + n + 1)
                    dve.wait_ge(out_done, PROJ * b + max(n - 1, 0))
                    dve.tensor_scalar(z[n % 2][:], turned[:, :, :, AD], Z_EPS, None, ALU.add).then_inc(z_ready, 1)
                    dve.wait_ge(z_ready, PROJ * b + n + 1)
                    dve.reciprocal(z[n % 2][:], z[n % 2][:]).then_inc(z_recip, 1)
                    dve.wait_ge(z_recip, PROJ * b + n + 1)
                    to = out_tm[:, CT * c:CT * (c + 1), AR * AD * g:AR * AD * (g + 1)]
                    dve.tensor_tensor(to.rearrange("p k (r f) -> p k r f", r=AR), turned[:, :, :, 0:AD],
                                      z[n % 2][:].unsqueeze(3).broadcast_to([P, CT, AR, AD]), ALU.mult).then_inc(out_done, 1)

                for c in range(NQC):
                    dve.wait_ge(v_done, NQC * b + c + 1)
                    bank = (ps_q, ps_k)[c]
                    dve.tensor_copy(vx[:, CT * c:CT * (c + 1), :, 0:AD].rearrange("p k h f -> p (k h) f"),
                                    bank[:].rearrange("p (k f) -> p k f", f=AD)).then_inc(v_copied, 1)
                make_rows(0, 0)
                make_rows(0, 1)
                for g, s, c, k, off in each_step():
                    for r in range(2):
                        half = HALVES * g + 2 * s + r
                        buf = a[half % len(a)]
                        diagonal = k >= CT * c
                        dve.wait_ge(squared, HALVES * AG * b + half + 1)
                        full = off + P * diagonal
                        if diagonal:
                            last = dve.scalar_tensor_tensor(buf[:, :, off:full], buf[:, :, off:full], 0.5, mask[:],
                                                            ALU.add, ALU.mult)
                        if full < QC:
                            last = dve.tensor_scalar(buf[:, :, full:], buf[:, :, full:], 0.5, None, ALU.add)
                        last.then_inc(a_ready, 1)
                    if g < AG - 1 and (c, k) in AHEAD:
                        make_rows(g + 1, AHEAD[c, k])
                    if k == LAG + 1 and (g or c):
                        normalise(NQC * g + c - 1)
                normalise(PROJ - 1)
                for c in range(NQC):
                    dve.wait_ge(wo_done[c], b + 1)
                    dve.tensor_tensor(z_tm[c][:], sum_bank[c][:].rearrange("p (k f) -> p k f", k=CT),
                                      t.x2_tm[:, bass.ds(b * TT + c * CT, CT), :], ALU.add).then_inc(sum_done[c], 1)
                for c in range(NQC):
                    dve.wait_ge(sum_done[c], b + 1)
                    dve.wait_ge(x3_turned[c], b)
                    layer_norm(dve, ln[c], norm_steps(CT) * b, lambda k, c=c: z_tm[c][:, k], lambda k, c=c: x3_tm[c][:, k], [x3_done[c]])

        @block.tensor
        def _(pe):
            pe.wait_ge(weights_in, 16 * 6)
            pe.wait_ge(vx_set, 2 * AR + 2)
            with pe.Fori(0, B) as b:
                def project(g, c):
                    n = PROJ * b + NQC * g + c
                    at = slice(c * QC, (c + 1) * QC)
                    pe.wait_ge(split_done, n)
                    pe.matmul(ps_q[:], wq[:, g], x_now[:, at], start=True, stop=True)
                    pe.matmul(ps_k[:], wk[:, g], x_now[:, at], start=True, stop=True).then_inc(proj_done, 1)

                def scores(g, s, c, k, off):
                    for r in range(2):
                        half = HALVES * g + 2 * s + r
                        pe.wait_ge(squared, HALVES * AG * b + max(half - 1, 0))
                        for h in range(2):
                            last = pe.matmul(ps_s[r][:, h, off:], k_rows[g % 2][:, k * P:(k + 1) * P],
                                             q_rows[g % 2][2 * r + h][:, c * QC + off:(c + 1) * QC], start=True, stop=True)
                        last.then_inc(qk_done, 1)

                def weigh(g, s, c, k, off):
                    pe.wait_ge(a_ready, HALVES * AG * b + HALVES * g + 2 * s + 2)
                    if k == 0:
                        pe.wait_ge(o_copied, PROJ * b + NQC * g + c)
                    for r in range(AR):
                        half = HALVES * g + 2 * s + r // 2
                        last = pe.matmul(ps_o[r * SLOT:(r + 1) * SLOT, off:], vx[:, k, AR * g + r],
                                         a[half % len(a)][:, r % 2, off:], start=(k == 0), stop=(k == CT * (c + 1) - 1))
                    last.then_inc(pv_done, 1)

                def turn_o(n):
                    pe.wait_ge(o_copied, PROJ * b + n + 1)
                    pe.wait_ge(out_done, PROJ * b + n)
                    for k in range(CT):
                        last = pe.transpose(ps_t[:, k * P:(k + 1) * P], o_rows[n % 2][:, k * P:(k + 1) * P], t.ident[:])
                    last.then_inc(o_turned, 1)

                pe.wait_ge(x_in, 16 * (b + 1))
                for c in range(NQC):
                    pe.wait_ge((x3_copied, sum_done)[c][0], b)
                    for k in range(CT):
                        tile = CT * c + k
                        last = pe.matmul((ps_q, ps_k)[c][:, k * P:(k + 1) * P], x_now[:, tile * P:(tile + 1) * P], wv[:],
                                         start=True, stop=True, skip_group_check=True)
                    last.then_inc(v_done, 1)
                pe.wait_ge(v_copied, NQC * (b + 1))
                project(0, 0)
                project(0, 1)
                before = []
                for g, s, c, k, off in each_step():
                    if s == 0:
                        pe.wait_ge(rows_done, PROJ * b + NQC * (g + 1))
                    scores(g, s, c, k, off)
                    if len(before) == LAG:
                        weigh(*before.pop(0))
                    before.append((g, s, c, k, off))
                    if g < AG - 1 and (c, k) in AHEAD:
                        project(g + 1, AHEAD[c, k])
                    if k == LAG and (g or c):
                        turn_o(NQC * g + c - 1)
                for late in before:
                    weigh(*late)
                turn_o(PROJ - 1)
                for c in range(NQC):
                    pe.wait_ge(out_done, PROJ * (b + 1))
                    for k in range(CT):
                        last = pe.transpose(turn_bank[c][:, k * P:(k + 1) * P], out_tm[:, CT * c + k], t.ident[:])
                    last.then_inc(y_turned[c], 1)
                for c in range(NQC):
                    pe.wait_ge(y_ready[c], b + 1)
                    for k in range(CT):
                        last = pe.matmul(sum_bank[c][:, k * P:(k + 1) * P], out_fm[c][:, k * P:(k + 1) * P], wo[:],
                                         start=True, stop=True, skip_group_check=True)
                    last.then_inc(wo_done[c], 1)
                for c in range(NQC):
                    pe.wait_ge(x3_done[c], CT * (b + 1))
                    for k in range(CT):
                        last = pe.transpose(turn_bank[c][:, k * P:(k + 1) * P], x3_tm[c][:, k], t.ident[:])
                    last.then_inc(x3_turned[c], 1)


QB = 3
LORA = 32
QGROUP = 16
HALF_RANGE = 7.5


def qlora(nc, t, d):
    with ExitStack() as ctx:
        sb = lambda n, s, dt=F32: ctx.enter_context(nc.sbuf_tensor(n, s, dt))
        sem = semaphores(nc, ctx, t)
        lanes = range(LANES)
        NW = 2 * QB
        weights_in = sem("e_weights_in")
        q_in = sb("q_in", [P, NW, D], I32)
        scale = sb("scale", [P, NW, D // QGROUP])
        la, lb = sb("la", [LORA, NW, D]), sb("lb", [LORA, NW, D])
        w = sb("w", [P, NW, D])
        w_t = sb("w_t", [P, NW, D])
        bias1 = sb("bias1", [P, QB, D])
        cols = sb("cols", [P, 3, QB])
        h_fm = [sb(f"h_fm{x}", [P, S]) for x in lanes]
        y_tm = [sb(f"y_tm{x}", [P, TT, D]) for x in lanes]
        n_tm = [sb(f"n_tm{x}", [P, TT, D]) for x in lanes]
        g_fm = [sb(f"g_fm{x}", [P, S]) for x in lanes]
        out_tm = [sb(f"out_tm{x}", [P, TT, D]) for x in lanes]
        ln = [norm_buffers(sb, sem, f"e_ln{x}", TT) for x in lanes]
        ps = [ctx.enter_context(nc.psum_tensor(f"ps_e{x}", [P, 4, QC], F32)) for x in lanes]
        linear = [ps[x][:, 0:2].rearrange("p b q -> p (b q)") for x in lanes]
        turned = [ps[x][:, 2:4].rearrange("p b q -> p (b q)") for x in lanes]
        each = lambda n: [sem(f"e_{n}{x}") for x in lanes]
        dequant, lora_done, w_ready, w_turned, w_copied = map(
            sem, ("e_dequant", "e_lora_done", "e_w_ready", "e_w_turned", "e_w_copied"))
        h_in, lin1_done, y_done, n_done, n_turned, g_ready, lin2_done = map(
            each, ("h_in", "lin1_done", "y_done", "n_done", "n_turned", "g_ready", "lin2_done"))
        h_added, total_done, total_turned, out_done, out_kept = map(
            each, ("h_added", "total_done", "total_turned", "out_done", "out_kept"))
        block = ctx.enter_context(nc.Block())
        ITER = B // LANES

        @block.sync
        def _(sp):
            for dst, src in ((q_in, d.qweights), (scale, d.qscales), (la, d.la), (lb, d.lb), (bias1, d.bias1), (cols, d.cols)):
                sp.dma_start(dst[:], src).then_inc(weights_in, 16)
            with sp.Fori(0, ITER) as i:
                for x in lanes:
                    sp.wait_ge(total_done[x], i)
                    sp.dma_start(h_fm[x][:], t.y_fm[:, bass.ds((i * LANES + x) * S, S)]).then_inc(h_in[x], 16)
                for x in lanes:
                    sp.wait_ge(out_done[x], TT * (i + 1))
                    sp.dma_start(d.out[bass.ds((i * LANES + x) * S, S), :].rearrange("(k p) f -> p k f", p=P),
                                 out_tm[x][:]).then_inc(out_kept[x], 16)
            for x in lanes:
                sp.wait_ge(out_kept[x], 16 * ITER)

        @block.scalar
        def _(act):
            act.wait_ge(weights_in, 16 * 6)
            for m in range(NW):
                act.wait_ge(w_turned, m + 1)
                act.copy(w_t[:, m], ps[1][:, m % 4, 0:P]).then_inc(w_copied, 1)
            with act.Fori(0, ITER) as i:
                for m in range(QB):
                    for x in lanes:
                        act.wait_ge(n_turned[x], QB * i + m + 1)
                        act.wait_ge(lin2_done[x], QB * i + m)
                        act.activation(g_fm[x][:], turned[x], ACT.Gelu, bias=cols[:, 1, m:m + 1],
                                       scale=cols[:, 0, m:m + 1]).then_inc(g_ready[x], 1)

        @block.vector
        def _(dve):
            dve.wait_ge(weights_in, 16 * 6)
            dve.tensor_scalar(w[:], q_in[:], 1.0 / HALF_RANGE, -1.0, ALU.mult, ALU.add).then_inc(dequant, 1)
            dve.wait_ge(dequant, 1)
            by_group = w[:].rearrange("p m (g f) -> p (m g) f", f=QGROUP)
            dve.tensor_tensor(by_group, by_group, scale[:].rearrange("p m g -> p (m g)").unsqueeze(2).broadcast_to(
                [P, NW * D // QGROUP, QGROUP]), ALU.mult).then_inc(dequant, 1)
            dve.wait_ge(dequant, 2)
            for m in range(NW):
                dve.wait_ge(lora_done, m + 1)
                dve.tensor_tensor(w[:, m], w[:, m], ps[0][:, m % 4, 0:P], ALU.add).then_inc(w_ready, 1)
            with dve.Fori(0, ITER) as i:
                def add_h(x, m):
                    dve.wait_ge(lin2_done[x], QB * i + m + 1)
                    dve.scalar_tensor_tensor(h_fm[x][:], linear[x], cols[:, 2, m:m + 1], h_fm[x][:],
                                             ALU.add, ALU.add).then_inc(h_added[x], 1)

                for m in range(QB):
                    for x in lanes:
                        n = QB * i + m
                        last_h = None if x == 0 and m == 0 else lambda x=x, m=m: add_h(1 - x, m - (x == 0))
                        dve.wait_ge(lin1_done[x], n + 1)
                        bias = bias1[:, m].unsqueeze(1).broadcast_to([P, TT, D])
                        dve.tensor_tensor(y_tm[x][:], linear[x].rearrange("p (k f) -> p k f", k=TT), bias,
                                          ALU.add).then_inc(y_done[x], 1)
                        dve.wait_ge(y_done[x], n + 1)
                        dve.wait_ge(n_turned[x], n)
                        layer_norm(dve, ln[x], norm_steps(TT) * ((QB + 1) * i + m), lambda k, x=x: y_tm[x][:, k],
                                   lambda k, x=x: n_tm[x][:, k], [n_done[x]], last_h)
                for x in lanes:
                    if x == LANES - 1:
                        add_h(x, QB - 1)
                    dve.wait_ge(h_added[x], QB * (i + 1))
                    dve.tensor_tensor(g_fm[x][:], h_fm[x][:], t.y_fm[:, bass.ds((i * LANES + x) * S, S)],
                                      ALU.add).then_inc(total_done[x], 1)
                for x in lanes:
                    dve.wait_ge(total_turned[x], i + 1)
                    dve.wait_ge(out_kept[x], 16 * i)
                    layer_norm(dve, ln[x], norm_steps(TT) * ((QB + 1) * i + QB),
                               lambda k, x=x: turned[x][:, k * P:(k + 1) * P],
                               lambda k, x=x: out_tm[x][:, k], [out_done[x]])

        @block.tensor
        def _(pe):
            pe.wait_ge(weights_in, 16 * 6)
            for m in range(NW):
                if m >= 4:
                    pe.wait_ge(w_ready, m - 3)
                pe.matmul(ps[0][:, m % 4, 0:P], lb[:, m], la[:, m], start=True, stop=True).then_inc(lora_done, 1)
            for m in range(NW):
                pe.wait_ge(w_ready, m + 1)
                if m >= 4:
                    pe.wait_ge(w_copied, m - 3)
                pe.transpose(ps[1][:, m % 4, 0:P], w[:, m], t.ident[:]).then_inc(w_turned, 1)
            pe.wait_ge(w_copied, NW)
            with pe.Fori(0, ITER) as i:
                def linear1(x, m):
                    if m == 0:
                        pe.wait_ge(h_in[x], 16 * (i + 1))
                    else:
                        pe.wait_ge(h_added[x], QB * i + m)
                    for k in range(TT):
                        last = pe.matmul(linear[x][:, k * P:(k + 1) * P], h_fm[x][:, k * P:(k + 1) * P], w_t[:, 2 * m],
                                         start=True, stop=True, skip_group_check=True)
                    last.then_inc(lin1_done[x], 1)

                def turn(x, m):
                    pe.wait_ge(n_done[x], TT * (QB * i + m + 1))
                    if m == 0:
                        pe.wait_ge(out_done[x], TT * i)
                    for k in range(TT):
                        last = pe.transpose(turned[x][:, k * P:(k + 1) * P], n_tm[x][:, k], t.ident[:])
                    last.then_inc(n_turned[x], 1)

                def linear2(x, m):
                    pe.wait_ge(g_ready[x], QB * i + m + 1)
                    for c in range(NQC):
                        half = slice(c * QC, (c + 1) * QC)
                        last = pe.matmul(linear[x][:, half], w_t[:, 2 * m + 1], g_fm[x][:, half], start=True, stop=True)
                    last.then_inc(lin2_done[x], 1)

                for x in lanes:
                    linear1(x, 0)
                for m in range(QB):
                    for x in lanes:
                        turn(x, m)
                        linear2(x, m)
                        if m < QB - 1:
                            linear1(x, m + 1)
                for x in lanes:
                    pe.wait_ge(total_done[x], i + 1)
                    for k in range(TT):
                        last = pe.transpose(turned[x][:, k * P:(k + 1) * P], g_fm[x][:, k * P:(k + 1) * P], t.ident[:])
                    last.then_inc(total_turned[x], 1)


def build(nc, d):
    with ExitStack() as ctx:
        t = Bag()
        t.made_before = []
        t.ident = ctx.enter_context(nc.sbuf_tensor("ident", [P, P], F32))
        t.y_fm = ctx.enter_context(nc.sbuf_tensor("y_fm", [P, B * S], F32))
        with ExitStack() as attention:
            t.cos = attention.enter_context(nc.sbuf_tensor("cos", [P, S], F32))
            t.sin = attention.enter_context(nc.sbuf_tensor("sin", [P, S], F32))
            t.c_fm = attention.enter_context(nc.sbuf_tensor("c_fm", [P, B * S], F32))
            t.v_tm = attention.enter_context(nc.sbuf_tensor("v_tm", [P, B * TT, DH], F32))
            t.g_all = attention.enter_context(nc.sbuf_tensor("g_all", [P, PAIRS, D], F32))
            project_inputs(nc, t, d)
            latent_attention(nc, t, d)
        t.x2_tm = ctx.enter_context(nc.sbuf_tensor("x2_tm", [P, B * TT, D], F32))
        experts(nc, t, d)
        causal(nc, t, d)
        qlora(nc, t, d)


def lay_out(i):
    f = {n: np.ascontiguousarray(a) for n, a in i.items()}
    f32 = np.float32
    wq, wk = (f[n].reshape(PAIRS, 2, DH, DH) for n in ("L0_attn_w_up_q", "L0_attn_w_up_k"))
    wqk = np.zeros((PAIRS, P, 2, P), f32)
    wqk[:, :DH, :, :DH] = wq.transpose(0, 3, 1, 2)
    wqk[:, DH:, :, DH:] = wk.transpose(0, 3, 1, 2)
    inv = (1.0 / 10000.0 ** (np.arange(0, DH, 2, dtype=f32) / DH)).astype(f32)
    freqs = np.outer(np.arange(S, dtype=f32), inv)
    cos, sin = (np.concatenate([g(freqs), g(freqs)], -1)[:, ::2].astype(f32) for g in (np.cos, np.sin))
    sign = np.tile(np.array([-1.0, 1.0], f32), P // 2)[:, None]
    rows = np.tile(np.repeat(np.arange(DH // 2), 2), 2)
    tiled = lambda a: np.ascontiguousarray(np.broadcast_to(a, (P, LANES * CT) + a.shape))
    before = lambda n: tiled(np.tril(np.ones((n, n), f32), -1))
    gp, up = (f["L0_ffn_" + n].reshape(EP, P, D).transpose(2, 0, 1) for n in ("gate_proj", "up_proj"))
    kinds = {"q": [0, 1, 0, 1], "k": [0, 0, 1, 1]}
    is_lo = {n: np.tile(np.repeat(np.array(v, f32), AD), AR) for n, v in kinds.items()}
    four = lambda w: np.ascontiguousarray(np.broadcast_to(
        w.reshape(AG, AR, 1, AD, D), (AG, AR, 4, AD, D)).reshape(AG, P, D).transpose(2, 0, 1))
    return {
        "wq1": four(f["L1_attn_Wq"]),
        "wk1": four(f["L1_attn_Wk"]),
        "wv1": np.ascontiguousarray(f["L1_attn_Wv"].T),
        "wo1": np.ascontiguousarray(f["L1_attn_Wo"].T),
        "part_rows": np.stack([is_lo["q"], 1 - 2 * is_lo["q"], is_lo["k"], 1 - 2 * is_lo["k"]], 1),
        "causal_mask": np.ascontiguousarray(np.broadcast_to(np.triu(np.ones((P, 1, P), f32)[:, 0])[:, None], (P, 2, P))),
        "qweights": np.ascontiguousarray(f["L1_ffn_qweights"].transpose(1, 0, 2)),
        "qscales": np.ascontiguousarray(f["L1_ffn_scales"].transpose(1, 0, 2)),
        "la": np.ascontiguousarray(f["L1_ffn_lora_a"].transpose(1, 0, 2)),
        "lb": np.ascontiguousarray(f["L1_ffn_lora_b"].transpose(2, 0, 1)),
        "bias1": np.ascontiguousarray(np.broadcast_to(f["L1_ffn_biases"][0::2], (P, QB, D))),
        "cols": np.ascontiguousarray(np.stack([f["L1_ffn_ln_gamma"].T, f["L1_ffn_ln_beta"].T, f["L1_ffn_biases"][1::2].T], 1)),
        "gate_w": np.ascontiguousarray(f["L0_ffn_gate_weight"].T),
        "route_bias": tiled(f["L0_ffn_e_score_correction_bias"]),
        "before_g": before(NG),
        "before_e": before(E),
        "w_gate": np.ascontiguousarray(gp),
        "w_up": np.ascontiguousarray(up),
        "w_down": np.ascontiguousarray(f["L0_ffn_down_proj"].transpose(0, 2, 1).reshape(EP, P, D).transpose(1, 0, 2)),
        "x": f["L0_attn_x"].reshape(B * S, D),
        "ident": np.eye(P, dtype=f32),
        "wd": np.ascontiguousarray(np.concatenate([f["L0_attn_w_down_q"], f["L0_attn_w_down_kv"]], 0).T),
        "lnp": np.stack([f["L0_attn_ln_scale"], f["L0_attn_ln_bias"]], 1),
        "wv": np.ascontiguousarray(f["L0_attn_w_up_v"].reshape(H, DH, DH).transpose(1, 0, 2)),
        "wo": np.ascontiguousarray(f["L0_attn_w_out"].T.reshape(H, DH, D).transpose(1, 0, 2)),
        "wqk": wqk,
        "cos": np.ascontiguousarray(cos.T[rows]),
        "sin": np.ascontiguousarray(sin.T[rows] * sign),
    }


def kernel(**inputs):
    from concourse import bacc
    from concourse.bass_utils import run_bass_kernel_spmd

    nc = bacc.Bacc("TRN2", target_bir_lowering=False, num_devices=1)
    arrays = lay_out(inputs)
    d = Bag()
    for name, a in arrays.items():
        d.__dict__[name] = nc.dram_tensor(f"in_{name}", a.shape, mybir.dt.from_np(a.dtype), kind="ExternalInput").ap()
    d.out = nc.dram_tensor("out", (B * S, D), F32, kind="ExternalOutput").ap()
    build(nc, d)
    r = run_bass_kernel_spmd(nc, [{f"in_{n}": a for n, a in arrays.items()}], core_ids=[0])
    return r.results[0]["out"].reshape(B, S, D)
```

```python
from contextlib import ExitStack

import numpy as np

import concourse.bass as bass
from concourse import mybir

ALU = mybir.AluOpType
ACT = mybir.ActivationFunctionType
AX = mybir.AxisListType
F32 = mybir.dt.float32
F32R = mybir.dt.float32r
I32 = mybir.dt.int32

P = 128
B, S, D = 4, 1024, 128
TT = S // P
QC = 512
NQC = S // QC
CT = QC // P
H, DH = 16, 64
PAIRS = H // 2
NP = B * PAIRS
UNITS = NQC * TT
LN_EPS = 1e-5
MAXIMA_IN_SLOT = [0] * 6 + [1, 2] * 5 + [1] + [0] * 10 + [1] * 8 + [1, 1, 2] * 2 + [0] * 7
PROJECT_AT, TURN_AT = [[17, 18], [21, 23]], 42
SUMS_AT, SPREAD_AT, OUT_AT = (7, 29), (11, 32), (16, 37)
HI_AT = (8, 9)
KEEP_AT = (0, 2)
LO_AT = (2 * TT, 2 * TT)


def maxima_before(slot):
    return sum(MAXIMA_IN_SLOT[:slot])


def place_of(slot):
    full = -(-maxima_before(slot) // NQC)
    if full == TT and slot > PROJECT_AT[1][1]:
        return "rope 1"
    if full == TT and slot > PROJECT_AT[0][1]:
        return "rope 0"
    return full


SWAP = [i ^ 1 for i in range(32)]
RSQRT_GUESS = 0x5F3759DF


def rsqrt_on_vector(dve, done, base, value, half, guess):
    dve.tensor_scalar(half.bitcast(I32), value.bitcast(I32), 1, None, ALU.logical_shift_right).then_inc(done, 1)
    dve.wait_ge(done, base + 1)
    dve.tensor_scalar(guess.bitcast(I32), half.bitcast(I32), -1, RSQRT_GUESS, ALU.mult, ALU.add).then_inc(done, 1)
    for k in range(3):
        dve.wait_ge(done, base + 3 * k + 2)
        dve.scalar_tensor_tensor(half, guess, -0.5, guess, ALU.mult, ALU.mult).then_inc(done, 1)
        dve.wait_ge(done, base + 3 * k + 3)
        dve.tensor_tensor(half, half, value, ALU.mult).then_inc(done, 1)
        dve.wait_ge(done, base + 3 * k + 4)
        dve.scalar_tensor_tensor(guess, half, 1.5, guess, ALU.add, ALU.mult).then_inc(done, 1)
    dve.wait_ge(done, base + 11)


RSQRT_STEPS = 11


def semaphores(nc, stage, t, started=False):
    t.to_start = []
    made, before = [], t.made_before
    t.made_before = made

    def end():
        for s in made:
            nc.gpsimd.sem_clear(s)
        for s in before:
            nc.release_semaphore(s)

    def sem(name, started=started):
        made.append(nc.alloc_semaphore(name))
        if started:
            t.to_start.append(made[-1])
        return made[-1]

    stage.callback(end)
    return sem


START = 1


def start(nc, scrap, to_start):
    with nc.Block() as block:
        @block.vector
        def _(dve):
            for j in range(0, len(to_start), 2):
                dve.memset(scrap[:, j:j + 1], 0.0).then_inc(to_start[j], START)

        @block.gpsimd
        def _(pool):
            for j in range(1, len(to_start), 2):
                pool.memset(scrap[:, j:j + 1], 0.0).then_inc(to_start[j], START)


def project_inputs(nc, t, d):
    with ExitStack() as ctx:
        sb = lambda n, s, dt=F32: ctx.enter_context(nc.sbuf_tensor(n, s, dt))
        sem = semaphores(nc, ctx, t)
        x_tm = sb("x_tm", [P, 2, TT, D])
        n_tm = sb("n_tm", [P, 2, TT, D])
        h_fm = sb("h_fm", [P, 2, S])
        stats = sb("stats", [P, TT, 6])
        mean_var = sb("mean_var", [P, TT, 2])
        var = sb("var", [P, TT])
        half = sb("half", [P, TT])
        rstd = sb("rstd", [P, TT])
        wd = sb("wd", [P, P])
        lnp = sb("lnp", [P, 2])
        wv = sb("wv", [DH, H, DH])
        wo = sb("wo", [DH, H, D])
        ps = ctx.enter_context(nc.psum_tensor("ps_a", [P, 8, QC], F32))

        weights_in, tables_in = sem("a_weights_in"), sem("a_tables_in")
        x_in = [sem(f"a_x_in{i}") for i in range(2)]
        stats_done, aggr_done, var_done, rsqrt_done = sem("a_stats"), sem("a_aggr"), sem("a_var"), sem("a_rsqrt")
        norm_done = sem("a_norm")
        x_turned, n_turned = sem("a_x_turned"), sem("a_n_turned")
        x_copied, h_ready = sem("a_x_copied"), sem("a_h_ready")
        c_done, v_done, c_copied, v_copied = sem("a_c_done"), sem("a_v_done"), sem("a_c_copied"), sem("a_v_copied")
        g_done, g_copied = sem("a_g_done"), sem("a_g_copied")
        block = ctx.enter_context(nc.Block())

        @block.sync
        def _(sp):
            for dst, src in ((t.ident[:], d.ident), (wd[:], d.wd), (lnp[:], d.lnp), (wv[:], d.wv), (wo[:], d.wo)):
                sp.dma_start(dst, src).then_inc(weights_in, 16)
            for b in range(B):
                if b >= 2:
                    sp.wait_ge(x_turned, 2 * (b - 1))
                    sp.wait_ge(norm_done, TT * (b - 1))
                sp.dma_start(x_tm[:, b % 2], d.x[b * S:(b + 1) * S, :].rearrange("(t p) f -> p t f", p=P)).then_inc(x_in[b % 2], 16)
            for dst, src in ((t.cos[:], d.cos), (t.sin[:], d.sin)):
                sp.dma_start(dst, src).then_inc(tables_in, 16)
            sp.wait_ge(tables_in, 16 * 2)

        @block.vector
        def _(dve):
            def copy_out(b):
                dve.wait_ge(v_done, b + 1)
                dve.tensor_copy(t.v_tm[:, b * TT:(b + 1) * TT], ps[:, 4].rearrange("p (k c) -> p k c", k=TT)).then_inc(v_copied, 1)
                dve.wait_ge(g_done, b + 1)
                dve.tensor_copy(t.g_all[:, 2 * b:2 * b + 2], ps[:, 7, 0:2 * D].rearrange("p (k o) -> p k o", k=2)).then_inc(g_copied, 1)

            for b in range(B):
                dve.wait_ge(x_in[b % 2], 16 * (b // 2 + 1))
                for k in range(TT):
                    dve.bn_stats(stats[:, k], x_tm[:, b % 2, k]).then_inc(stats_done, 1)
                for k in range(TT):
                    dve.wait_ge(stats_done, TT * b + k + 1)
                    dve.bn_aggr(mean_var[:, k], stats[:, k]).then_inc(aggr_done, 1)
                dve.wait_ge(aggr_done, TT * (b + 1))
                dve.tensor_scalar(var[:], mean_var[:, :, 1], LN_EPS, None, ALU.add).then_inc(var_done, 1)
                dve.wait_ge(var_done, b + 1)
                rsqrt_on_vector(dve, rsqrt_done, RSQRT_STEPS * b, var[:], half[:], rstd[:])
                if b >= 2:
                    dve.wait_ge(n_turned, 2 * (b - 1))
                for k in range(TT):
                    dve.tensor_scalar(n_tm[:, b % 2, k], x_tm[:, b % 2, k], mean_var[:, k, 0:1], rstd[:, k:k + 1],
                                      ALU.subtract, ALU.mult).then_inc(norm_done, 1)
                dve.wait_ge(norm_done, TT * (b + 1))
                if b:
                    copy_out(b - 1)
            copy_out(B - 1)

        @block.scalar
        def _(act):
            act.wait_ge(weights_in, 16 * 5)
            for b in range(B):
                for c in range(NQC):
                    at = slice(b * S + c * QC, b * S + (c + 1) * QC)
                    act.wait_ge(x_turned, NQC * b + c + 1)
                    act.mul(t.y_fm[:, at], ps[:, c], 2.0).then_inc(x_copied, 1)
                for c in range(NQC):
                    act.wait_ge(n_turned, NQC * b + c + 1)
                    if b >= 2 and c == 0:
                        act.wait_ge(v_done, b - 1)
                    act.activation(h_fm[:, b % 2, c * QC:(c + 1) * QC], ps[:, 2 + c], ACT.Identity, bias=lnp[:, 1:2],
                                   scale=lnp[:, 0:1]).then_inc(h_ready, 1)
                for c in range(NQC):
                    at = slice(b * S + c * QC, b * S + (c + 1) * QC)
                    act.wait_ge(c_done, NQC * b + c + 1)
                    act.copy(t.c_fm[:, at], ps[:, 5 + c]).then_inc(c_copied, 1)

        @block.tensor
        def _(pe):
            pe.wait_ge(weights_in, 16 * 5)
            for b in range(B):
                pe.wait_ge(x_in[b % 2], 16 * (b // 2 + 1))
                for c in range(NQC):
                    if b >= 1:
                        pe.wait_ge(x_copied, NQC * (b - 1) + c + 1)
                    for k in range(CT):
                        last = pe.transpose(ps[:, c, k * P:(k + 1) * P], x_tm[:, b % 2, c * CT + k], t.ident[:])
                    last.then_inc(x_turned, 1)
                for c in range(NQC):
                    if b >= 1:
                        pe.wait_ge(h_ready, NQC * (b - 1) + c + 1)
                    for k in range(CT):
                        pe.wait_ge(norm_done, TT * b + c * CT + k + 1)
                        last = pe.transpose(ps[:, 2 + c, k * P:(k + 1) * P], n_tm[:, b % 2, c * CT + k], t.ident[:])
                    last.then_inc(n_turned, 1)
                for c in range(NQC):
                    pe.wait_ge(h_ready, NQC * b + c + 1)
                    if b >= 1:
                        pe.wait_ge(c_copied, NQC * (b - 1) + c + 1)
                    pe.matmul(ps[:, 5 + c], wd[:], h_fm[:, b % 2, c * QC:(c + 1) * QC], start=True, stop=True).then_inc(c_done, 1)
                if b >= 1:
                    pe.wait_ge(v_copied, b)
                for k in range(TT):
                    last = pe.matmul(ps[:, 4, k * DH:(k + 1) * DH], h_fm[:, b % 2, k * P:(k + 1) * P], wd[:, DH:P],
                                     start=True, stop=True, skip_group_check=True)
                last.then_inc(v_done, 1)
                if b >= 1:
                    pe.wait_ge(g_copied, b)
                for k in range(2):
                    for h in range(2):
                        head = 2 * (2 * b + k) + h
                        last = pe.matmul(ps[h * DH:(h + 1) * DH, 7, k * D:(k + 1) * D], wv[:, head], wo[:, head],
                                         start=True, stop=True, skip_group_check=True)
                last.then_inc(g_done, 1)


def latent_attention(nc, t, d):
    with ExitStack() as ctx:
        sb = lambda n, s, dt=F32: ctx.enter_context(nc.sbuf_tensor(n, s, dt))
        sem = semaphores(nc, ctx, t)
        q_hi_twice = [[sb(f"q_hi_twice{p}{h}", [P, S], F32R) for h in range(2)] for p in range(2)]
        k_hi_lo = [[sb(f"k_hi_lo{p}{h}", [P, S], F32R) for h in range(2)] for p in range(2)]
        q_lo_shift = [[sb(f"q_lo_shift{p}{h}", [P, S], F32R) for h in range(2)] for p in range(2)]
        k_hi_minus = [[sb(f"k_hi_minus{p}{h}", [P, S], F32R) for h in range(2)] for p in range(2)]
        rot = [sb(f"rot{h}", [P, S]) for h in range(2)]
        swapped = [sb(f"swapped{h}", [P, S]) for h in range(2)]
        probs = [sb(f"probs{i}", [P, 2, QC]) for i in range(4)]
        prob_sum = [sb(f"prob_sum{i}", [P, 2, QC]) for i in range(2)]
        wqk = [sb(f"wqk{i}", [P, 2, P]) for i in range(2)]
        v_now = [sb(f"v_now{i}", [P, TT, DH]) for i in range(2)]
        g_now = [sb(f"g_now{i}", [P, D]) for i in range(2)]
        ones = sb("ones", [P, DH])
        o_raw = sb("o_raw", [P, QC])
        recip_tm = sb("recip_tm", [P, 2 * CT])
        o_norm = sb("o_norm", [P, QC])
        maxima = sb("maxima", [P, NQC, 2 * TT])
        shift_tm = sb("shift_tm", [P, 2 * TT])
        shift_fm = sb("shift_fm", [2 * TT, P], F32R)
        ps_s = ctx.enter_context(nc.psum_tensor("ps_s", [P, 2, 2, QC], F32))
        ps_p = ctx.enter_context(nc.psum_tensor("ps_p", [P, S], F32))
        ps_o = ctx.enter_context(nc.psum_tensor("ps_o", [P, QC], F32))
        ps_x = ctx.enter_context(nc.psum_tensor("ps_x", [P, QC], F32))

        const_set, cleared = sem("b_const_set"), sem("b_cleared")
        wqk_in, vg_in = sem("b_wqk_in"), sem("b_vg_in")
        hi_done, lo_done = sem("b_hi_done"), sem("b_lo_done")
        hi_placed = [sem(f"b_hi_placed{h}") for h in range(2)]
        rest_placed = [sem(f"b_rest_placed{h}") for h in range(2)]
        kept_placed = [sem(f"b_kept_placed{h}") for h in range(2)]
        shift_in = sem("b_shift_in")
        prep_full, prep_read = ([sem(f"b_{n}{c}") for c in range(NQC)] for n in ("prep_full", "prep_read"))
        shift_turned = sem("b_shift_turned")
        sin_done, cos_done, rot_done = sem("b_sin"), sem("b_cos"), sem("b_rot")
        max_done, shift_ready = sem("b_max_done"), sem("b_shift_ready")
        qk_done, exp_done, pv_done, added = sem("b_qk_done"), sem("b_exp_done"), sem("b_pv_done"), sem("b_added")
        o_copied, sum_done, recip_done, norm_done = sem("b_o_copied"), sem("b_sum_done"), sem("b_recip_done"), sem("b_norm_done")
        spread_done = sem("b_spread_done")
        out_done, y_added = sem("b_out_done"), sem("b_y_added")
        block = ctx.enter_context(nc.Block())

        USES = 2 * TT + 2
        max_use = lambda j: j if j < TT else j + 2
        ROPE_USE = TT

        def use(m, r):
            return 2 + USES * (m + 1) + r

        def schedule(emit_step, make_loop):
            where = lambda m: ((m // PAIRS) % B, m % PAIRS)
            emit_step(-1, 1, where, False, True)
            emit_step(0, 0, where, False, True)
            with make_loop(0, (NP - 2) // 2) as i:
                for k in (1, 2):
                    def at(m_minus_n, i=i, k=k):
                        j = k + m_minus_n
                        half = i + j // 2
                        return (half // (PAIRS // 2)) % B, (half % (PAIRS // 2)) * 2 + j % 2
                    emit_step(2 * i + k, k % 2, at, True, True)
            emit_step(NP - 1, (NP - 1) % 2, where, True, False)

        def locate(n, at, m_minus_n):
            return at(n + m_minus_n) if isinstance(n, int) else at(m_minus_n)

        @block.sync
        def _(sp):
            sp.dma_start(wqk[0][:], d.wqk[0]).then_inc(wqk_in, 16)
            sp.wait_ge(wqk_in, 16)
            sp.dma_start(wqk[1][:], d.wqk[1]).then_inc(wqk_in, 16)
            sp.wait_ge(const_set, 9)

            def step(n, p, at, attend, prepare):
                if not prepare:
                    return
                nxt = 1 - p
                if not (isinstance(n, int) and n < 1):
                    sp.wait_ge(qk_done, UNITS * n)
                hi, lo = ([x[:].bitcast(F32) for x in xs] for xs in (swapped, rot))
                for h in range(2):
                    q2, k2 = q_hi_twice[nxt][h][:].bitcast(F32), k_hi_lo[nxt][h][:].bitcast(F32)
                    for dst, src in ((q2[DH:P], hi[h][0:DH]), (k2[0:DH], hi[h][DH:P])):
                        sp.dma_start(dst, src).then_inc(hi_placed[h], 16)
                for h in range(2):
                    for dst, src in ((q_lo_shift[nxt][h], lo[h][0:DH]), (k_hi_minus[nxt][h], hi[h][DH:P])):
                        sp.dma_start(dst[0:DH].bitcast(F32), src).then_inc(rest_placed[h], 16)
                b1, pair1 = locate(n, at, 1)
                if not (isinstance(n, int) and n < 1):
                    sp.wait_ge(out_done, 2 * n)
                sp.dma_start(v_now[nxt][:], t.v_tm[:, bass.ds(b1 * TT, TT), :]).then_inc(vg_in, 16)
                sp.wait_ge(wqk_in, 16 * (n + 3))
                sp.dma_start(g_now[nxt][:], t.g_all[:, bass.ds(pair1, 1), :].rearrange("p a o -> p (a o)")).then_inc(vg_in, 16)
                sp.wait_ge(shift_ready, n + 2)
                for h in range(2):
                    sp.dma_start(q_lo_shift[nxt][h][DH:DH + 1, :].bitcast(F32).rearrange("o (t q) -> o t q", t=TT),
                                 shift_fm[h * TT:(h + 1) * TT, :].bitcast(F32)).then_inc(shift_in, 16)
                _, pair = locate(n, at, 3)
                sp.wait_ge(lo_done, 2 * (n + 3))
                sp.dma_start(wqk[nxt][:], d.wqk[bass.ds(pair, 1)].rearrange("a p h f -> p (a h) f")).then_inc(wqk_in, 16)

            sp.wait_ge(lo_done, 2)
            schedule(step, sp.Fori)
            sp.wait_ge(wqk_in, 16 * (NP + 2))
            sp.wait_ge(shift_in, 32 * NP)

        @block.gpsimd
        def _(pool):
            for p in range(2):
                for h in range(2):
                    pool.memset(q_lo_shift[p][h][DH:P, :].bitcast(F32), 0.0).then_inc(const_set, 1)

            def step(n, p, at, attend, prepare):
                if isinstance(n, int) and n < 0:
                    return
                for c in range(NQC):
                    for k in range(1, TT):
                        u = c * TT + k
                        pool.wait_ge(exp_done, UNITS * n + u + 1)
                        if k == 1:
                            if not (isinstance(n, int) and n == 0):
                                pool.wait_ge(sum_done, 2 * n + c - 1)
                        else:
                            pool.wait_ge(added, 7 * (2 * n + c) + k - 1)
                        first = probs[(u - 1) % 4] if k == 1 else prob_sum[c]
                        pool.tensor_tensor(prob_sum[c][:], first[:], probs[u % 4][:], ALU.add).then_inc(added, 1)

            schedule(step, pool.Fori)

        @block.scalar
        def _(act):
            def step(n, p, at, attend, prepare):
                zero = isinstance(n, int) and n == 0
                if isinstance(n, int) and n < 0:
                    for h in range(2):
                        keep(n + 1, h, 1 - p)
                    for h in range(2):
                        hi(n + 2, h)
                    return
                for u in range(UNITS + (not prepare) * 2):
                    for h in range(2):
                        if prepare and u == KEEP_AT[h]:
                            keep(n + 1, h, 1 - p)
                    if u < UNITS:
                        act.wait_ge(qk_done, UNITS * n + u + 1)
                        if not (zero and u < 4):
                            act.wait_ge(pv_done, UNITS * n + u - 3)
                            c, k = divmod((u - 4) % UNITS, TT)
                            if u >= 4:
                                act.wait_ge(added, 7 * (2 * n + c) + max(k, 1))
                            else:
                                act.wait_ge(added, 7 * (2 * n - 2 + c) + k)
                        act.activation(probs[u % 4][:], ps_s[:, u % 2], ACT.Exp, scale=DH ** -0.5).then_inc(exp_done, 1)
                    if u == 1 and not zero:
                        copy_o(2 * n - 1)
                    if u == 9:
                        copy_o(2 * n)
                    if u == UNITS + 1:
                        copy_o(2 * n + 1)
                    if prepare and u in HI_AT:
                        hi(n + 2, HI_AT.index(u))

            def hi(m, h):
                act.wait_ge(rot_done, 2 * m + h + 1)
                act.copy(swapped[h][:].bitcast(F32R), rot[h][:]).then_inc(hi_done, 1)

            def keep(m, h, par):
                act.wait_ge(lo_done, 2 * m + h + 1)
                act.copy(q_hi_twice[par][h][0:DH], swapped[h][0:DH].bitcast(F32R))
                act.copy(k_hi_lo[par][h][DH:P], rot[h][DH:P].bitcast(F32R)).then_inc(kept_placed[h], 1)

            def copy_o(c):
                act.wait_ge(pv_done, TT * (c + 1))
                if not (isinstance(c, int) and c == 0):
                    act.wait_ge(norm_done, c)
                act.copy(o_raw[:], ps_o[:]).then_inc(o_copied, 1)

            for h in range(2):
                hi(0, h)
            schedule(step, act.Fori)

        @block.vector
        def _(dve):
            dve.memset(ones[:], 1.0).then_inc(const_set, 1)
            for p in range(2):
                for h in range(2):
                    dve.memset(k_hi_minus[p][h][DH:P, :].bitcast(F32), 0.0).then_inc(cleared, 1)
            for p in range(2):
                for h in range(2):
                    dve.wait_ge(cleared, 2 * p + h + 1)
                    dve.memset(k_hi_minus[p][h][DH:DH + 1, :].bitcast(F32), -1.0).then_inc(const_set, 1)

            def rope(m, base, h):
                done = 2 * m + h
                if not (isinstance(m, int) and m == 0):
                    dve.wait_ge(hi_placed[h], 32 * m)
                    dve.wait_ge(kept_placed[h], m)
                    dve.wait_ge(rest_placed[h], 32 * m)
                for c in range(NQC):
                    half = slice(c * QC, (c + 1) * QC)
                    dve.wait_ge(prep_full[c], base + h + 1)
                    dve.tensor_tensor(rot[h][:, half], ps_p[:, half], t.cos[:, half], ALU.mult).then_inc(cos_done, 1)
                    dve.stream_shuffle(swapped[h][:, half], ps_p[:, half], SWAP).then_inc(prep_read[c], 1)
                for c in range(NQC):
                    dve.wait_ge(prep_read[c], base + h + 1)
                dve.tensor_tensor(swapped[h][:], swapped[h][:], t.sin[:], ALU.mult).then_inc(sin_done, 1)
                dve.wait_ge(sin_done, done + 1)
                dve.wait_ge(cos_done, NQC * (done + 1))
                dve.tensor_tensor(rot[h][:], rot[h][:], swapped[h][:], ALU.add).then_inc(rot_done, 1)

            def lo(m, h):
                dve.wait_ge(hi_done, 2 * m + h + 1)
                dve.tensor_tensor(rot[h][:].bitcast(F32R), rot[h][:], swapped[h][:], ALU.subtract).then_inc(lo_done, 1)

            def invert(c):
                dve.wait_ge(sum_done, c + 1)
                if not (isinstance(c, int) and c == 0):
                    dve.wait_ge(spread_done, c)
                dve.reciprocal(recip_tm[:], ps_x[:, 0:2 * CT]).then_inc(recip_done, 1)

            def normalise(c):
                dve.wait_ge(spread_done, c + 1)
                dve.wait_ge(o_copied, c + 1)
                if not (isinstance(c, int) and c == 0):
                    dve.wait_ge(out_done, c)
                dve.tensor_tensor(o_norm[:], o_raw[:], ps_x[:], ALU.mult).then_inc(norm_done, 1)

            def add_y(c, batch, half):
                dve.wait_ge(out_done, c + 1)
                if not (isinstance(c, int) and c == 0):
                    dve.wait_ge(y_added, c)
                at = t.y_fm[:, bass.ds(batch * S + half * QC, QC)]
                dve.tensor_tensor(at, at, ps_x[:], ALU.add).then_inc(y_added, 1)

            def step(n, p, at, attend, prepare):
                past = not (isinstance(n, int) and n < 1)
                nxt = 1 - p
                now = not (isinstance(n, int) and n < 0)
                def rest(place):
                    if place == place_of(SUMS_AT[0]) and past:
                        invert(2 * n - 1)
                    if place == place_of(SPREAD_AT[0]) and past:
                        normalise(2 * n - 1)
                    if place == place_of(OUT_AT[0]) and past:
                        add_y(2 * n - 1, locate(n, at, -1)[0], 1)
                    if place == place_of(SUMS_AT[1]) and now:
                        invert(2 * n)
                    if place == place_of(SPREAD_AT[1]) and now:
                        normalise(2 * n)
                    if place == place_of(OUT_AT[1]) and now:
                        add_y(2 * n, locate(n, at, 0)[0], 0)

                for j in range(2 * TT):
                    rest(j)
                    if j == TT:
                        if prepare:
                            rope(n + 2, use(n, ROPE_USE), 0)
                        rest("rope 0")
                        if prepare:
                            rope(n + 2, use(n, ROPE_USE), 1)
                        rest("rope 1")
                    if not prepare:
                        continue
                    for h in range(2):
                        if j == LO_AT[h]:
                            lo(n + 2, h)
                    if j == 0 and now:
                        dve.wait_ge(max_done, n + 1)
                    for c in range(NQC):
                        dve.wait_ge(prep_full[c], use(n, max_use(j)) + 1)
                        dve.tensor_reduce(maxima[:, c, j:j + 1], ps_p[:, c * QC:(c + 1) * QC],
                                          AX.X, ALU.max).then_inc(prep_read[c], 1)
                if prepare:
                    for c in range(NQC):
                        dve.wait_ge(prep_read[c], use(n, USES))
                    if now:
                        dve.wait_ge(shift_turned, n + 1)
                    dve.tensor_tensor(shift_tm[:], maxima[:, 0], maxima[:, 1], ALU.max).then_inc(max_done, 1)
                    dve.wait_ge(shift_turned, n + 2)
                    if now:
                        dve.wait_ge(shift_in, 32 * (n + 1))
                    dve.tensor_copy(shift_fm[:], ps_p[0:2 * TT, 0:P]).then_inc(shift_ready, 1)
                    for h in range(2):
                        if LO_AT[h] == 2 * TT:
                            lo(n + 2, h)
                rest(2 * TT)
                if not prepare:
                    invert(2 * n + 1)
                    normalise(2 * n + 1)
                    add_y(2 * n + 1, locate(n, at, 0)[0], 1)

            for h in range(2):
                rope(0, 0, h)
            for h in range(2):
                lo(0, h)
            schedule(step, dve.Fori)

        @block.tensor
        def _(pe):

            def project(m, par, batch, base, h, c):
                if h == 0 and c == 0:
                    pe.wait_ge(wqk_in, 16 * (m + 1))
                if not (isinstance(base, int) and base + h == 0):
                    pe.wait_ge(prep_read[c], base + h)
                pe.matmul(ps_p[:, c * QC:(c + 1) * QC], wqk[par][:, h],
                          t.c_fm[:, bass.ds(batch * S + c * QC, QC)], start=True, stop=True).then_inc(prep_full[c], 1)

            def scores(n, p, u, heads):
                c, k = divmod(u, TT)
                if 0 in heads and not (isinstance(n, int) and n == 0 and u < 2):
                    pe.wait_ge(exp_done, UNITS * n + u - 1)
                if u == 0 and 0 in heads:
                    pe.wait_ge(shift_in, 32 * (n + 1))
                for h in heads:
                    if u == 0:
                        pe.wait_ge(rest_placed[h], 32 * (n + 1))
                    q, keys = slice(c * QC, (c + 1) * QC), slice(k * P, (k + 1) * P)
                    pe.matmul(ps_s[:, u % 2, h], k_hi_lo[p][h][:, keys], q_hi_twice[p][h][:, q], start=True, stop=False)
                    last = pe.matmul(ps_s[:, u % 2, h], k_hi_minus[p][h][:, keys], q_lo_shift[p][h][:, q], start=False, stop=True)
                if 1 in heads:
                    last.then_inc(qk_done, 1)

            def weigh(n, p, u):
                c, k = divmod(u, TT)
                pe.wait_ge(exp_done, UNITS * n + u + 1)
                if k == 0:
                    if u == 0:
                        pe.wait_ge(vg_in, 32 * (n + 1))
                    if not (isinstance(n, int) and n == 0 and c == 0):
                        pe.wait_ge(o_copied, 2 * n + c)
                for h in range(2):
                    last = pe.matmul(ps_o[h * DH:(h + 1) * DH, :], v_now[p][:, k], probs[u % 4][:, h],
                                     start=(k == 0), stop=(k == TT - 1))
                last.then_inc(pv_done, 1)

            def sums(c, half):
                pe.wait_ge(added, 7 * (c + 1))
                if not (isinstance(c, int) and c == 0):
                    pe.wait_ge(y_added, c)
                for h in range(2):
                    for k in range(CT):
                        at = h * CT + k
                        last = pe.matmul(ps_x[:, at:at + 1], prob_sum[half][:, h, k * P:(k + 1) * P], ones[:, 0:1],
                                         start=True, stop=True)
                last.then_inc(sum_done, 1)

            def spread(c):
                pe.wait_ge(recip_done, c + 1)
                for h in range(2):
                    for k in range(CT):
                        at = h * CT + k
                        last = pe.matmul(ps_x[h * DH:(h + 1) * DH, k * P:(k + 1) * P],
                                         recip_tm[:, at:at + 1].broadcast_to((P, DH)), t.ident[:], start=True, stop=True)
                last.then_inc(spread_done, 1)

            def project_out(c, par):
                pe.wait_ge(norm_done, c + 1)
                pe.matmul(ps_x[:], g_now[par][:], o_norm[:], start=True, stop=True).then_inc(out_done, 1)

            def maximum(n, nxt, j, c):
                h, k = divmod(j, TT)
                if k == 0 and c == 0:
                    pe.wait_ge(hi_placed[h], 32 * (n + 2))
                    pe.wait_ge(kept_placed[h], n + 2)
                if j == 0 and c == 0 and not (isinstance(n, int) and n < 0):
                    pe.wait_ge(shift_ready, n + 1)
                pe.wait_ge(prep_read[c], use(n, max_use(j)))
                pe.matmul(ps_p[:, c * QC:(c + 1) * QC], q_hi_twice[nxt][h][:, k * P:(k + 1) * P],
                          k_hi_lo[nxt][h][:, c * QC:(c + 1) * QC], start=True, stop=True).then_inc(prep_full[c], 1)

            def turn_shift(n):
                pe.wait_ge(max_done, n + 2)
                pe.transpose(ps_p[0:2 * TT, 0:P], shift_tm[:], t.ident[:]).then_inc(shift_turned, 1)

            def step(n, p, at, attend, prepare):
                nxt = 1 - p
                past = not (isinstance(n, int) and n < 1)
                now = not (isinstance(n, int) and n < 0)

                def prepare_next(slot):
                    for r in range(maxima_before(slot), maxima_before(slot + 1)):
                        maximum(n, nxt, r // NQC, r % NQC)
                    if slot == TURN_AT:
                        turn_shift(n)
                    for h in range(2):
                        for c in range(NQC):
                            if slot == PROJECT_AT[h][c]:
                                project(n + 2, p, locate(n, at, 2)[0], use(n, ROPE_USE), h, c)

                def finish(slot):
                    if slot == SUMS_AT[0] and past:
                        sums(2 * n - 1, 1)
                    if slot == SUMS_AT[1] and now:
                        sums(2 * n, 0)
                    if slot == SPREAD_AT[0] and past:
                        spread(2 * n - 1)
                    if slot == SPREAD_AT[1] and now:
                        spread(2 * n)
                    if slot == OUT_AT[0] and past:
                        project_out(2 * n - 1, 1 - p)
                    if slot == OUT_AT[1] and now:
                        project_out(2 * n, p)
                    if prepare:
                        prepare_next(slot)

                for u in range(UNITS):
                    for h in range(2):
                        if now:
                            scores(n, p, u, [h])
                        finish(3 * u + h)
                    if now and u >= 2:
                        weigh(n, p, u - 2)
                    elif past:
                        weigh(n - 1, 1 - p, UNITS - 2 + u)
                    finish(3 * u + 2)
                if not prepare:
                    weigh(n, p, UNITS - 2)
                    weigh(n, p, UNITS - 1)
                    sums(2 * n + 1, 1)
                    spread(2 * n + 1)
                    project_out(2 * n + 1, p)

            for h in range(2):
                for c in range(NQC):
                    project(0, 0, 0, 0, h, c)
            pe.wait_ge(const_set, 9)
            schedule(step, pe.Fori)


class Bag:
    pass


def norm_steps(tiles):
    return tiles + 7 + RSQRT_STEPS


def norm_buffers(sb, sem, name, tiles=CT):
    w = Bag()
    w.tiles = tiles
    w.stats = sb(f"{name}_stats", [P, tiles, 6])
    w.mean, w.gap, w.sq, w.var, w.half, w.rstd = (sb(f"{name}_{x}", [P, tiles]) for x in ("mean", "gap", "sq", "var", "half", "rstd"))
    w.chain = sem(f"{name}_chain", False)
    return w


def layer_norm(dve, w, base, src, dst, done, meanwhile=None):
    for k in range(w.tiles):
        dve.bn_stats(w.stats[:, k], src(k)).then_inc(w.chain, 1)
    even, odd, even_sq, odd_sq = (w.stats[:, :, j] for j in (1, 4, 2, 5))
    dve.wait_ge(w.chain, base + w.tiles)
    dve.tensor_tensor(w.mean[:], even, odd, ALU.add).then_inc(w.chain, 1)
    dve.tensor_tensor(w.gap[:], even, odd, ALU.subtract).then_inc(w.chain, 1)
    dve.tensor_tensor(w.sq[:], even_sq, odd_sq, ALU.add).then_inc(w.chain, 1)
    dve.wait_ge(w.chain, base + w.tiles + 3)
    dve.tensor_scalar(w.mean[:], w.mean[:], 0.5, None, ALU.mult).then_inc(w.chain, 1)
    dve.scalar_tensor_tensor(w.gap[:], w.gap[:], 0.25, w.gap[:], ALU.mult, ALU.mult).then_inc(w.chain, 1)
    dve.tensor_scalar(w.sq[:], w.sq[:], 1.0 / D, LN_EPS, ALU.mult, ALU.add).then_inc(w.chain, 1)
    dve.wait_ge(w.chain, base + w.tiles + 6)
    dve.tensor_tensor(w.var[:], w.gap[:], w.sq[:], ALU.add).then_inc(w.chain, 1)
    dve.wait_ge(w.chain, base + w.tiles + 7)
    rsqrt_on_vector(dve, w.chain, base + w.tiles + 7, w.var[:], w.half[:], w.rstd[:])
    if meanwhile:
        meanwhile()
    for k in range(w.tiles):
        dve.tensor_scalar(dst(k), src(k), w.mean[:, k:k + 1], w.rstd[:, k:k + 1],
                          ALU.subtract, ALU.mult).then_inc(done[k * len(done) // w.tiles], 1)


NCH = B * S // QC
LANES = 2
E, EI, EP = 8, 64, 4
NG, GS = 4, 2
ROUTE_STEPS = 16


def experts(nc, t, d):
    with ExitStack() as ctx:
        sb = lambda n, s, dt=F32: ctx.enter_context(nc.sbuf_tensor(n, s, dt))
        sem = semaphores(nc, ctx, t, True)
        lanes = range(LANES)
        LT = LANES * CT
        weights_in = sem("c_weights_in")
        gate_w = sb("gate_w", [P, E])
        warm = sb("c_warm", [P, 1])
        bias = sb("bias", [P, LT, E])
        before_g = sb("before_g", [P, LT, NG, NG])
        before_e = sb("before_e", [P, LT, E, E])
        w_gate, w_up, w_down = (sb(n, [P, EP, P]) for n in ("w_gate", "w_up", "w_down"))
        y_now = [sb(f"y_now{x}", [P, QC]) for x in lanes]
        x1_tm = [sb(f"x1_tm{x}", [P, CT, D]) for x in lanes]
        x1_fm = [sb(f"x1_fm{x}", [P, QC]) for x in lanes]
        scores = sb("scores", [P, LT, E])
        choice = sb("choice", [P, LT, E])
        group = sb("group", [P, LT, NG])
        gt = sb("gt", [P, LT, E, E])
        eq = sb("eq", [P, LT, E, E])
        rank = sb("rank", [P, LT, E])
        rank_g = sb("rank_g", [P, LT, NG])
        weight = sb("weight", [P, LT, E])
        total = sb("total", [P, LT])
        spread = [sb(f"spread{x}", [P, CT, E, EI]) for x in lanes]
        sig = [sb(f"sig{x}", [P, QC]) for x in lanes]
        hid = [sb(f"hid{x}", [P, QC]) for x in lanes]
        z_tm = [sb(f"z_tm{x}", [P, CT, D]) for x in lanes]
        x2_now = [sb(f"x2_now{x}", [P, CT, D]) for x in lanes]
        x2_fm = [sb(f"x2_fm{x}", [P, QC]) for x in lanes]
        ln = norm_buffers(sb, sem, "c_ln", LT)
        ps = [ctx.enter_context(nc.psum_tensor(f"ps_c{x}", [P, 4, QC], F32)) for x in lanes]

        each = lambda n: [sem(f"c_{n}{x}") for x in lanes]
        y_in, y_turned, x1_done, x1_turned, x1_ready = map(each, ("y_in", "y_turned", "x1_done", "x1_turned", "x1_ready"))
        logits_done, scores_ready, spread_done = map(each, ("logits_done", "scores_ready", "spread_done"))
        route, spread_total = sem("c_route"), sem("c_spread_total")
        gate_up_done, sig_done, mul1, mul2, hid_done, down_done = map(
            each, ("gate_up_done", "sig_done", "mul1", "mul2", "hid_done", "down_done"))
        z_done, x2_done, x2_kept, x2_turned, x2_copied, x2_fm_kept = map(
            each, ("z_done", "x2_done", "x2_kept", "x2_turned", "x2_copied", "x2_fm_kept"))
        start(nc, sb("c_scrap", [P, len(t.to_start)]), t.to_start)
        block = ctx.enter_context(nc.Block())
        ITER = NCH // LANES

        def column(i, x):
            return bass.ds((i * LANES + x) * QC, QC)

        @block.sync
        def _(sp):
            for dst, src in ((gate_w, d.gate_w), (bias, d.route_bias), (before_g, d.before_g), (before_e, d.before_e),
                             (w_gate, d.w_gate), (w_up, d.w_up), (w_down, d.w_down)):
                sp.dma_start(dst[:], src).then_inc(weights_in, 16)

            def load(i):
                for x in lanes:
                    sp.dma_start(y_now[x][:], t.y_fm[:, column(i, x)]).then_inc(y_in[x], 16)

            def store(i):
                for x in lanes:
                    sp.wait_ge(x2_done[x], CT * (i + 1) + START)
                    sp.dma_start(t.x2_tm[:, bass.ds((i * LANES + x) * CT, CT), :], x2_now[x][:]).then_inc(x2_kept[x], 16)
                for x in lanes:
                    sp.wait_ge(x2_copied[x], i + 1 + START)
                    sp.dma_start(t.y_fm[:, column(i, x)], x2_fm[x][:]).then_inc(x2_fm_kept[x], 16)

            load(0)
            with sp.Fori(0, ITER - 1) as i:
                for x in lanes:
                    sp.wait_ge(y_turned[x], i + 1 + START)
                load(i + 1)
                store(i)
            store(ITER - 1)
            for x in lanes:
                sp.wait_ge(x2_kept[x], 16 * ITER + START)
                sp.wait_ge(x2_fm_kept[x], 16 * ITER + START)

        @block.scalar
        def _(act):
            act.wait_ge(weights_in, 16 * 7 + START)
            with act.Fori(0, ITER) as i:
                act.activation(warm[:], gate_w[:, 0:1], ACT.Sigmoid)
                for x in lanes:
                    act.wait_ge(x1_turned[x], i + 1 + START)
                    act.wait_ge(gate_up_done[x], EP * i + START)
                    act.copy(x1_fm[x][:], ps[x][:, 1]).then_inc(x1_ready[x], 1)
                for x in lanes:
                    act.wait_ge(logits_done[x], i + 1 + START)
                    act.wait_ge(spread_done[x], i + START)
                    act.activation(scores[:, x * CT:(x + 1) * CT].rearrange("p k e -> p (k e)"), ps[x][:, 0, 0:CT * E],
                                   ACT.Sigmoid).then_inc(scores_ready[x], 1)
                for e in range(EP):
                    for x in lanes:
                        act.wait_ge(gate_up_done[x], EP * i + e + 1 + START)
                        act.wait_ge(mul1[x], EP * i + e + START)
                        act.activation(sig[x][:], ps[x][:, 1], ACT.Sigmoid).then_inc(sig_done[x], 1)
                for x in lanes:
                    act.wait_ge(x2_turned[x], i + 1 + START)
                    act.wait_ge(x2_fm_kept[x], 16 * i + START)
                    act.copy(x2_fm[x][:], ps[x][:, 1]).then_inc(x2_copied[x], 1)

        @block.vector
        def _(dve):
            dve.wait_ge(weights_in, 16 * 7 + START)
            with dve.Fori(0, ITER) as i:
                for x in lanes:
                    dve.wait_ge(y_turned[x], i + 1 + START)
                    dve.wait_ge(z_done[x], i + START)
                layer_norm(dve, ln, 2 * norm_steps(LT) * i, lambda k: ps[k // CT][:, 0, k % CT * P:(k % CT + 1) * P],
                           lambda k: x1_tm[k // CT][:, k % CT], x1_done)
                steps = 0

                def then(ins):
                    nonlocal steps
                    steps += 1
                    ins.then_inc(route, 1)
                    dve.wait_ge(route, ROUTE_STEPS * i + steps + START)

                def ranks(out, score, n, before):
                    g, q = (m[:, :, 0:n, 0:n] for m in (gt, eq))
                    b = score.unsqueeze(2).broadcast_to([P, LT, n, n])
                    a = score.unsqueeze(3).broadcast_to([P, LT, n, n])
                    then(dve.tensor_tensor(g, b, a, ALU.is_gt))
                    then(dve.tensor_tensor(q, b, a, ALU.is_equal))
                    then(dve.tensor_tensor(q, q, before[:], ALU.mult))
                    then(dve.tensor_tensor(g, g, q, ALU.add))
                    then(dve.tensor_reduce(out[:], g, AX.X, ALU.add))

                for x in lanes:
                    dve.wait_ge(scores_ready[x], i + 1 + START)
                then(dve.tensor_tensor(choice[:], scores[:], bias[:], ALU.add))
                then(dve.tensor_tensor(group[:], choice[:, :, 0::GS], choice[:, :, 1::GS], ALU.add))
                ranks(rank_g, group[:], NG, before_g)
                kept = rank_g[:].rearrange("p k g -> p (k g)").unsqueeze(2).broadcast_to([P, LT * NG, GS])
                by_group = choice[:].rearrange("p k (g s) -> p (k g) s", g=NG)
                then(dve.scalar_tensor_tensor(by_group, kept, 2.0, by_group, ALU.is_lt, ALU.mult))
                ranks(rank, choice[:], E, before_e)
                then(dve.scalar_tensor_tensor(weight[:], rank[:], 2.0, scores[:], ALU.is_lt, ALU.mult))
                then(dve.tensor_reduce(total[:], weight[:], AX.X, ALU.add))
                then(dve.tensor_scalar(total[:], total[:], 1e-20, None, ALU.add))
                dve.reciprocal(total[:], total[:]).then_inc(spread_total, 1)
                dve.wait_ge(spread_total, i + 1 + START)
                for x in lanes:
                    mine = slice(x * CT, (x + 1) * CT)
                    dve.tensor_tensor(spread[x][:], weight[:, mine].unsqueeze(3).broadcast_to([P, CT, E, EI]),
                                      total[:, mine].unsqueeze(2).unsqueeze(3).broadcast_to([P, CT, E, EI]),
                                      ALU.mult).then_inc(spread_done[x], 1)
                for e in range(EP):
                    for x in lanes:
                        n = EP * i + e
                        dve.wait_ge(sig_done[x], n + 1 + START)
                        dve.wait_ge(down_done[x], n + START)
                        dve.tensor_tensor(hid[x][:], sig[x][:], ps[x][:, 1], ALU.mult).then_inc(mul1[x], 1)
                        dve.wait_ge(mul1[x], n + 1 + START)
                        dve.tensor_tensor(hid[x][:], hid[x][:], ps[x][:, 2], ALU.mult).then_inc(mul2[x], 1)
                        dve.wait_ge(mul2[x], n + 1 + START)
                        dve.tensor_tensor(hid[x][:], hid[x][:], ps[x][:, 3], ALU.mult).then_inc(hid_done[x], 1)
                for x in lanes:
                    dve.wait_ge(down_done[x], EP * (i + 1) + START)
                    dve.tensor_tensor(z_tm[x][:].rearrange("p k f -> p (k f)"), x1_tm[x][:].rearrange("p k f -> p (k f)"),
                                      ps[x][:, 0], ALU.add).then_inc(z_done[x], 1)
                for x in lanes:
                    dve.wait_ge(z_done[x], i + 1 + START)
                    dve.wait_ge(x2_kept[x], 16 * i + START)
                    dve.wait_ge(x2_turned[x], i + START)
                layer_norm(dve, ln, 2 * norm_steps(LT) * i + norm_steps(LT), lambda k: z_tm[k // CT][:, k % CT],
                           lambda k: x2_now[k // CT][:, k % CT], x2_done)

        @block.tensor
        def _(pe):
            pe.wait_ge(weights_in, 16 * 7 + START)
            with pe.Fori(0, ITER) as i:
                def turn(bank, src, x):
                    for k in range(CT):
                        last = pe.transpose(ps[x][:, bank, k * P:(k + 1) * P], src(k), t.ident[:])
                    return last

                for x in lanes:
                    pe.wait_ge(y_in[x], 16 * (i + 1) + START)
                    pe.wait_ge(z_done[x], i + START)
                    turn(0, lambda k: y_now[x][:, k * P:(k + 1) * P], x).then_inc(y_turned[x], 1)
                for x in lanes:
                    pe.wait_ge(x1_done[x], CT * (i + 1) + START)
                    pe.wait_ge(x2_copied[x], i + START)
                    turn(1, lambda k: x1_tm[x][:, k], x).then_inc(x1_turned[x], 1)
                for x in lanes:
                    pe.wait_ge(x1_ready[x], i + 1 + START)
                    for k in range(CT):
                        last = pe.matmul(ps[x][:, 0, k * E:(k + 1) * E], x1_fm[x][:, k * P:(k + 1) * P], gate_w[:],
                                         start=True, stop=True, skip_group_check=True)
                    last.then_inc(logits_done[x], 1)
                def gate_up(x, e):
                    pe.wait_ge(hid_done[x], EP * i + e + START)
                    if e == 0:
                        pe.wait_ge(scores_ready[x], i + 1 + START)
                    pe.matmul(ps[x][:, 1], w_gate[:, e], x1_fm[x][:], start=True, stop=True)
                    pe.matmul(ps[x][:, 2], w_up[:, e], x1_fm[x][:], start=True, stop=True)
                    if e == 0:
                        pe.wait_ge(spread_done[x], i + 1 + START)
                    two = lambda k: spread[x][:, k, 2 * e:2 * e + 2].rearrange("p e r -> p (e r)")
                    turn(3, two, x).then_inc(gate_up_done[x], 1)

                def down(x, e):
                    pe.wait_ge(hid_done[x], EP * i + e + 1 + START)
                    for k in range(CT):
                        last = pe.matmul(ps[x][:, 0, k * P:(k + 1) * P], hid[x][:, k * P:(k + 1) * P], w_down[:, e],
                                         start=(e == 0 and k == 0), stop=(e == EP - 1), skip_group_check=True)
                    last.then_inc(down_done[x], 1)

                for x in lanes:
                    gate_up(x, 0)
                for e in range(EP):
                    for x in lanes:
                        down(x, e)
                        if e < EP - 1:
                            gate_up(x, e + 1)
                for x in lanes:
                    pe.wait_ge(x2_done[x], CT * (i + 1) + START)
                    turn(1, lambda k: x2_now[x][:, k], x).then_inc(x2_turned[x], 1)


AH, AD = 16, 8
AG, AR = 4, 4
SLOT = P // AR
Z_EPS = 1e-6
STEPS = [(c, k) for c in range(NQC) for k in range(CT * (c + 1))]
HALVES = 2 * len(STEPS)
LAG = 2


def causal(nc, t, d):
    with ExitStack() as ctx:
        sb = lambda n, s, dt=F32: ctx.enter_context(nc.sbuf_tensor(n, s, dt))
        sem = semaphores(nc, ctx, t, True)
        weights_in = sem("d_weights_in")
        wq, wk = sb("wq1", [P, AG, P]), sb("wk1", [P, AG, P])
        wv, wo = sb("wv1", [P, D]), sb("wo1", [P, D])
        rows = sb("part_rows", [P, 4])
        mask = sb("causal_mask", [P, 2, P])
        shift = sb("square_shift", [P, 1])
        x_now = sb("x_now", [P, S])
        vx = sb("vx", [P, TT, AH, SLOT])
        q_rows = [[sb(f"q_rows{p}{r}", [P, S], F32R) for r in range(AR)] for p in range(2)]
        k_rows = [sb(f"k_rows{p}", [P, S], F32R) for p in range(2)]
        q_hi, k_hi = ([sb(f"{n}_hi{i}", [P, QC], F32R) for i in range(2)] for n in "qk")
        warm = sb("warm", [P, 1])
        a = [sb(f"a{i}", [P, 2, QC]) for i in range(2 * (LAG + 1))]
        o_rows = [sb(f"o_rows{i}", [P, QC]) for i in range(2)]
        z = [sb(f"z{i}", [P, CT, AR]) for i in range(2)]
        out_tm = sb("out_tm", [P, TT, D])
        out_fm = [sb(f"out_fm{c}", [P, QC]) for c in range(NQC)]
        z_tm = [sb(f"sum_tm{c}", [P, CT, D]) for c in range(NQC)]
        x3_tm = [sb(f"x3_tm{c}", [P, CT, D]) for c in range(NQC)]
        x3_fm = [sb(f"x3_fm{c}", [P, QC]) for c in range(NQC)]
        ln = norm_buffers(sb, sem, "d_ln", TT)
        ps_s = [ctx.enter_context(nc.psum_tensor(f"ps_d_s{i}", [P, 2, QC], F32)) for i in range(2)]
        bank = lambda n: ctx.enter_context(nc.psum_tensor(n, [P, QC], F32))
        ps_o, ps_t, ps_q, ps_k = bank("ps_d_o"), bank("ps_d_t"), bank("ps_d_q"), bank("ps_d_k")
        turn_bank, sum_bank = [ps_q, ps_o], [ps_k, ps_t]

        vx_set, vx_zero = sem("d_vx_set"), sem("d_vx_zero")
        x_in, v_done, v_copied = sem("d_x_in"), sem("d_v_done"), sem("d_v_copied")
        proj_done, split_done, rows_done = sem("d_proj_done"), sem("d_split_done"), sem("d_rows_done")
        qk_done, squared, a_ready, pv_done = sem("d_qk_done"), sem("d_squared"), sem("d_a_ready"), sem("d_pv_done")
        o_copied, o_turned, z_ready, z_recip, out_done = map(sem, ("d_o_copied", "d_o_turned", "d_z_ready", "d_z_recip", "d_out_done"))
        each = lambda n: [sem(f"d_{n}{c}") for c in range(NQC)]
        y_turned, y_ready, wo_done, sum_done, x3_done, x3_turned, x3_copied, x3_kept = map(
            each, ("y_turned", "y_ready", "wo_done", "sum_done", "x3_done", "x3_turned", "x3_copied", "x3_kept"))
        start(nc, sb("d_scrap", [P, len(t.to_start)]), t.to_start)
        block = ctx.enter_context(nc.Block())
        PROJ = AG * NQC
        AHEAD = {(0, 1): 0, (1, 1): 1}

        def banks(g, c):
            return (ps_s[0][:, 0], ps_s[0][:, 1]) if (g, c) == (0, 1) else (ps_q[:], ps_k[:])

        def each_step():
            for g in range(AG):
                for s, (c, k) in enumerate(STEPS):
                    yield g, s, c, k, max(0, (k - CT * c) * P)

        def copy_o(act, b, g, c):
            n = NQC * g + c - 1
            steps = len(STEPS) * (n // NQC) + (CT if n % NQC == 0 else len(STEPS))
            act.wait_ge(pv_done, len(STEPS) * AG * b + steps + START)
            act.wait_ge(o_turned, PROJ * b + max(n - 1, 0) + START)
            act.copy(o_rows[n % 2][:], ps_o[:]).then_inc(o_copied, 1)

        @block.sync
        def _(sp):
            for dst, src in ((wq, d.wq1), (wk, d.wk1), (wv, d.wv1), (wo, d.wo1), (rows, d.part_rows), (mask, d.causal_mask)):
                sp.dma_start(dst[:], src).then_inc(weights_in, 16)

            def load(b):
                sp.dma_start(x_now[:], t.y_fm[:, bass.ds(b * S, S)]).then_inc(x_in, 16)

            def store(b):
                for c in range(NQC):
                    sp.wait_ge(x3_copied[c], b + 1 + START)
                    sp.dma_start(t.y_fm[:, bass.ds(b * S + c * QC, QC)], x3_fm[c][:]).then_inc(x3_kept[c], 16)

            load(0)
            with sp.Fori(0, B - 1) as b:
                sp.wait_ge(proj_done, PROJ * (b + 1) + START)
                load(b + 1)
                store(b)
            store(B - 1)
            for c in range(NQC):
                sp.wait_ge(x3_kept[c], 16 * B + START)

        @block.gpsimd
        def _(pool):
            pool.memset(vx[:], 0.0).then_inc(vx_zero, 1)
            for p in range(2):
                for r in range(AR):
                    pool.memset(q_rows[p][r][:].bitcast(F32), 0.0).then_inc(vx_set, 1)

        @block.scalar
        def _(act):
            act.wait_ge(weights_in, 16 * 6 + START)
            act.wait_ge(vx_set, 2 * AR + 2 + START)
            with act.Fori(0, B) as b:
                act.activation(warm[:], shift[:], ACT.Square)
                def split(g, c):
                    n = PROJ * b + NQC * g + c
                    act.wait_ge(proj_done, n + 1 + START)
                    act.wait_ge(rows_done, PROJ * b + max(NQC * g + c - 1, 0) + START)
                    q_bank, k_bank = banks(g, c)
                    act.mul(q_hi[c][:], q_bank, rows[:, 1:2])
                    act.mul(k_hi[c][:], k_bank, rows[:, 3:4]).then_inc(split_done, 1)

                split(0, 0)
                split(0, 1)
                for g, s, c, k, off in each_step():
                    for r in range(2):
                        half = HALVES * g + 2 * s + r
                        act.wait_ge(qk_done, HALVES * AG * b + half + 1 + START)
                        act.wait_ge(pv_done, len(STEPS) * AG * b + max(len(STEPS) * g + s - LAG, 0) + START)
                        act.activation(a[half % len(a)][:, :, off:], ps_s[r][:, :, off:], ACT.Square, bias=shift[:],
                                       scale=0.25).then_inc(squared, 1)
                    if g < AG - 1 and (c, k) in AHEAD:
                        split(g + 1, AHEAD[c, k])
                    if k == LAG - 1 and (g or c):
                        copy_o(act, b, g, c)
                    if (g, c, k) == (AG - 1, NQC - 1, TT - 1):
                        copy_o(act, b, AG, 0)
                for c in range(NQC):
                    act.wait_ge(y_turned[c], b + 1 + START)
                    act.copy(out_fm[c][:], turn_bank[c][:]).then_inc(y_ready[c], 1)
                for c in range(NQC):
                    act.wait_ge(x3_turned[c], b + 1 + START)
                    act.wait_ge(x3_kept[c], 16 * b + START)
                    act.copy(x3_fm[c][:], turn_bank[c][:]).then_inc(x3_copied[c], 1)

        @block.vector
        def _(dve):
            dve.memset(shift[:], 0.5 ** 0.5).then_inc(vx_set, 1)
            dve.wait_ge(vx_zero, 1 + START)
            dve.memset(vx[:, :, :, AD:AD + 1], 1.0).then_inc(vx_set, 1)
            dve.wait_ge(vx_set, 2 * AR + 2 + START)
            dve.wait_ge(weights_in, 16 * 6 + START)
            with dve.Fori(0, B) as b:
                def make_rows(g, c):
                    n = PROJ * b + NQC * g + c
                    at = slice(c * QC, (c + 1) * QC)
                    dve.wait_ge(split_done, n + 1 + START)
                    dve.wait_ge(qk_done, HALVES * AG * b + max(HALVES * (g - 1), 0) + START)
                    q_bank, k_bank = banks(g, c)
                    for r in range(AR):
                        q = slice(r * SLOT, (r + 1) * SLOT)
                        dve.scalar_tensor_tensor(q_rows[g % 2][r][q, at], q_bank[q], rows[q, 0:1], q_hi[c][q].bitcast(F32),
                                                 ALU.mult, ALU.add)
                    dve.scalar_tensor_tensor(k_rows[g % 2][:, at], k_bank, rows[:, 2:3], k_hi[c][:].bitcast(F32),
                                             ALU.mult, ALU.add).then_inc(rows_done, 1)

                def normalise(n):
                    g, c = divmod(n, NQC)
                    turned = ps_t[:].rearrange("p (k r f) -> p k r f", k=CT, r=AR)
                    dve.wait_ge(o_turned, PROJ * b + n + 1 + START)
                    dve.wait_ge(out_done, PROJ * b + max(n - 1, 0) + START)
                    dve.tensor_scalar(z[n % 2][:], turned[:, :, :, AD], Z_EPS, None, ALU.add).then_inc(z_ready, 1)
                    dve.wait_ge(z_ready, PROJ * b + n + 1 + START)
                    dve.reciprocal(z[n % 2][:], z[n % 2][:]).then_inc(z_recip, 1)
                    dve.wait_ge(z_recip, PROJ * b + n + 1 + START)
                    to = out_tm[:, CT * c:CT * (c + 1), AR * AD * g:AR * AD * (g + 1)]
                    dve.tensor_tensor(to.rearrange("p k (r f) -> p k r f", r=AR), turned[:, :, :, 0:AD],
                                      z[n % 2][:].unsqueeze(3).broadcast_to([P, CT, AR, AD]), ALU.mult).then_inc(out_done, 1)

                make_rows(0, 0)
                make_rows(0, 1)
                for c in range(NQC):
                    dve.wait_ge(v_done, NQC * b + c + 1 + START)
                    dve.tensor_copy(vx[:, CT * c:CT * (c + 1), :, 0:AD].rearrange("p k h f -> p (k h) f"),
                                    ps_s[1][:, c].rearrange("p (k f) -> p k f", f=AD)).then_inc(v_copied, 1)
                for g, s, c, k, off in each_step():
                    for r in range(2):
                        half = HALVES * g + 2 * s + r
                        buf = a[half % len(a)]
                        diagonal = k >= CT * c
                        dve.wait_ge(squared, HALVES * AG * b + half + 1 + START)
                        full = off + P * diagonal
                        if diagonal:
                            last = dve.scalar_tensor_tensor(buf[:, :, off:full], buf[:, :, off:full], 0.5, mask[:],
                                                            ALU.add, ALU.mult)
                        if full < QC:
                            last = dve.tensor_scalar(buf[:, :, full:], buf[:, :, full:], 0.5, None, ALU.add)
                        last.then_inc(a_ready, 1)
                    if g < AG - 1 and (c, k) in AHEAD:
                        make_rows(g + 1, AHEAD[c, k])
                    if k == LAG + 1 and (g or c):
                        normalise(NQC * g + c - 1)
                normalise(PROJ - 1)
                for c in range(NQC):
                    dve.wait_ge(wo_done[c], b + 1 + START)
                    dve.tensor_tensor(z_tm[c][:], sum_bank[c][:].rearrange("p (k f) -> p k f", k=CT),
                                      t.x2_tm[:, bass.ds(b * TT + c * CT, CT), :], ALU.add).then_inc(sum_done[c], 1)
                for c in range(NQC):
                    dve.wait_ge(sum_done[c], b + 1 + START)
                    dve.wait_ge(x3_turned[c], b + START)
                layer_norm(dve, ln, norm_steps(TT) * b, lambda k: z_tm[k // CT][:, k % CT],
                           lambda k: x3_tm[k // CT][:, k % CT], x3_done)

        @block.tensor
        def _(pe):
            pe.wait_ge(weights_in, 16 * 6 + START)
            pe.wait_ge(vx_set, 2 * AR + 2 + START)
            with pe.Fori(0, B) as b:
                def project(g, c):
                    n = PROJ * b + NQC * g + c
                    at = slice(c * QC, (c + 1) * QC)
                    q_bank, k_bank = banks(g, c)
                    if (g, c) != (0, 1):
                        pe.wait_ge(rows_done, n + START)
                    pe.matmul(q_bank, wq[:, g], x_now[:, at], start=True, stop=True)
                    pe.matmul(k_bank, wk[:, g], x_now[:, at], start=True, stop=True).then_inc(proj_done, 1)

                def scores(g, s, c, k, off):
                    for r in range(2):
                        half = HALVES * g + 2 * s + r
                        pe.wait_ge(squared, HALVES * AG * b + max(half - 1, 0) + START)
                        for h in range(2):
                            last = pe.matmul(ps_s[r][:, h, off:], k_rows[g % 2][:, k * P:(k + 1) * P],
                                             q_rows[g % 2][2 * r + h][:, c * QC + off:(c + 1) * QC], start=True, stop=True)
                        last.then_inc(qk_done, 1)

                def weigh(g, s, c, k, off):
                    pe.wait_ge(a_ready, HALVES * AG * b + HALVES * g + 2 * s + 2 + START)
                    if k == 0:
                        pe.wait_ge(o_copied, PROJ * b + NQC * g + c + START)
                    for r in range(AR):
                        half = HALVES * g + 2 * s + r // 2
                        last = pe.matmul(ps_o[r * SLOT:(r + 1) * SLOT, off:], vx[:, k, AR * g + r],
                                         a[half % len(a)][:, r % 2, off:], start=(k == 0), stop=(k == CT * (c + 1) - 1))
                    last.then_inc(pv_done, 1)

                def turn_o(n):
                    pe.wait_ge(o_copied, PROJ * b + n + 1 + START)
                    pe.wait_ge(out_done, PROJ * b + n + START)
                    for k in range(CT):
                        last = pe.transpose(ps_t[:, k * P:(k + 1) * P], o_rows[n % 2][:, k * P:(k + 1) * P], t.ident[:])
                    last.then_inc(o_turned, 1)

                pe.wait_ge(x_in, 16 * (b + 1) + START)
                pe.wait_ge(x3_copied[0], b + START)
                pe.wait_ge(sum_done[0], b + START)
                project(0, 0)
                project(0, 1)
                for c in range(NQC):
                    for k in range(CT):
                        tile = CT * c + k
                        last = pe.matmul(ps_s[1][:, c, k * P:(k + 1) * P], x_now[:, tile * P:(tile + 1) * P], wv[:],
                                         start=True, stop=True, skip_group_check=True)
                    last.then_inc(v_done, 1)
                pe.wait_ge(v_copied, NQC * (b + 1) + START)
                before = []
                for g, s, c, k, off in each_step():
                    if s == 0:
                        pe.wait_ge(rows_done, PROJ * b + NQC * (g + 1) + START)
                    scores(g, s, c, k, off)
                    if len(before) == LAG:
                        weigh(*before.pop(0))
                    before.append((g, s, c, k, off))
                    if g < AG - 1 and (c, k) in AHEAD:
                        project(g + 1, AHEAD[c, k])
                    if k == LAG and (g or c):
                        turn_o(NQC * g + c - 1)
                for late in before:
                    weigh(*late)
                turn_o(PROJ - 1)
                for c in range(NQC):
                    pe.wait_ge(out_done, PROJ * (b + 1) + START)
                    for k in range(CT):
                        last = pe.transpose(turn_bank[c][:, k * P:(k + 1) * P], out_tm[:, CT * c + k], t.ident[:])
                    last.then_inc(y_turned[c], 1)
                for c in range(NQC):
                    pe.wait_ge(y_ready[c], b + 1 + START)
                    for k in range(CT):
                        last = pe.matmul(sum_bank[c][:, k * P:(k + 1) * P], out_fm[c][:, k * P:(k + 1) * P], wo[:],
                                         start=True, stop=True, skip_group_check=True)
                    last.then_inc(wo_done[c], 1)
                for c in range(NQC):
                    pe.wait_ge(x3_done[c], CT * (b + 1) + START)
                    for k in range(CT):
                        last = pe.transpose(turn_bank[c][:, k * P:(k + 1) * P], x3_tm[c][:, k], t.ident[:])
                    last.then_inc(x3_turned[c], 1)


QB = 3
LORA = 32
QGROUP = 16
HALF_RANGE = 7.5


def qlora(nc, t, d):
    with ExitStack() as ctx:
        sb = lambda n, s, dt=F32: ctx.enter_context(nc.sbuf_tensor(n, s, dt))
        sem = semaphores(nc, ctx, t, True)
        lanes = range(LANES)
        NW = 2 * QB
        weights_in = sem("e_weights_in")
        q_in = sb("q_in", [P, NW, D], I32)
        warm = sb("e_warm", [P, 1])
        scale = sb("scale", [P, NW, D // QGROUP])
        la, lb = sb("la", [LORA, NW, D]), sb("lb", [LORA, NW, D])
        w = sb("w", [P, NW, D])
        w_t = sb("w_t", [P, NW, D])
        bias1 = sb("bias1", [P, QB, D])
        cols = sb("cols", [P, 3, QB])
        h_fm = [sb(f"h_fm{x}", [P, S]) for x in lanes]
        y_tm = [sb(f"y_tm{x}", [P, TT, D]) for x in lanes]
        n_tm = [sb(f"n_tm{x}", [P, TT, D]) for x in lanes]
        g_fm = [sb(f"g_fm{x}", [P, S]) for x in lanes]
        out_tm = [sb(f"out_tm{x}", [P, TT, D]) for x in lanes]
        ln = [norm_buffers(sb, sem, f"e_ln{x}", TT) for x in lanes]
        ps = [ctx.enter_context(nc.psum_tensor(f"ps_e{x}", [P, 4, QC], F32)) for x in lanes]
        linear = [ps[x][:, 0:2].rearrange("p b q -> p (b q)") for x in lanes]
        turned = [ps[x][:, 2:4].rearrange("p b q -> p (b q)") for x in lanes]
        each = lambda n: [sem(f"e_{n}{x}") for x in lanes]
        dequant, lora_done, w_ready, w_turned, w_copied = map(
            sem, ("e_dequant", "e_lora_done", "e_w_ready", "e_w_turned", "e_w_copied"))
        h_in, lin1_done, y_done, n_done, n_turned, g_ready, lin2_done = map(
            each, ("h_in", "lin1_done", "y_done", "n_done", "n_turned", "g_ready", "lin2_done"))
        h_added, total_done, total_turned, out_done, out_kept = map(
            each, ("h_added", "total_done", "total_turned", "out_done", "out_kept"))
        start(nc, sb("e_scrap", [P, len(t.to_start)]), t.to_start)
        block = ctx.enter_context(nc.Block())
        ITER = B // LANES

        @block.sync
        def _(sp):
            for dst, src in ((q_in, d.qweights), (scale, d.qscales), (la, d.la), (lb, d.lb), (bias1, d.bias1), (cols, d.cols)):
                sp.dma_start(dst[:], src).then_inc(weights_in, 16)

            def load(i):
                for x in lanes:
                    sp.dma_start(h_fm[x][:], t.y_fm[:, bass.ds((i * LANES + x) * S, S)]).then_inc(h_in[x], 16)

            def store(i):
                for x in lanes:
                    sp.wait_ge(out_done[x], TT * (i + 1) + START)
                    sp.dma_start(d.out[bass.ds((i * LANES + x) * S, S), :].rearrange("(k p) f -> p k f", p=P),
                                 out_tm[x][:]).then_inc(out_kept[x], 16)

            load(0)
            with sp.Fori(0, ITER - 1) as i:
                for x in lanes:
                    sp.wait_ge(total_done[x], i + 1 + START)
                load(i + 1)
                store(i)
            store(ITER - 1)
            for x in lanes:
                sp.wait_ge(out_kept[x], 16 * ITER + START)

        @block.scalar
        def _(act):
            act.wait_ge(weights_in, 16 * 6 + START)
            for m in range(NW):
                act.wait_ge(w_turned, m + 1 + START)
                act.copy(w_t[:, m], ps[1][:, m % 4, 0:P]).then_inc(w_copied, 1)
            with act.Fori(0, ITER) as i:
                act.activation(warm[:], cols[:, 0, 0:1], ACT.Gelu)
                for m in range(QB):
                    for x in lanes:
                        act.wait_ge(n_turned[x], QB * i + m + 1 + START)
                        act.wait_ge(lin2_done[x], QB * i + m + START)
                        act.activation(g_fm[x][:], turned[x], ACT.Gelu, bias=cols[:, 1, m:m + 1],
                                       scale=cols[:, 0, m:m + 1]).then_inc(g_ready[x], 1)

        @block.vector
        def _(dve):
            dve.wait_ge(weights_in, 16 * 6 + START)
            dve.tensor_scalar(w[:], q_in[:], 1.0 / HALF_RANGE, -1.0, ALU.mult, ALU.add).then_inc(dequant, 1)
            dve.wait_ge(dequant, 1 + START)
            by_group = w[:].rearrange("p m (g f) -> p (m g) f", f=QGROUP)
            dve.tensor_tensor(by_group, by_group, scale[:].rearrange("p m g -> p (m g)").unsqueeze(2).broadcast_to(
                [P, NW * D // QGROUP, QGROUP]), ALU.mult).then_inc(dequant, 1)
            dve.wait_ge(dequant, 2 + START)
            for m in range(NW):
                dve.wait_ge(lora_done, m + 1 + START)
                dve.tensor_tensor(w[:, m], w[:, m], ps[0][:, m % 4, 0:P], ALU.add).then_inc(w_ready, 1)
            with dve.Fori(0, ITER) as i:
                def add_h(x, m):
                    dve.wait_ge(lin2_done[x], QB * i + m + 1 + START)
                    dve.scalar_tensor_tensor(h_fm[x][:], linear[x], cols[:, 2, m:m + 1], h_fm[x][:],
                                             ALU.add, ALU.add).then_inc(h_added[x], 1)

                for m in range(QB):
                    for x in lanes:
                        n = QB * i + m
                        last_h = None if x == 0 and m == 0 else lambda x=x, m=m: add_h(1 - x, m - (x == 0))
                        dve.wait_ge(lin1_done[x], n + 1 + START)
                        bias = bias1[:, m].unsqueeze(1).broadcast_to([P, TT, D])
                        dve.tensor_tensor(y_tm[x][:], linear[x].rearrange("p (k f) -> p k f", k=TT), bias,
                                          ALU.add).then_inc(y_done[x], 1)
                        dve.wait_ge(y_done[x], n + 1 + START)
                        dve.wait_ge(n_turned[x], n + START)
                        layer_norm(dve, ln[x], norm_steps(TT) * ((QB + 1) * i + m), lambda k, x=x: y_tm[x][:, k],
                                   lambda k, x=x: n_tm[x][:, k], [n_done[x]], last_h)
                for x in lanes:
                    if x == LANES - 1:
                        add_h(x, QB - 1)
                    dve.wait_ge(h_added[x], QB * (i + 1) + START)
                    dve.tensor_tensor(g_fm[x][:], h_fm[x][:], t.y_fm[:, bass.ds((i * LANES + x) * S, S)],
                                      ALU.add).then_inc(total_done[x], 1)
                for x in lanes:
                    dve.wait_ge(total_turned[x], i + 1 + START)
                    dve.wait_ge(out_kept[x], 16 * i + START)
                    layer_norm(dve, ln[x], norm_steps(TT) * ((QB + 1) * i + QB),
                               lambda k, x=x: turned[x][:, k * P:(k + 1) * P],
                               lambda k, x=x: out_tm[x][:, k], [out_done[x]])

        @block.tensor
        def _(pe):
            pe.wait_ge(weights_in, 16 * 6 + START)
            for m in range(NW):
                if m >= 4:
                    pe.wait_ge(w_ready, m - 3 + START)
                pe.matmul(ps[0][:, m % 4, 0:P], lb[:, m], la[:, m], start=True, stop=True).then_inc(lora_done, 1)
            for m in range(NW):
                pe.wait_ge(w_ready, m + 1 + START)
                if m >= 4:
                    pe.wait_ge(w_copied, m - 3 + START)
                pe.transpose(ps[1][:, m % 4, 0:P], w[:, m], t.ident[:]).then_inc(w_turned, 1)
            pe.wait_ge(w_copied, NW + START)
            with pe.Fori(0, ITER) as i:
                def linear1(x, m):
                    if m == 0:
                        pe.wait_ge(h_in[x], 16 * (i + 1) + START)
                    else:
                        pe.wait_ge(h_added[x], QB * i + m + START)
                    for k in range(TT):
                        last = pe.matmul(linear[x][:, k * P:(k + 1) * P], h_fm[x][:, k * P:(k + 1) * P], w_t[:, 2 * m],
                                         start=True, stop=True, skip_group_check=True)
                    last.then_inc(lin1_done[x], 1)

                def turn(x, m):
                    pe.wait_ge(n_done[x], TT * (QB * i + m + 1) + START)
                    if m == 0:
                        pe.wait_ge(out_done[x], TT * i + START)
                    for k in range(TT):
                        last = pe.transpose(turned[x][:, k * P:(k + 1) * P], n_tm[x][:, k], t.ident[:])
                    last.then_inc(n_turned[x], 1)

                def linear2(x, m):
                    pe.wait_ge(g_ready[x], QB * i + m + 1 + START)
                    for c in range(NQC):
                        half = slice(c * QC, (c + 1) * QC)
                        last = pe.matmul(linear[x][:, half], w_t[:, 2 * m + 1], g_fm[x][:, half], start=True, stop=True)
                    last.then_inc(lin2_done[x], 1)

                for x in lanes:
                    linear1(x, 0)
                for m in range(QB):
                    for x in lanes:
                        turn(x, m)
                        linear2(x, m)
                        if m < QB - 1:
                            linear1(x, m + 1)
                for x in lanes:
                    pe.wait_ge(total_done[x], i + 1 + START)
                    for k in range(TT):
                        last = pe.transpose(turned[x][:, k * P:(k + 1) * P], g_fm[x][:, k * P:(k + 1) * P], t.ident[:])
                    last.then_inc(total_turned[x], 1)


def build(nc, d):
    with ExitStack() as ctx:
        t = Bag()
        t.made_before = []
        t.ident = ctx.enter_context(nc.sbuf_tensor("ident", [P, P], F32))
        t.y_fm = ctx.enter_context(nc.sbuf_tensor("y_fm", [P, B * S], F32))
        with ExitStack() as attention:
            t.cos = attention.enter_context(nc.sbuf_tensor("cos", [P, S], F32))
            t.sin = attention.enter_context(nc.sbuf_tensor("sin", [P, S], F32))
            t.c_fm = attention.enter_context(nc.sbuf_tensor("c_fm", [P, B * S], F32))
            t.v_tm = attention.enter_context(nc.sbuf_tensor("v_tm", [P, B * TT, DH], F32))
            t.g_all = attention.enter_context(nc.sbuf_tensor("g_all", [P, PAIRS, D], F32))
            project_inputs(nc, t, d)
            latent_attention(nc, t, d)
        t.x2_tm = ctx.enter_context(nc.sbuf_tensor("x2_tm", [P, B * TT, D], F32))
        experts(nc, t, d)
        causal(nc, t, d)
        qlora(nc, t, d)


def lay_out(i):
    f = {n: np.ascontiguousarray(a) for n, a in i.items()}
    f32 = np.float32
    wq, wk = (f[n].reshape(PAIRS, 2, DH, DH) for n in ("L0_attn_w_up_q", "L0_attn_w_up_k"))
    wqk = np.zeros((PAIRS, P, 2, P), f32)
    wqk[:, :DH, :, :DH] = wq.transpose(0, 3, 1, 2)
    wqk[:, DH:, :, DH:] = wk.transpose(0, 3, 1, 2)
    inv = (1.0 / 10000.0 ** (np.arange(0, DH, 2, dtype=f32) / DH)).astype(f32)
    freqs = np.outer(np.arange(S, dtype=f32), inv)
    cos, sin = (np.concatenate([g(freqs), g(freqs)], -1)[:, ::2].astype(f32) for g in (np.cos, np.sin))
    sign = np.tile(np.array([-1.0, 1.0], f32), P // 2)[:, None]
    rows = np.tile(np.repeat(np.arange(DH // 2), 2), 2)
    tiled = lambda a: np.ascontiguousarray(np.broadcast_to(a, (P, LANES * CT) + a.shape))
    before = lambda n: tiled(np.tril(np.ones((n, n), f32), -1))
    gp, up = (f["L0_ffn_" + n].reshape(EP, P, D).transpose(2, 0, 1) for n in ("gate_proj", "up_proj"))
    kinds = {"q": [0, 1, 0, 1], "k": [0, 0, 1, 1]}
    is_lo = {n: np.tile(np.repeat(np.array(v, f32), AD), AR) for n, v in kinds.items()}
    four = lambda w: np.ascontiguousarray(np.broadcast_to(
        w.reshape(AG, AR, 1, AD, D), (AG, AR, 4, AD, D)).reshape(AG, P, D).transpose(2, 0, 1))
    return {
        "wq1": four(f["L1_attn_Wq"]),
        "wk1": four(f["L1_attn_Wk"]),
        "wv1": np.ascontiguousarray(f["L1_attn_Wv"].T),
        "wo1": np.ascontiguousarray(f["L1_attn_Wo"].T),
        "part_rows": np.stack([is_lo["q"], 1 - 2 * is_lo["q"], is_lo["k"], 1 - 2 * is_lo["k"]], 1),
        "causal_mask": np.ascontiguousarray(np.broadcast_to(np.triu(np.ones((P, 1, P), f32)[:, 0])[:, None], (P, 2, P))),
        "qweights": np.ascontiguousarray(f["L1_ffn_qweights"].transpose(1, 0, 2)),
        "qscales": np.ascontiguousarray(f["L1_ffn_scales"].transpose(1, 0, 2)),
        "la": np.ascontiguousarray(f["L1_ffn_lora_a"].transpose(1, 0, 2)),
        "lb": np.ascontiguousarray(f["L1_ffn_lora_b"].transpose(2, 0, 1)),
        "bias1": np.ascontiguousarray(np.broadcast_to(f["L1_ffn_biases"][0::2], (P, QB, D))),
        "cols": np.ascontiguousarray(np.stack([f["L1_ffn_ln_gamma"].T, f["L1_ffn_ln_beta"].T, f["L1_ffn_biases"][1::2].T], 1)),
        "gate_w": np.ascontiguousarray(f["L0_ffn_gate_weight"].T),
        "route_bias": tiled(f["L0_ffn_e_score_correction_bias"]),
        "before_g": before(NG),
        "before_e": before(E),
        "w_gate": np.ascontiguousarray(gp),
        "w_up": np.ascontiguousarray(up),
        "w_down": np.ascontiguousarray(f["L0_ffn_down_proj"].transpose(0, 2, 1).reshape(EP, P, D).transpose(1, 0, 2)),
        "x": f["L0_attn_x"].reshape(B * S, D),
        "ident": np.eye(P, dtype=f32),
        "wd": np.ascontiguousarray(np.concatenate([f["L0_attn_w_down_q"], f["L0_attn_w_down_kv"]], 0).T),
        "lnp": np.stack([f["L0_attn_ln_scale"], f["L0_attn_ln_bias"]], 1),
        "wv": np.ascontiguousarray(f["L0_attn_w_up_v"].reshape(H, DH, DH).transpose(1, 0, 2)),
        "wo": np.ascontiguousarray(f["L0_attn_w_out"].T.reshape(H, DH, D).transpose(1, 0, 2)),
        "wqk": wqk,
        "cos": np.ascontiguousarray(cos.T[rows]),
        "sin": np.ascontiguousarray(sin.T[rows] * sign),
    }


def kernel(**inputs):
    from concourse import bacc
    from concourse.bass_utils import run_bass_kernel_spmd

    nc = bacc.Bacc("TRN2", target_bir_lowering=False, num_devices=1)
    arrays = lay_out(inputs)
    d = Bag()
    for name, a in arrays.items():
        d.__dict__[name] = nc.dram_tensor(f"in_{name}", a.shape, mybir.dt.from_np(a.dtype), kind="ExternalInput").ap()
    d.out = nc.dram_tensor("out", (B * S, D), F32, kind="ExternalOutput").ap()
    build(nc, d)
    r = run_bass_kernel_spmd(nc, [{f"in_{n}": a for n, a in arrays.items()}], core_ids=[0])
    return r.results[0]["out"].reshape(B, S, D)
```
